# Optimizing a Trainium2 kernel written in Bass

```python
import numpy as np
import jax
import jax.numpy as jnp

def _softmax(x, axis=-1):
    return jax.nn.softmax(x, axis=axis)

def _gelu(x):
    return jax.nn.gelu(x, approximate=True)

def _silu(x):
    return jax.nn.silu(x)

def _sigmoid(x):
    return jax.nn.sigmoid(x)

def _layernorm(x, axis=-1, eps=1e-05):
    m = jnp.mean(x, axis=axis, keepdims=True)
    v = jnp.var(x, axis=axis, keepdims=True)
    return (x - m) / jnp.sqrt(v + eps)

def _scatter_add(tgt, idx, src, axis=0):
    return tgt.at[idx].add(src)

def _segment_sum(src, seg, n):
    return jax.ops.segment_sum(src, seg, n)
kernel_name = 'mk_gps_d1_gnn_r8_5a20bb'

def setup_inputs(seed: int=0):
    np.random.seed(seed)
    _w = jnp.asarray

    def _rec_inputs():
        import jax
        import jax.numpy as jnp
        _gk = jax.random.key(seed)
        x = -0.0002117 + 1 * jax.random.normal(jax.random.fold_in(_gk, 1), (6250, 256), jnp.float32)
        src = jax.random.randint(jax.random.fold_in(_gk, 2), (100000,), 0, 6250, jnp.int32)
        dst = jax.random.randint(jax.random.fold_in(_gk, 3), (100000,), 0, 6250, jnp.int32)
        _o = jnp.argsort(dst, stable=True)
        src = src[_o]
        dst = dst[_o]
        return (x, src, dst)
    x, src, dst = _rec_inputs()

    def _L0_gnn_setup():
        import jax, jax.numpy as jnp
        import numpy as np
        ALPHA = 0.2
        N_NODES = 12500
        N_EDGES = 200000
        NFEAT = 256
        HID = 64
        NHEADS = 4

        def _gat_head(x, src, dst, Wh, ah, n_nodes):
            hid = Wh.shape[1]
            h = x @ Wh
            h = jnp.where(jnp.isnan(h), 0.0, h)
            a1, a2 = (ah[0, :hid], ah[0, hid:])
            alpha_src = h @ a1
            alpha_dst = h @ a2
            s = alpha_src[src] + alpha_dst[dst]
            e = jnp.exp(-jax.nn.leaky_relu(s, ALPHA))
            e = jnp.where(jnp.isnan(e), 0.0, e)
            rowsum = jax.ops.segment_sum(e, src, num_segments=n_nodes)
            hp = jax.ops.segment_sum(e[:, None] * h[dst], src, num_segments=n_nodes)
            hp = jnp.where(jnp.isnan(hp), 0.0, hp)
            hp = hp / rowsum[:, None]
            hp = jnp.where(jnp.isnan(hp), 0.0, hp)
            return jax.nn.elu(hp)
        key = jax.random.key(seed)
        k1, k2, k3, k4 = jax.random.split(key, 4)
        x = jax.random.normal(k1, (N_NODES, NFEAT), dtype=jnp.float32)
        edge_index = jax.random.randint(k2, (2, N_EDGES), 0, N_NODES, dtype=jnp.int64)
        W = jax.random.normal(k3, (NHEADS, NFEAT, HID), dtype=jnp.float32) * (1.414 * np.sqrt(2.0 / (NFEAT + HID)))
        a = jax.random.normal(k4, (NHEADS, 1, 2 * HID), dtype=jnp.float32) * (1.414 * np.sqrt(2.0 / (1 + 2 * HID)))
        return {'x': x, 'edge_index': edge_index, 'W': W, 'a': a}
    _L0_gnn_all = _L0_gnn_setup()
    _L0_gnn_in = {k: v for k, v in _L0_gnn_all.items() if k in ('W', 'a')}
    del _L0_gnn_all

    def _L0_mix_setup():
        import jax, jax.numpy as jnp
        import numpy as np
        N, F, C, H = (32, 512, 256, 8)
        D = C // H
        EPS_ATTN = 1e-06
        EPS_LN = 1e-05

        def layer_norm(x, g, b):
            mu = jnp.mean(x, axis=-1, keepdims=True)
            var = jnp.var(x, axis=-1, keepdims=True)
            return (x - mu) * jax.lax.rsqrt(var + EPS_LN) * g + b
        key = jax.random.key(seed)
        ks = jax.random.split(key, 8)
        s = 1.0 / np.sqrt(C)
        return {'x': jax.random.normal(ks[0], (N, F, C), jnp.float32), 'Wqkv': jax.random.uniform(ks[1], (3 * C, C), jnp.float32, -s, s), 'ln1_g': jnp.ones((C,), jnp.float32), 'ln1_b': jnp.zeros((C,), jnp.float32), 'W1': jax.random.uniform(ks[2], (C, C), jnp.float32, -s, s), 'b1': jax.random.uniform(ks[3], (C,), jnp.float32, -s, s), 'W2': jax.random.uniform(ks[4], (C, C), jnp.float32, -s, s), 'b2': jax.random.uniform(ks[5], (C,), jnp.float32, -s, s), 'ln2_g': jnp.ones((C,), jnp.float32), 'ln2_b': jnp.zeros((C,), jnp.float32)}
    _L0_mix_all = _L0_mix_setup()
    _L0_mix_in = {k: v for k, v in _L0_mix_all.items() if k in ('Wqkv', 'ln1_g', 'ln1_b', 'W1', 'b1', 'W2', 'b2', 'ln2_g', 'ln2_b')}
    del _L0_mix_all

    def _L0_ffn_setup():
        import jax, jax.numpy as jnp
        import numpy as np
        C = 256
        HID = 1024
        E = 8
        TEMP = 1.0
        key = jax.random.key(seed)
        ks = jax.random.split(key, 7)
        x = jax.random.normal(ks[0], (8, 2048, C), dtype=jnp.float32)
        W1 = jax.random.normal(ks[1], (C, HID), dtype=jnp.float32) * 0.02
        b1 = jnp.zeros((HID,), dtype=jnp.float32)
        Wg = jax.random.normal(ks[2], (HID, E), dtype=jnp.float32) * 0.02
        bg = jnp.zeros((E,), dtype=jnp.float32)
        Wd = jax.random.normal(ks[3], (E, HID, C), dtype=jnp.float32) * 0.02
        bd = jnp.zeros((E, C), dtype=jnp.float32)
        return {'x': x, 'W1': W1, 'b1': b1, 'Wg': Wg, 'bg': bg, 'Wd': Wd, 'bd': bd}
    _L0_ffn_all = _L0_ffn_setup()
    _L0_ffn_in = {k: v for k, v in _L0_ffn_all.items() if k in ('W1', 'b1', 'Wg', 'bg', 'Wd', 'bd')}
    del _L0_ffn_all
    return {'x': x, 'src': src, 'dst': dst, 'L0_gnn_W': _L0_gnn_in['W'], 'L0_gnn_a': _L0_gnn_in['a'], 'L0_mix_Wqkv': _L0_mix_in['Wqkv'], 'L0_mix_ln1_g': _L0_mix_in['ln1_g'], 'L0_mix_ln1_b': _L0_mix_in['ln1_b'], 'L0_mix_W1': _L0_mix_in['W1'], 'L0_mix_b1': _L0_mix_in['b1'], 'L0_mix_W2': _L0_mix_in['W2'], 'L0_mix_b2': _L0_mix_in['b2'], 'L0_mix_ln2_g': _L0_mix_in['ln2_g'], 'L0_mix_ln2_b': _L0_mix_in['ln2_b'], 'L0_ffn_W1': _L0_ffn_in['W1'], 'L0_ffn_b1': _L0_ffn_in['b1'], 'L0_ffn_Wg': _L0_ffn_in['Wg'], 'L0_ffn_bg': _L0_ffn_in['bg'], 'L0_ffn_Wd': _L0_ffn_in['Wd'], 'L0_ffn_bd': _L0_ffn_in['bd']}

def reference(x, src, dst, L0_gnn_W, L0_gnn_a, L0_mix_Wqkv, L0_mix_ln1_g, L0_mix_ln1_b, L0_mix_W1, L0_mix_b1, L0_mix_W2, L0_mix_b2, L0_mix_ln2_g, L0_mix_ln2_b, L0_ffn_W1, L0_ffn_b1, L0_ffn_Wg, L0_ffn_bg, L0_ffn_Wd, L0_ffn_bd):
    import jax
    import jax.numpy as jnp

    def _L0_gnn_ref(x, edge_index, W, a):
        import jax, jax.numpy as jnp
        import numpy as np
        ALPHA = 0.2
        N_NODES = 12500
        N_EDGES = 200000
        NFEAT = 256
        HID = 64
        NHEADS = 4

        def _gat_head(x, src, dst, Wh, ah, n_nodes):
            hid = Wh.shape[1]
            h = x @ Wh
            h = jnp.where(jnp.isnan(h), 0.0, h)
            a1, a2 = (ah[0, :hid], ah[0, hid:])
            alpha_src = h @ a1
            alpha_dst = h @ a2
            s = alpha_src[src] + alpha_dst[dst]
            e = jnp.exp(-jax.nn.leaky_relu(s, ALPHA))
            e = jnp.where(jnp.isnan(e), 0.0, e)
            rowsum = jax.ops.segment_sum(e, src, num_segments=n_nodes)
            hp = jax.ops.segment_sum(e[:, None] * h[dst], src, num_segments=n_nodes)
            hp = jnp.where(jnp.isnan(hp), 0.0, hp)
            hp = hp / rowsum[:, None]
            hp = jnp.where(jnp.isnan(hp), 0.0, hp)
            return jax.nn.elu(hp)
        n_nodes = x.shape[0]
        src, dst = (edge_index[0], edge_index[1])
        outs = [_gat_head(x, src, dst, W[h], a[h], n_nodes) for h in range(W.shape[0])]
        out = jnp.concatenate(outs, axis=1)
        return jax.nn.elu(out)

    def _L0_mix_ref(x, Wqkv, ln1_g, ln1_b, W1, b1, W2, b2, ln2_g, ln2_b):
        import jax, jax.numpy as jnp
        import numpy as np
        N, F, C, H = (32, 512, 256, 8)
        D = C // H
        EPS_ATTN = 1e-06
        EPS_LN = 1e-05

        def layer_norm(x, g, b):
            mu = jnp.mean(x, axis=-1, keepdims=True)
            var = jnp.var(x, axis=-1, keepdims=True)
            return (x - mu) * jax.lax.rsqrt(var + EPS_LN) * g + b
        n, f, c = x.shape
        qkv = jnp.einsum('nfc,oc->nfo', x, Wqkv)
        q, k, v = jnp.split(qkv, 3, axis=-1)
        q = q.reshape(n, f, H, D)
        k = k.reshape(n, f, H, D)
        v = v.reshape(n, f, H, D)
        q = jax.nn.elu(q) + 1.0
        k = jax.nn.elu(k) + 1.0
        kv = jnp.einsum('nshd,nshm->nhmd', k, v)
        ksum = jnp.sum(k, axis=1)
        z = 1.0 / (jnp.einsum('nlhd,nhd->nlh', q, ksum) + EPS_ATTN)
        t = jnp.einsum('nlhd,nhmd,nlh->nlhm', q, kv, z)
        t = t.reshape(n, f, c)
        x1 = layer_norm(t + x, ln1_g, ln1_b)
        h = jax.nn.gelu(jnp.einsum('nfc,oc->nfo', x1, W1) + b1, approximate=False)
        y = jnp.einsum('nfc,oc->nfo', h, W2) + b2
        return layer_norm(y + x1, ln2_g, ln2_b)

    def _L0_ffn_ref(x, W1, b1, Wg, bg, Wd, bd):
        import jax, jax.numpy as jnp
        import numpy as np
        C = 256
        HID = 1024
        E = 8
        TEMP = 1.0
        orig_shape = x.shape
        xf = x.reshape(-1, orig_shape[-1])
        H = jax.nn.gelu(xf @ W1 + b1, approximate=False)
        probs = jax.nn.softmax((H @ Wg + bg) / TEMP, axis=-1)
        assign = jnp.argmax(probs, axis=-1)
        out = jnp.zeros_like(xf)
        for e in range(Wd.shape[0]):
            y = H @ Wd[e] + bd[e]
            sel = (assign == e)[:, None]
            out = out + jnp.where(sel, probs[:, e:e + 1] * y, 0.0)
        return out.reshape(orig_shape)
    edge_index = jnp.stack([src, dst])
    xn = _layernorm(x, axis=-1)
    x = x + _L0_gnn_ref(xn, edge_index, L0_gnn_W, L0_gnn_a) + _L0_mix_ref(xn[None], L0_mix_Wqkv, L0_mix_ln1_g, L0_mix_ln1_b, L0_mix_W1, L0_mix_b1, L0_mix_W2, L0_mix_b2, L0_mix_ln2_g, L0_mix_ln2_b)[0]
    x = x + _L0_ffn_ref(_layernorm(x, axis=-1)[None], L0_ffn_W1, L0_ffn_b1, L0_ffn_Wg, L0_ffn_bg, L0_ffn_Wd, L0_ffn_bd)[0]
    return x

_drawn_inputs = setup_inputs


def setup_inputs(seed=0):
    import zlib

    import numpy as np

    out = dict(_drawn_inputs(seed))
    spreads = {'L0_mix_ln1_g': (1.0, 0.2),
     'L0_mix_ln1_b': (0.0, 0.1),
     'L0_mix_ln2_g': (1.0, 0.2),
     'L0_mix_ln2_b': (0.0, 0.1),
     'L0_ffn_b1': (0.0, 0.8),
     'L0_ffn_bg': (0.0, 0.8),
     'L0_ffn_bd': (0.0, 0.8)}
    factors = {'L0_mix_Wqkv': 8.0,
     'L0_mix_b1': 8.0,
     'L0_mix_b2': 3.334,
     'L0_ffn_W1': 5.528,
     'L0_ffn_Wg': 5.936,
     'L0_ffn_Wd': 6.758}
    for name, (base, spread) in spreads.items():
        noise = np.random.default_rng([zlib.crc32(name.encode()), seed]).standard_normal(out[name].shape)
        drawn = base * np.exp(spread * noise) if base else spread * noise
        out[name] = jnp.asarray(drawn.astype(out[name].dtype))
    for name, factor in factors.items():
        out[name] = (out[name] * factor).astype(out[name].dtype)
    return out
```

```python
from contextlib import ExitStack

import concourse.bass as bass
from concourse import mybir

P = 128
C = 256
CC = C // P
N_NODES = 6250
NT = 50
ROWS = NT * P
BINS = -(-N_NODES // P)
N_EDGES = 100000
LOG_SLOTS = 17
SLOTS = 1 << LOG_SLOTS
SC = SLOTS // P
LOG_SC = 10
PAIR = 2 * P
TPP = SC // PAIR
FIELD = 13
NOBODY = (1 << FIELD) - 1
KEY_ONE = 1 << 30
HEADS = 4
HID = C // HEADS
HROW = C + HEADS
HCOL = C + 2 * HEADS
PER_BATCH = 8
NBATCH = -(-(-(-N_EDGES // PAIR) + BINS - 1) // PER_BATCH)
ITEMS = NBATCH * PER_BATCH
NPAIR = NT // 2
MH = 8
MD = C // MH
FF = 1024
FC = FF // P
EXPERTS = 8
NSLOT = NT + EXPERTS
FROW = FF + C + 4
SKIP = 100000
EPS = 1e-5
EPS_ATTN = 1e-6
TINY = 1.1754944e-38

ALU = mybir.AluOpType
ACT = mybir.ActivationFunctionType
AX_X = mybir.AxisListType.X
F32 = mybir.dt.float32
BF16 = mybir.dt.bfloat16
I32 = mybir.dt.int32
ds = bass.ds


def gps_layer(nc, x, src, dst, gw, gwt, ga, wqkv_t, ln1_g, ln1_b, ln1_g_rows, ln1_b_rows, w1_t, b1, w2_t,
              b2, ln2_g, ln2_b, fw1, fb1, fwg, fbg, fwd, fbd, out):
    ctx = ExitStack()
    with ctx:
        def sb(name, shape, dt=F32):
            return ctx.enter_context(nc.sbuf_tensor(name, shape, dt))

        def sem(name):
            return ctx.enter_context(nc.semaphore(name))

        node_table = nc.dram_tensor("node_table", [ROWS, HROW], F32, kind="Internal").ap()
        expert_table = nc.dram_tensor("expert_table", [ROWS, FROW], F32, kind="Internal").ap()

        xall = sb("xall", [P, NT, C])
        asrc = sb("asrc", [P, NT * HEADS])
        w_gat = sb("w_gat", [P, CC, HCOL])
        w_kv = sb("w_kv", [P, CC, 2 * C])
        w_q = sb("w_q", [P, CC, C])
        w1g = sb("w1g", [P, CC, C])
        w2s = sb("w2s", [P, CC, C])
        wt_heads = sb("wt_heads", [HID, HEADS, C])
        a_heads = sb("a_heads", [HID, HEADS, 2])
        b1col = sb("b1col", [P, CC])
        b1eff = sb("b1eff", [P, CC])
        g1col = sb("g1col", [P, CC])
        be1col = sb("be1col", [P, CC])
        g1rep = sb("g1rep", [P, C])
        c1rep = sb("c1rep", [P, C])
        b2rep = sb("b2rep", [P, C])
        g2rep = sb("g2rep", [P, C])
        c2rep = sb("c2rep", [P, C])
        kvbd = sb("kvbd", [P, CC, P + HEADS])
        std = sb("std", [P, NT])
        rstd = sb("rstd", [P, NT])
        nmr = sb("nmr", [P, NT])
        ident = sb("ident", [P, P])
        upper = sb("upper", [P, P])
        ones = sb("ones", [P, P])
        iota_p = sb("iota_p", [P, P])
        iota_k = sb("iota_k", [P, ITEMS])
        valid = sb("valid", [P, NT + 1])
        minus1 = sb("minus1", [P, 1])
        pm1 = sb("pm1", [P, 2])
        part_i = sb("part_i", [P, 8], I32)
        bit_i = sb("bit_i", [P, 8], I32)
        sign = sb("sign", [P, 8])
        srcrel = sb("srcrel", [P, (ITEMS + PER_BATCH) * 2])
        dst_tab = sb("dst_tab", [P, (ITEMS + PER_BATCH) * 2], I32)
        bin_acc = sb("bin_acc", [1, ITEMS + PER_BATCH], I32)
        bin_asrc = sb("bin_asrc", [1, ITEMS + PER_BATCH], I32)
        xs = sb("xs", [P, 2, C])
        xT = sb("xT", [P, CC, 2 * P])
        ev = sb("ev", [P, 2, C])
        em = sb("em", [P, 2, C])
        qs = sb("qs", [P, CC, 2 * P])

        stat = sb("stat", [P, NT, 6])
        st_s = sb("st_s", [P, 4, NT])
        slot_wd = sb("slot_wd", [1, 64], I32)
        slot_bd = sb("slot_bd", [1, 64], I32)

        ACC = NT * HROW
        WD = EXPERTS * FC * C
        ARENA = 27300
        arena = sb("arena", [P, ARENA])

        class Carve:
            def __init__(self, at):
                self.at = at

            def take(self, n, dt=F32):
                view = arena[:, self.at:self.at + n]
                self.at += n
                assert self.at <= ARENA, self.at
                return view if dt is F32 else view.bitcast(dt)

        def two(view):
            return view.rearrange("p (j c) -> p j c", j=2)

        c0 = Carve(0)
        key_a = c0.take(SC)
        key_b = c0.take(SC)
        hbuf, hpos, hneg, hcl = (two(c0.take(2 * HCOL)) for _ in range(4))
        kexp, kpos, kcap, kbuf, vbuf = (two(c0.take(2 * C)) for _ in range(5))
        field = [c0.take(SC // 2, BF16) for _ in range(4)]
        fint = [c0.take(SC, I32) for _ in range(2)]
        sel = c0.take(TPP * ITEMS // 2, BF16).rearrange("p (b k) -> p b k", b=TPP)
        selg = two(c0.take(2 * ITEMS))
        rep = c0.take(TPP * P, BF16).rearrange("p (s b m) -> p s b m", s=2, b=TPP)
        small = c0.take(16 * TPP).rearrange("p (s b) -> p s b", b=TPP)
        smalli = c0.take(4 * TPP, I32).rearrange("p (s b) -> p s b", b=TPP)
        binf = c0.take(ITEMS)
        binc = c0.take(ITEMS)
        acc = arena[:, 0:ACC]
        acc_t = acc.rearrange("p (t c) -> p t c", c=HROW)
        c1 = Carve(ACC)
        rows = c1.take(16 * HROW).rearrange("p (s c) -> p s c", c=HROW)
        onehot = c1.take(16 * P).rearrange("p (s c) -> p s c", c=P)
        onehot_t = c1.take(8 * P).rearrange("p (q c) -> p q c", q=2)
        score, leaky, expd = (c1.take(8 * HEADS).rearrange("p (q s h) -> p q s h", q=2, h=HEADS)
                              for _ in range(3))
        idx_buf = c1.take(16, I32)
        zden = c1.take(2 * MH)
        zrec = c1.take(2 * MH)
        tz = c1.take(2 * C)
        hT = c1.take(2 * C).rearrange("p (c n) -> p c n", c=CC)
        c2 = Carve(ACC)
        xin = two(c2.take(2 * C))
        rsum = two(c2.take(2 * HEADS))
        rrec = c2.take(2 * HEADS)
        hpn, gneg, ge1, ge2, gout = (c2.take(2 * C) for _ in range(5))
        n2, n2g, n2b, n2x = (two(c2.take(2 * C)) for _ in range(4))
        wd_s = arena[:, 0:WD]
        c3 = Carve(WD)
        fb1_s = c3.take(FC)
        fbg_s = c3.take(EXPERTS)
        bd_s = c3.take(EXPERTS * C)
        ptop = c3.take(2)
        lg, lexp, lsh, leq, lix = (two(c3.take(2 * EXPERTS)) for _ in range(5))
        lmax, lsum, letop, lidx = (c3.take(2) for _ in range(4))
        iota_e8 = c3.take(EXPERTS)
        oh_e = c3.take(EXPERTS * NT).rearrange("p (e t) -> p e t", e=EXPERTS)
        tok1 = c3.take(NT)
        fhT = c3.take(FC * PAIR)
        fhT_p = fhT.rearrange("p (c n) -> p c n", c=FC)
        gT = fhT.rearrange("p (j c n) -> p j c n", j=2, c=FC)
        c4 = Carve(c3.at)
        fw1_s = c3.take(CC * FF).rearrange("p (c n) -> p c n", c=CC)
        fwg_s = c3.take(FC * EXPERTS).rearrange("p (c n) -> p c n", c=FC)
        frow = two(c3.take(2 * FROW))
        grow = two(c4.take(2 * FROW))
        gx = two(c4.take(2 * C))
        yout = two(c4.take(2 * C))
        gidx = c4.take(2, I32)
        oidx = c4.take(2, I32)
        permi = c4.take(NSLOT, I32)
        assert c4.at <= c3.at
        rk_base, rk_all, rk_mul = (v.rearrange("p (e t) -> p e t", e=EXPERTS)
                                   for v in (ev.rearrange("p j c -> p (j c)")[:, 0:EXPERTS * NT],
                                                   em.rearrange("p j c -> p (j c)")[:, 0:EXPERTS * NT],
                                                   qs.rearrange("p c n -> p (c n)")[:, 0:EXPERTS * NT]))
        xTf = xT.rearrange("p c n -> p (c n)")
        xsf = xs.rearrange("p j c -> p (j c)")
        lane_oh = two(xTf[:, 0:2 * P])
        tile_oh = two(xTf[:, 2 * P:2 * P + 2 * NSLOT])
        posf = xsf[:, 0:NT]
        posi = xsf[:, 64:64 + 3 * NT].bitcast(I32).rearrange("p (s t) -> p s t", s=3)
        lanef = xsf[:, 220:220 + NT]
        tilef = xsf[:, 272:272 + NT]
        rt = xsf[:, 324:324 + 5 * EXPERTS].rearrange("p (s e) -> p s e", e=EXPERTS)
        rti = xsf[:, 364:364 + 2 * EXPERTS].bitcast(I32).rearrange("p (s e) -> p s e", e=EXPERTS)
        zeros_r = xsf[:, 384:384 + NSLOT]
        permz = xsf[:, 444:444 + NSLOT]
        sl_e = xTf[:, 2 * P + 2 * NSLOT:2 * P + 3 * NSLOT]

        pb = [ctx.enter_context(nc.psum_tensor(f"bank{n}", [P, 512], F32)) for n in range(8)]

        s_x = [sem(f"x_loaded{g}") for g in range(5)]
        s_keys = sem("keys_loaded")
        s_wgt = sem("weights_loaded")
        s_const = sem("constants_ready")
        s_cstep = sem("constant_step")
        s_stat = sem("row_stats")
        s_vare = sem("variance_plus_eps")
        s_std = sem("row_std")
        s_rstd = sem("row_rstd")
        s_norm = sem("row_norm_ready")
        s_fold = sem("folded_weight_in_psum")
        s_foldc = sem("folded_weight_ready")
        s_prep = sem("prepared_vectors")
        s_xn = sem("xn_ready")
        s_xtp = sem("xnT_in_psum")
        s_xt = sem("xnT_ready")
        s_hp = sem("h_in_psum")
        s_kvp = sem("kv_in_psum")
        s_hc = sem("h_copied")
        s_kc = sem("kv_copied")
        s_hs = sem("h_signs")
        s_hcl = sem("h_clean")
        s_as = sem("asrc_saved")
        s_km = sem("k_exp_capped")
        s_kk = sem("k_ready")
        s_gram = sem("gram_added")
        s_hw = [sem(f"h_row_stored{j}") for j in range(2)]
        s_kvbd0 = sem("kvbd_cleared")
        s_kvbd = sem("kvbd_ready")
        s_key = sem("key_built")
        s_st = [sem("sort_stream_a"), sem("sort_stream_b")]
        s_tp = sem("sort_transposed")
        s_te = [sem("sort_half_a_copied"), sem("sort_half_b_copied")]
        s_ns = sem("norm_step")
        s_sg = sem("sort_signed")
        s_dec = sem("decoded")
        s_cnt = sem("tile_counts")
        s_cross = sem("tile_prefix_in_psum")
        s_self = sem("selectors_ready")
        s_tab = sem("item_tables_in_psum")
        s_tabs = sem("item_table_steps")
        s_items = sem("item_tables_ready")
        s_acc0 = sem("acc_cleared")
        s_idx = sem("gather_rows_named")
        s_gat = [sem(f"rows_gathered{g}") for g in range(4)]
        s_oh = sem("onehot_ready")
        s_otp = sem("onehotT_in_psum")
        s_ot = sem("onehotT_ready")
        s_al = sem("src_score_in_psum")
        s_sc = sem("score_ready")
        s_lk = sem("leaky_ready")
        s_ex = sem("exp_ready")
        s_eg = sem("exp_guarded")
        s_msg = sem("messages_ready")
        s_agg = sem("aggregated")
        s_add = sem("added")
        m_xn = sem("m_xn")
        m_xi = sem("m_xn_in_place")
        m_tp = sem("m_xT_in_psum")
        m_xt = sem("m_xT_ready")
        m_qp = sem("m_q_in_psum")
        m_qe = sem("m_q_exp")
        m_qm = sem("m_q_capped")
        m_q = sem("m_q_ready")
        m_tps = sem("m_t_in_psum")
        m_z = sem("m_z_steps")
        m_tz = sem("m_tz_ready")
        m_r = sem("m_r_ready")
        m_bs = sem("m_r_stats")
        m_mv = sem("m_r_mean_var")
        n_xn = sem("n_ready")
        n_tp = sem("n_T_in_psum")
        n_xt = sem("n_T_ready")
        n_hp = sem("n_h_in_psum")
        n_h = sem("n_h_ready")
        n_yp = sem("n_y_in_psum")
        n_g = sem("n_gained")
        n_c = sem("n_shifted")
        n_y = sem("n_y_ready")
        n_bs = sem("n_y_stats")
        n_mv = sem("n_y_mean_var")
        u_x = sem("u_x_loaded")
        u_n = sem("u_normed")
        u_rs = sem("u_rowsum_steps")
        u_hp = sem("u_hp_divided")
        u_ng = sem("u_negative_part")
        u_e1 = sem("u_exp_once")
        u_e2 = sem("u_exp_twice")
        u_g = sem("u_gat_ready")
        u_p = sem("u_mixer_steps")
        u_m = sem("u_mixer_plus_x")
        u_x2 = sem("u_x2_ready")
        u_bs = sem("u_x2_stats")
        u_mv = sem("u_x2_mean_var")
        f_w = sem("f_weights_loaded")
        f_wd = sem("f_wd_loaded")
        f_c = sem("f_consts")
        f_xn = sem("f_xn_ready")
        f_tp = sem("f_xT_in_psum")
        f_xt = sem("f_xT_ready")
        f_hp = sem("f_h_in_psum")
        f_h = sem("f_h_ready")
        f_lp = sem("f_logits_in_psum")
        f_rt = sem("f_route_step")
        f_le = sem("f_logit_exp")
        f_x2 = sem("f_x2_copied")
        f_htp = sem("f_hrow_in_psum")
        f_hr = sem("f_hrow_ready")
        f_st = [sem(f"f_row_stored{j}") for j in range(2)]
        r_mm = sem("r_counts_in_psum")
        r_st = sem("r_step")
        r_oh = sem("r_onehots_ready")
        r_acc = sem("r_perm_added")
        r_done = sem("r_tables_ready")
        e_ix = sem("e_rows_named")
        e_clr = sem("e_rows_cleared")
        e_g = [sem(f"e_rows_gathered{j}") for j in range(2)]
        e_tp = sem("e_rowT_in_psum")
        e_t = sem("e_rowT_ready")
        e_yp = sem("e_y_in_psum")
        e_b = sem("e_bias_added")
        e_y = sem("e_y_ready")
        e_out = [sem(f"e_out_stored{j}") for j in range(2)]

        block = ctx.enter_context(nc.Block())

        AHEAD, GA, IA, FA = 2, 4, 8, 4
        MA = 2

        def head(view):
            return view.rearrange("p (e t) -> p e t", e=EXPERTS)

        SEGMENTS = [(0, NPAIR, 0), (NPAIR, 2, None), (NPAIR + 2, NPAIR, 1),
                    (2 * NPAIR + 2, NBATCH - 2 * NPAIR - 2, None)]

        def edge_batches(eng, batch, *mixer, between=None):
            for n, (at, count, kind) in enumerate(SEGMENTS):
                mix = None if kind is None else mixer[kind]
                start, end = at, at + count
                if mix:
                    batch(at, mix, 0, first=(at == 0), pairs_before=0)
                    batch(at + 1, mix, 1, pairs_before=1)
                    start += 2
                if end == NBATCH:
                    end -= 1
                with eng.Fori(start, end) as b:
                    batch(b, mix, b - at)
                if end == NBATCH - 1:
                    batch(end, None, 0, last=True)
                if between and mix:
                    between(n)

        keys = [key_a, key_b]
        turn_src, at = [], (sum(range(1, LOG_SC)) + LOG_SC) % 2
        for level in range(LOG_SC + 1, LOG_SLOTS + 1):
            for stages in (level - 7, 7):
                turn_src.append(keys[at])
                at = (at + 1 + stages) % 2
        TURNS = len(turn_src)
        sorted_keys = keys[at]
        NROUTE = 10

        def chunked(w):
            return w.rearrange("(c p) n -> p c n", p=P)

        WEIGHTS = [
            (wt_heads[:, :, :], gwt), (a_heads[:, :, :], ga), (w_gat[:, :, 0:C], chunked(gw)),
            (w_kv[:, :, :], chunked(wqkv_t[:, C:3 * C])), (w_q[:, :, :], chunked(wqkv_t[:, 0:C])),
            (w1g[:, :, :], chunked(w1_t)), (w2s[:, :, :], chunked(w2_t)),
            (b1col[:, :], b1), (g1col[:, :], ln1_g), (be1col[:, :], ln1_b),
            (g1rep[:, :], ln1_g_rows), (c1rep[:, :], ln1_b_rows), (b2rep[:, :], b2),
            (g2rep[:, :], ln2_g), (c2rep[:, :], ln2_b),
        ]
        N_WEIGHTS = len(WEIGHTS)

        trp = [pb[0][:, 0:C], pb[0][:, C:2 * C]]
        hps = [pb[1][:, 0:HCOL], pb[2][:, 0:HCOL]]
        kvps = [pb[3], pb[4]]
        gram = pb[5][:, 0:CC * (P + 1)].rearrange("p (c m) -> p c m", c=CC)
        sortp = [pb[6], pb[7]]
        psT, psA = pb[0], pb[1]
        psG = [pb[2], pb[3], pb[6], pb[7]]
        score_ps = psA[:, 0:32].rearrange("p (q s h) -> p q s h", q=2, h=HEADS)
        den_ps = psA[:, 32:32 + 2 * MH].rearrange("p (u c h) -> p u c h", u=2, c=CC)
        mixT = pb[4][:, :].rearrange("p (c n) -> p c n", c=CC)
        mixQ = pb[5][:, :].rearrange("p (c n) -> p c n", c=CC)
        mixY = pb[4][:, :].rearrange("p (u n) -> p u n", u=2)

        due_reg = {}

        def held(eng, signal, value):
            due = due_reg[eng.engine]
            eng.reg_mov(due, value)
            eng.wait_ge(s_const, 1)
            eng.wait_ge(signal, due)

        def ones_start(eng, sems, n):
            for s in sems:
                eng.sem_inc(s, n)

        @block.sync
        def _(sp):
            due_reg[sp.engine] = sp.alloc_register("due_count")
            for g in range(5):
                t0 = g * (NT // 5)
                sp.dma_start(xall[:, t0:t0 + NT // 5, :],
                             x[t0 * P:(t0 + NT // 5) * P, :].rearrange("(t p) c -> p t c", p=P)
                             ).then_inc(s_x[g], 16)
                if g == 0:
                    sp.dma_start(key_a.bitcast(I32), src.rearrange("(p c) -> p c", p=P)).then_inc(s_keys, 16)
                    sp.dma_start(key_b.bitcast(I32), dst.rearrange("(p c) -> p c", p=P)).then_inc(s_keys, 16)
            def store(i, j):
                held(sp, s_hcl, 2 * i + j + 1 + AHEAD)
                sp.dma_start(node_table[ds((2 * i + j) * P, P), :], hcl[:, j, 0:HROW]).then_inc(s_hw[j], 16)
            with sp.Fori(0, NPAIR) as i:
                store(i, 0)
                store(i, 1)
            def reload(i):
                held(sp, u_p, 3 * i)
                sp.dma_start(xin, x[ds(2 * i * P, 2 * P), :].rearrange("(t p) c -> p t c", p=P)
                             ).then_inc(u_x, 16)
            sp.wait_ge(s_add, ITEMS + IA)
            with sp.Fori(0, NPAIR) as i:
                reload(i)
            sp.wait_ge(u_x2, NPAIR)
            sp.dma_start(fw1_s, fw1.rearrange("(c p) n -> p c n", p=P)).then_inc(f_w, 16)
            sp.dma_start(fwg_s, fwg.rearrange("(c p) n -> p c n", p=P)).then_inc(f_w, 16)
            sp.dma_start(fb1_s, fb1).then_inc(f_w, 16)
            sp.dma_start(fbg_s, fbg).then_inc(f_w, 16)
            sp.dma_start(bd_s, fbd).then_inc(f_w, 16)
            for e in range(EXPERTS):
                sp.dma_start(wd_s[:, e * FC * C:(e + 1) * FC * C].rearrange("p (c n) -> p c n", c=FC),
                             fwd[e].rearrange("(c p) n -> p c n", p=P)).then_inc(f_wd, 16)
            def store_row(i, u):
                held(sp, f_hr, 4 * i + 2 * u + 2 + AHEAD)
                held(sp, f_x2, 2 * i + u + 1)
                sp.dma_start(expert_table[ds((2 * i + u) * P, P), :], frow[:, u, :]).then_inc(f_st[u], 16)
            with sp.Fori(0, NPAIR) as i:
                store_row(i, 0)
                store_row(i, 1)

        @block.gpsimd
        def _(pool):
            due_reg[pool.engine] = pool.alloc_register("due_count")
            ones_start(pool, (s_hs, s_hcl, s_as, s_km, s_kk), AHEAD)
            pool.memset(ident[:, :], 0.0).then_inc(s_cstep, 1)
            pool.memset(upper[:, :], 1.0).then_inc(s_cstep, 1)
            pool.memset(valid[:, :], 1.0).then_inc(s_cstep, 1)
            pool.memset(ones[:, :], 1.0)
            pool.memset(minus1[:, :], -1.0)
            pool.memset(ev[:, :, :], 0.0)
            pool.memset(em[:, :, :], 0.0)
            pool.memset(kbuf[:, 1, :], 0.0)
            pool.memset(vbuf[:, 1, :], 0.0)
            pool.memset(kvbd[:, :, :], 0.0)
            pool.iota(iota_p[:, :], [[1, P]], 0, 0, allow_small_or_imprecise_dtypes=True)
            pool.iota(iota_k[:, :], [[1, ITEMS]], 0, 0, allow_small_or_imprecise_dtypes=True)
            pool.iota(pm1[:, :], [[-2, 2]], 1, 0, allow_small_or_imprecise_dtypes=True)
            pool.iota(part_i[:, :], [[0, 8]], 0, 1)
            pool.wait_ge(s_cstep, 3)
            pool.affine_select(out=ident[:, :], in_=ident[:, :], compare_op=ALU.not_equal, fill=1.0,
                               base=0, pattern=[[-1, P]], channel_multiplier=1)
            pool.affine_select(out=upper[:, :], in_=upper[:, :], compare_op=ALU.is_gt, fill=0.0,
                               base=0, pattern=[[1, P]], channel_multiplier=-1)
            pool.affine_select(out=valid[:, :], in_=valid[:, :], compare_op=ALU.is_ge, fill=0.0,
                               base=N_NODES - 1 + P, pattern=[[-P, NT + 1]], channel_multiplier=-1
                               ).then_inc(s_const, 1)

            def guard(i, j):
                t = 2 * i + j
                done, two_ago = t + 1 + AHEAD, t + 1
                held(pool, s_hc, done)
                held(pool, s_hcl, two_ago)
                pool.tensor_scalar(hpos[:, j, :], hbuf[:, j, :], 0.0, None, op0=ALU.max)
                pool.tensor_scalar(hneg[:, j, :], hbuf[:, j, :], 0.0, None, op0=ALU.min).then_inc(s_hs, 1)
                held(pool, s_hs, done)
                held(pool, s_hw[j], 16 * i)
                held(pool, s_as, two_ago)
                pool.tensor_tensor(hcl[:, j, :], hpos[:, j, :], hneg[:, j, :], op=ALU.add).then_inc(s_hcl, 1)
                held(pool, s_kc, done)
                held(pool, s_kk, two_ago)
                pool.tensor_scalar(kcap[:, j, :], kexp[:, j, :], 1.0, None, op0=ALU.min).then_inc(s_km, 1)
                held(pool, s_hcl, done)
                pool.tensor_copy(asrc[:, ds(t * HEADS, HEADS)], hcl[:, j, HROW:HCOL]).then_inc(s_as, 1)
                held(pool, s_km, done)
                held(pool, s_gram, two_ago)
                pool.tensor_tensor(kbuf[:, j, :], kcap[:, j, :], kpos[:, j, :], op=ALU.add).then_inc(s_kk, 1)
            with pool.Fori(0, NPAIR) as i:
                guard(i, 0)
                guard(i, 1)

            pool.wait_ge(s_hw[0], 16 * NPAIR)
            pool.wait_ge(s_hw[1], 16 * NPAIR)
            def gather(b):
                for g in range(4):
                    q = 4 * b + g
                    held(pool, s_idx, q + 1)
                    held(pool, s_agg, 2 * q - 8 + IA + 2)
                    for s in range(4 * g, 4 * g + 4):
                        pool.indirect_dma_start(
                            out=rows[:, s, :], out_offset=None, in_=node_table[:, :],
                            in_offset=bass.IndirectOffsetOnAxis(ap=idx_buf[:, s:s + 1], axis=0)
                        ).then_inc(s_gat[g], 16)
            with pool.Fori(0, NBATCH) as b:
                gather(b)

            def mixer_out(i):
                held(pool, u_n, 2 * i + 2)
                held(pool, u_p, 3 * i)
                pool.tensor_tensor(n2g, n2, g2rep[:, None, :].to_broadcast([P, 2, C]), op=ALU.mult
                                   ).then_inc(u_p, 1)
                held(pool, u_p, 3 * i + 1)
                pool.tensor_tensor(n2b, n2g, c2rep[:, None, :].to_broadcast([P, 2, C]), op=ALU.add
                                   ).then_inc(u_p, 1)
                held(pool, u_p, 3 * i + 2)
                held(pool, u_x, 16 * i + 16)
                held(pool, u_x2, i)
                pool.tensor_tensor(n2x, n2b, xin, op=ALU.add).then_inc(u_p, 1)
            with pool.Fori(0, NPAIR) as i:
                mixer_out(i)

            pool.wait_ge(u_x2, NPAIR)
            pool.iota(tok1, [[P, NT]], 1, 1, allow_small_or_imprecise_dtypes=True)
            pool.iota(iota_e8, [[1, EXPERTS]], -EXPERTS, 0, allow_small_or_imprecise_dtypes=True)
            pool.memset(frow[:, :, FF + C:FROW], 0.0).then_inc(f_c, 1)
            pool.wait_ge(f_c, 1)
            def row_tail(i, u):
                t = 2 * i + u
                held(pool, f_st[u], 16 * i)
                pool.tensor_copy(frow[:, u, FF:FF + C], xall[:, t, :] if isinstance(t, int)
                                 else xall[:, ds(t, 1), :].rearrange("p a c -> p (a c)"))
                held(pool, f_rt, NROUTE * i + 5)
                pool.tensor_copy(frow[:, u, FF + C:FF + C + 1], ptop[:, u:u + 1]).then_inc(f_x2, 1)
            with pool.Fori(0, NPAIR) as i:
                row_tail(i, 0)
                row_tail(i, 1)

            pool.wait_ge(f_st[0], 16 * NPAIR)
            pool.wait_ge(f_st[1], 16 * NPAIR)
            def take(s, u):
                held(pool, e_ix, s + 1)
                pool.indirect_dma_start(
                    out=grow[:, u, :], out_offset=None, in_=expert_table[:, :],
                    in_offset=bass.IndirectOffsetOnAxis(ap=gidx[:, u:u + 1], axis=0),
                    bounds_check=ROWS - 1, oob_is_err=False).then_inc(e_g[u], 16)
            def give(s, u):
                held(pool, e_y, s + 1 + AHEAD)
                pool.indirect_dma_start(
                    out=out[:, :], out_offset=bass.IndirectOffsetOnAxis(ap=oidx[:, u:u + 1], axis=0),
                    in_=yout[:, u, :], in_offset=None,
                    bounds_check=ROWS - 1, oob_is_err=False).then_inc(e_out[u], 16)
            take(0, 0)
            def experts(i, last):
                take(2 * i + 1, 1)
                give(2 * i, 0)
                if not last:
                    take(2 * i + 2, 0)
                give(2 * i + 1, 1)
            with pool.Fori(0, NSLOT // 2 - 1) as i:
                experts(i, False)
            experts(NSLOT // 2 - 1, True)
            pool.wait_ge(e_out[0], 16 * (NSLOT // 2))
            pool.wait_ge(e_out[1], 16 * (NSLOT // 2))

        @block.tensor
        def _(pe):
            ones_start(pe, (s_xtp, s_hp, s_kvp), AHEAD)
            ones_start(pe, (s_otp, s_al), GA)
            ones_start(pe, (s_agg,), IA)
            ones_start(pe, (e_yp,), AHEAD)
            ones_start(pe, (m_tp, m_qp, m_tps, n_tp, n_hp, n_yp), MA)
            pe.sem_inc(s_gram, 1)

            def transpose(psum, tile):
                return pe.transpose(psum, tile, ident[:, :])

            pe.wait_ge(s_const, 1)
            pe.wait_ge(s_wgt, 16 * N_WEIGHTS)
            for c in range(CC):
                for h in range(HEADS):
                    at = (c * HEADS + h) * 2
                    last = pe.matmul(pb[7][:, at:at + 2], lhsT=wt_heads[:, h, c * P:(c + 1) * P],
                                     rhs=a_heads[:, h, :], start=True, stop=True)
            last.then_inc(s_fold, 1)
            pe.wait_ge(s_foldc, 1)
            for oc in range(CC):
                for c in range(CC):
                    last = pe.matmul(pb[7][:, 64 + oc:65 + oc], lhsT=w1g[:, c, oc * P:(oc + 1) * P],
                                     rhs=be1col[:, c:c + 1], start=(c == 0), stop=(c == CC - 1))
            last.then_inc(s_fold, 1)

            def node_t(t, j):
                pe.wait_ge(s_xn, t + 1 + AHEAD)
                pe.wait_ge(s_xt, t + 1)
                for c in range(CC):
                    last = transpose(trp[j][:, c * P:(c + 1) * P], xs[:, j, c * P:(c + 1) * P])
                last.then_inc(s_xtp, 1)

            def node_mm(t, j):
                pe.wait_ge(s_xt, t + 1 + AHEAD)
                pe.wait_ge(s_hc, t + 1)
                for c in range(CC):
                    last = pe.matmul(hps[j], lhsT=xT[:, c, j * P:(j + 1) * P], rhs=w_gat[:, c, :],
                                     start=(c == 0), stop=(c == CC - 1))
                last.then_inc(s_hp, 1)
                pe.wait_ge(s_kc, t + 1)
                for c in range(CC):
                    last = pe.matmul(kvps[j][:, :], lhsT=xT[:, c, j * P:(j + 1) * P], rhs=w_kv[:, c, :],
                                     start=(c == 0), stop=(c == CC - 1))
                last.then_inc(s_kvp, 1)

            def node_gram(t, j):
                pe.wait_ge(s_kk, t + 1 + AHEAD)
                for c in range(CC):
                    pe.matmul(gram[:, c, 0:P], lhsT=kbuf[:, j, c * P:(c + 1) * P],
                              rhs=vbuf[:, j, c * P:(c + 1) * P], start=False, stop=False,
                              skip_group_check=True)
                    last = pe.matmul(gram[:, c, P:P + 1], lhsT=kbuf[:, j, c * P:(c + 1) * P],
                                     rhs=valid[:, ds(t + 1, 1)], start=False, stop=False,
                                     skip_group_check=True)
                last.then_inc(s_gram, 1)

            pe.matmul(pb[5][:, 0:CC * (P + 1)], lhsT=ones[:, :],
                      rhs=ev.rearrange("p j c -> p (j c)")[:, 0:CC * (P + 1)], start=True, stop=False,
                      skip_group_check=True)
            node_t(0, 0)
            def node_pair(i, last):
                node_t(2 * i + 1, 1)
                node_mm(2 * i, 0)
                node_gram(2 * i - 1, 1)
                if not last:
                    node_t(2 * i + 2, 0)
                node_mm(2 * i + 1, 1)
                node_gram(2 * i, 0)
            with pe.Fori(0, NPAIR - 1) as i:
                node_pair(i, False)
            node_pair(NPAIR - 1, True)
            node_gram(NT - 1, 1)

            for n in range(TURNS):
                pe.wait_ge(s_sg, n + 1)
                for half in range(2):
                    for k in range(4):
                        blk = 4 * half + k
                        last = transpose(sortp[half][:, k * P:(k + 1) * P],
                                         turn_src[n][:, blk * P:(blk + 1) * P])
                    last.then_inc(s_tp, 1)

            pe.wait_ge(s_cnt, 1)
            pe.matmul(pb[0][:, 0:1], lhsT=upper[:, :], rhs=small[:, 15, 0:1], start=True, stop=True
                      ).then_inc(s_cross, 1)
            pe.wait_ge(s_dec, 4)
            pe.wait_ge(s_self, TPP)
            for f in range(2):
                for h in range(2):
                    for n in range(2 * TPP):
                        b, part = n // 2, n % 2
                        blk = 2 * b + h
                        last = pe.matmul(pb[1 + 2 * f + h][:, 0:ITEMS],
                                         lhsT=field[2 * f + part][:, blk * P:(blk + 1) * P],
                                         rhs=sel[:, b, :], start=(n == 0), stop=(n == 2 * TPP - 1))
            for n in range(2 * TPP):
                b, part = n // 2, n % 2
                last = pe.matmul(pb[5][:, 0:ITEMS], lhsT=rep[:, part, b, :], rhs=sel[:, b, :],
                                 start=(n == 0), stop=(n == 2 * TPP - 1))
            last.then_inc(s_tab, 1)

            def onehot_transpose(q, g):
                pe.wait_ge(s_oh, q + 1 + GA)
                pe.wait_ge(s_ot, q + GA)
                for n in range(4):
                    last = transpose(psT[:, n * P:(n + 1) * P], onehot[:, 4 * g + n, :])
                last.then_inc(s_otp, 1)

            def src_scores(q, g, bins):
                pe.wait_ge(s_ot, q + 1 + GA)
                pe.wait_ge(s_sc, q + GA)
                for n in range(4):
                    last = pe.matmul(score_ps[:, g % 2, n, :], lhsT=onehot_t[:, g % 2, n * P:(n + 1) * P],
                                     rhs=asrc[:, ds(bins[n // 2], HEADS)], start=True, stop=True,
                                     skip_group_check=True)
                last.then_inc(s_al, 1)

            def aggregate(q, g):
                pe.wait_ge(s_msg, q + 1 + GA)
                for m in range(2):
                    pe.wait_ge(s_add, 2 * q + m - 4 + 1 + IA)
                    for h in range(2):
                        s = 4 * g + 2 * m + h
                        last = pe.matmul(psG[2 * (g % 2) + m][:, 0:HROW], lhsT=onehot[:, s, :], rhs=rows[:, s, :],
                                         start=(h == 0), stop=(h == 1))
                    last.then_inc(s_agg, 1)

            def mix_turn(i, normed, free):
                pe.wait_ge(normed, 2 * (i + 1 + MA))
                pe.wait_ge(free, i - 1 + MA)
                for c in range(CC):
                    for u in range(2):
                        last = transpose(mixT[:, c, u * P:(u + 1) * P], xs[:, u, c * P:(c + 1) * P])
                return last

            def mix_columns(w, oc):
                for c in range(CC):
                    last = pe.matmul(mixQ[:, oc, :], lhsT=w[:, c, oc * P:(oc + 1) * P],
                                     rhs=xT[:, c, :], start=(c == 0), stop=(c == CC - 1))
                return last

            def mix_q_products(i):
                pe.wait_ge(m_q, i + 1 + MA)
                pe.wait_ge(m_tz, i + MA)
                for u in range(2):
                    for c in range(CC):
                        pe.matmul(mixY[:, u, c * P:(c + 1) * P], lhsT=qs[:, c, u * P:(u + 1) * P],
                                  rhs=kvbd[:, c, 0:P], start=True, stop=True)
                        last = pe.matmul(den_ps[:, u, c, :], lhsT=qs[:, c, u * P:(u + 1) * P],
                                         rhs=kvbd[:, c, P:P + HEADS], start=True, stop=True,
                                         skip_group_check=True)
                last.then_inc(m_tps, 1)

            def mix_q(i, g, before):
                if g == 0:
                    mix_turn(i, m_xn, m_tz).then_inc(m_tp, 1)
                if g == 1:
                    pe.wait_ge(m_xt, i + 1 + MA)
                    pe.wait_ge(m_q, i + MA)
                    mix_columns(w_q, 0)
                if g == 2:
                    mix_columns(w_q, 1).then_inc(m_qp, 1)
                if g == 3 and before >= 1:
                    mix_q_products(i - 1)

            def mix_mlp_products(i):
                pe.wait_ge(n_h, 2 * (i + 1 + MA))
                pe.wait_ge(n_y, i + MA)
                for u in range(2):
                    for oc in range(CC):
                        last = pe.matmul(mixY[:, u, :], lhsT=hT[:, oc, u * P:(u + 1) * P],
                                         rhs=w2s[:, oc, :], start=(oc == 0), stop=(oc == CC - 1))
                last.then_inc(n_yp, 1)

            def mix_mlp(i, g, before):
                if g == 0:
                    mix_turn(i, n_xn, n_y).then_inc(n_tp, 1)
                if g == 1:
                    pe.wait_ge(n_xt, i + 1 + MA)
                    pe.wait_ge(n_h, 2 * (i + MA))
                    mix_columns(w1g, 0)
                if g == 2:
                    mix_columns(w1g, 1).then_inc(n_hp, 1)
                if g == 3 and before >= 1:
                    mix_mlp_products(i - 1)

            def between(n):
                (mix_q_products if n == 0 else mix_mlp_products)(NPAIR - 1)

            asrc_regs = [pe.alloc_register(f"asrc_bin{n}") for n in range(PER_BATCH)]

            def edge_batch(b, mix, i, first=False, last=False, pairs_before=2):
                pe.load(asrc_regs, bin_asrc[0:1, ds(b * PER_BATCH + 2, PER_BATCH)])
                bins = [pe.snap(r, min_val=0, max_val=(BINS - 1) * HEADS) for r in asrc_regs]
                for g in range(4):
                    q = 4 * b + g
                    if not (last and g == 3):
                        src_scores(q + 1, (g + 1) % 4, bins[2 * g:2 * g + 2])
                    if not (first and g == 0):
                        aggregate(q - 1, (g - 1) % 4)
                    if not (last and g >= 2):
                        onehot_transpose(q + 2, (g + 2) % 4)
                    if mix:
                        mix(i, g, pairs_before)

            pe.wait_ge(s_items, 1)
            pe.wait_ge(s_as, NT + AHEAD)
            pe.wait_ge(s_kvbd, 1)
            onehot_transpose(0, 0)
            pe.load(asrc_regs[0:2], bin_asrc[0:1, 0:2])
            src_scores(0, 0, [pe.snap(r, min_val=0, max_val=(BINS - 1) * HEADS) for r in asrc_regs[0:2]])
            onehot_transpose(1, 1)
            edge_batches(pe, edge_batch, mix_q, mix_mlp, between=between)
            aggregate(4 * NBATCH - 1, 3)

            fT = pb[0][:, :].rearrange("p (c n) -> p c n", c=CC)
            lps = pb[5][:, 0:2 * EXPERTS].rearrange("p (u e) -> p u e", u=2)
            def ff_t(i):
                pe.wait_ge(f_xn, 2 * i + 2)
                pe.wait_ge(f_xt, i)
                for c in range(CC):
                    for u in range(2):
                        last = transpose(fT[:, c, u * P:(u + 1) * P], xs[:, u, c * P:(c + 1) * P])
                last.then_inc(f_tp, 1)
            def ff_pair(i, last_pair):
                pe.wait_ge(f_xt, i + 1)
                for oc in range(FC):
                    pe.wait_ge(f_h, FC * i + oc + 1)
                    for c in range(CC):
                        last = pe.matmul(pb[1 + oc % 4][:, 0:C],
                                         lhsT=fw1_s[:, c, oc * P:(oc + 1) * P], rhs=xT[:, c, :],
                                         start=(c == 0), stop=(c == CC - 1), skip_group_check=True)
                    last.then_inc(f_hp, 1)
                if not last_pair:
                    ff_t(i + 1)
                pe.wait_ge(f_h, FC * i + FC + FA)
                pe.wait_ge(f_rt, NROUTE * i)
                for u in range(2):
                    for c in range(FC):
                        last = pe.matmul(lps[:, u, :], lhsT=fhT_p[:, c, u * P:(u + 1) * P],
                                         rhs=fwg_s[:, c, :], start=(c == 0), stop=(c == FC - 1))
                last.then_inc(f_lp, 1)
                for n in range(4):
                    u, half = n // 2, n % 2
                    pe.wait_ge(f_hr, 4 * i + n + 1)
                    for k in range(4):
                        last = transpose(pb[6 + half][:, k * P:(k + 1) * P],
                                         fhT_p[:, 4 * half + k, u * P:(u + 1) * P])
                    last.then_inc(f_htp, 1)
            pe.wait_ge(f_w, 16 * 5)
            ff_t(0)
            with pe.Fori(0, NPAIR - 1) as i:
                ff_pair(i, False)
            ff_pair(NPAIR - 1, True)

            pe.wait_ge(f_rt, NROUTE * NPAIR)
            ohf = oh_e.rearrange("p e t -> p (e t)")
            pe.matmul(pb[1][:, 0:EXPERTS * NT], lhsT=upper[:, :], rhs=ohf, start=True, stop=True)
            pe.matmul(pb[2][:, 0:EXPERTS * NT], lhsT=ones[:, :], rhs=ohf, start=True, stop=True
                      ).then_inc(r_mm, 1)
            perm = pb[3][:, 0:NSLOT]
            pe.wait_ge(r_st, 1)
            pe.matmul(perm, lhsT=ones[:, :], rhs=zeros_r[:, 0:NSLOT], start=True, stop=False,
                      skip_group_check=True)
            def permute(i, u):
                pe.wait_ge(r_oh, 2 * i + u + 1)
                pe.matmul(perm, lhsT=lane_oh[:, u, :], rhs=tile_oh[:, u, :], start=False, stop=False,
                          skip_group_check=True).then_inc(r_acc, 1)
            pe.wait_ge(r_mm, 1)
            with pe.Fori(0, NPAIR) as i:
                permute(i, 0)
                permute(i, 1)

            wd_regs = [pe.alloc_register(f"wd_slot{n}") for n in range(2)]
            def row_t(s, u, i):
                pe.wait_ge(e_g[u], 16 * i + 16)
                pe.wait_ge(e_t, 2 * s + 2)
                for half in range(2):
                    for k in range(4):
                        blk = 4 * half + k
                        last = transpose(pb[2 * u + half][:, k * P:(k + 1) * P],
                                         grow[:, u, blk * P:(blk + 1) * P])
                    last.then_inc(e_tp, 1)
            def expert_mm(s, u, off):
                pe.wait_ge(e_t, 2 * s + 2 + 2 * AHEAD)
                pe.wait_ge(e_y, s + 1)
                for c in range(FC):
                    last = pe.matmul(pb[4 + u][:, 0:C], lhsT=gT[:, u, c, :], rhs=wd_s[:, ds(off + c * C, C)],
                                     start=(c == 0), stop=(c == FC - 1))
                last.then_inc(e_yp, 1)
            def expert_pair(i, last_pair):
                pe.load(wd_regs, slot_wd[0:1, ds(2 * i, 2)])
                offs = [pe.snap(r, min_val=0, max_val=(EXPERTS - 1) * FC * C) for r in wd_regs]
                row_t(2 * i + 1, 1, i)
                expert_mm(2 * i, 0, offs[0])
                if not last_pair:
                    row_t(2 * i + 2, 0, i + 1)
                expert_mm(2 * i + 1, 1, offs[1])
            pe.wait_ge(r_done, 1)
            pe.wait_ge(f_wd, 16 * EXPERTS)
            row_t(0, 0, 0)
            with pe.Fori(0, NSLOT // 2 - 1) as i:
                expert_pair(i, False)
            expert_pair(NSLOT // 2 - 1, True)

        @block.scalar
        def _(act):
            ones_start(act, (s_xn, s_xt, s_hc, s_kc), AHEAD)
            ones_start(act, (s_ot, s_ex), GA)
            ones_start(act, (f_h,), FA)
            ones_start(act, (e_t,), 2 * AHEAD)
            ones_start(act, (m_xt, m_qe, n_xt), MA)
            ones_start(act, (m_xn, m_xi, n_xn, n_h), 2 * MA)
            due_reg[act.engine] = act.alloc_register("due_count")
            for dst_ap, src_ap in WEIGHTS:
                act.dma_start(dst_ap, src_ap).then_inc(s_wgt, 16)

            def root(n):
                act.wait_ge(s_vare, n)
                act.activation(std[:, :], st_s[:, 2, :], ACT.Sqrt).then_inc(s_std, 1)

            def normalise(dst_ap, t, signal):
                act.activation(dst_ap, tile(t), ACT.Identity, bias=nmr[:, ds(t, 1)],
                               scale=rstd[:, ds(t, 1)]).then_inc(signal, 1)

            def tile(t):
                return xall[:, ds(t, 1), :].rearrange("p a c -> p (a c)")

            root(1)
            act.wait_ge(s_rstd, 1)

            def node_norm(t, j):
                act.wait_ge(s_xtp, t + 1)
                normalise(xs[:, j, :], t, s_xn)

            def node_copies(t, j):
                done, two_ago = t + 1 + AHEAD, t + 1
                act.wait_ge(s_xtp, done)
                act.wait_ge(s_kvp, two_ago)
                act.activation(xT[:, :, j * P:(j + 1) * P], trp[j].rearrange("p (c n) -> p c n", c=CC),
                               ACT.Copy).then_inc(s_xt, 1)

            def node_out(t, j):
                done, two_ago = t + 1 + AHEAD, t + 1
                act.wait_ge(s_hp, done)
                act.wait_ge(s_hs, two_ago)
                act.activation(hbuf[:, j, :], hps[j], ACT.Copy).then_inc(s_hc, 1)
                act.wait_ge(s_kvp, done)
                act.wait_ge(s_kk, two_ago)
                act.activation(kexp[:, j, :], kvps[j][:, 0:C], ACT.Exp)
                act.activation(kpos[:, j, :], kvps[j][:, 0:C], ACT.Relu)
                act.wait_ge(s_gram, two_ago)
                act.activation(vbuf[:, j, :], kvps[j][:, C:2 * C], ACT.Copy).then_inc(s_kc, 1)

            node_norm(0, 0)
            node_copies(0, 0)
            def node_pair(i, last):
                node_norm(2 * i + 1, 1)
                node_copies(2 * i + 1, 1)
                node_out(2 * i, 0)
                if not last:
                    node_norm(2 * i + 2, 0)
                    node_copies(2 * i + 2, 0)
                node_out(2 * i + 1, 1)
            with act.Fori(0, NPAIR - 1) as i:
                node_pair(i, False)
            node_pair(NPAIR - 1, True)
            act.wait_ge(s_gram, NT + 2)
            act.wait_ge(s_const, 1)
            for c in range(CC):
                for h in range(P // MD):
                    rs = slice(h * MD, (h + 1) * MD)
                    act.activation(kvbd[rs, c, h * MD:(h + 1) * MD], gram[rs, c, h * MD:(h + 1) * MD], ACT.Copy)
                    last = act.activation(kvbd[rs, c, P + h:P + h + 1], gram[rs, c, P:P + 1], ACT.Copy)
            last.then_inc(s_kvbd, 1)

            for n in range(TURNS):
                level = LOG_SC + 1 + n // 2
                act.wait_ge(s_tp, 2 * n + 1)
                dst_ap = keys[1 - (0 if turn_src[n] is keys[0] else 1)][:, 0:SC // 2]
                if n % 2 and level < LOG_SLOTS:
                    act.activation(dst_ap, sortp[0][:, :], ACT.Copy,
                                   scale=sign[:, level - LOG_SC:level - LOG_SC + 1]).then_inc(s_te[0], 1)
                else:
                    act.activation(dst_ap, sortp[0][:, :], ACT.Copy).then_inc(s_te[0], 1)

            def copy_onehot(q, g):
                act.wait_ge(s_otp, q + 1 + GA)
                act.wait_ge(s_al, q - 2 + 1 + GA)
                act.activation(onehot_t[:, g % 2, :], psT[:, :], ACT.Copy).then_inc(s_ot, 1)

            def mix_q(i, g, before):
                if g == 0:
                    act.wait_ge(m_tp, i + MA)
                    for u in range(2):
                        normalise(xs[:, u, :], 2 * i + u, m_xn)
                    held(act, m_xn, 2 * (i + 1 + MA))
                    for u in range(2):
                        normalise(tile(2 * i + u), 2 * i + u, m_xi)
                if g == 1:
                    act.wait_ge(m_tp, i + 1 + MA)
                    act.activation(xT[:, :, :], mixT[:, :, :], ACT.Copy).then_inc(m_xt, 1)
                if g == 3:
                    act.wait_ge(m_qp, i + 1 + MA)
                    act.wait_ge(m_qm, i + MA)
                    act.activation(ev.rearrange("p j c -> p (j c)"), pb[5][:, :], ACT.Exp).then_inc(m_qe, 1)

            def mix_gelu(i):
                act.wait_ge(n_hp, i + 1 + MA)
                act.wait_ge(n_yp, i + MA)
                for oc in range(CC):
                    act.activation(hT[:, oc, :], mixQ[:, oc, :], ACT.Gelu,
                                   bias=b1eff[:, oc:oc + 1]).then_inc(n_h, 1)

            def mix_mlp(i, g, before):
                if g == 0:
                    act.wait_ge(n_g, i + MA)
                    for u in range(2):
                        normalise(xs[:, u, :], 2 * i + u, n_xn)
                    if before >= 1:
                        mix_gelu(i - 1)
                if g == 1:
                    act.wait_ge(n_tp, i + 1 + MA)
                    act.activation(xT[:, :, :], mixT[:, :, :], ACT.Copy).then_inc(n_xt, 1)

            def edge_batch(b, mix, i, first=False, last=False, pairs_before=2):
                for g in range(4):
                    q = 4 * b + g
                    act.wait_ge(s_lk, q + 1 + GA)
                    act.wait_ge(s_eg, q - 2 + 1 + GA)
                    act.activation(expd[:, g % 2], leaky[:, g % 2], ACT.Exp, scale=-1.0).then_inc(s_ex, 1)
                    if mix:
                        mix(i, g, pairs_before)
                    if not (last and g >= 2):
                        copy_onehot(q + 2, (g + 2) % 4)

            def between(n):
                if n == 0:
                    root(2)
                    act.wait_ge(s_rstd, 2)
                else:
                    mix_gelu(NPAIR - 1)

            copy_onehot(0, 0)
            copy_onehot(1, 1)
            edge_batches(act, edge_batch, mix_q, mix_mlp, between=between)

            root(3)
            act.wait_ge(s_rstd, 3)
            def x2_pair(i):
                act.wait_ge(u_p, 3 * i)
                for u in range(2):
                    normalise(n2[:, u, :], 2 * i + u, u_n)
                act.wait_ge(u_ng, i + 1)
                act.activation(ge1, gneg, ACT.Exp).then_inc(u_e1, 1)
                act.wait_ge(u_e1, i + 1)
                act.wait_ge(u_g, i)
                act.activation(ge2, ge1, ACT.Exp, bias=minus1[:, :]).then_inc(u_e2, 1)
            with act.Fori(0, NPAIR) as i:
                x2_pair(i)

            root(4)
            act.wait_ge(s_rstd, 4)
            act.wait_ge(f_w, 16 * 5)
            def ff_norm(i):
                act.wait_ge(f_tp, i)
                for u in range(2):
                    normalise(xs[:, u, :], 2 * i + u, f_xn)
            def ff_pair(i, last_pair):
                if not last_pair:
                    ff_norm(i + 1)
                act.wait_ge(f_htp, 4 * i)
                for oc in range(FC):
                    act.wait_ge(f_hp, FC * i + oc + 1)
                    act.activation(fhT_p[:, oc, :], pb[1 + oc % 4][:, 0:C],
                                   ACT.Gelu, bias=fb1_s[:, oc:oc + 1]).then_inc(f_h, 1)
                act.wait_ge(f_rt, NROUTE * i + 3)
                act.activation(lexp, lsh, ACT.Exp).then_inc(f_le, 1)
            ff_norm(0)
            with act.Fori(0, NPAIR - 1) as i:
                ff_pair(i, False)
            ff_pair(NPAIR - 1, True)

            act.wait_ge(r_done, 1)
            def expert_copies(s, u):
                act.wait_ge(e_yp, s + 1)
                for half in range(2):
                    act.wait_ge(e_tp, 2 * s + half + 1)
                    act.activation(gT[:, u, 4 * half:4 * half + 4, :],
                                   pb[2 * u + half][:, :].rearrange("p (k n) -> p k n", k=4),
                                   ACT.Copy).then_inc(e_t, 1)
            with act.Fori(0, NSLOT // 2) as i:
                expert_copies(2 * i, 0)
                expert_copies(2 * i + 1, 1)

        @block.vector
        def _(dve):
            due_reg[dve.engine] = dve.alloc_register("due_count")
            ones_start(dve, (s_oh, s_sc, s_lk, s_eg, s_msg), GA)
            ones_start(dve, (s_add,), IA)
            ones_start(dve, (f_hr, e_y), AHEAD)
            ones_start(dve, (m_qm, m_q, m_tz, m_r, n_g, n_c, n_y), MA)
            ones_start(dve, (m_z,), 2 * MA)

            def tile(t):
                return xall[:, ds(t, 1), :].rearrange("p a c -> p (a c)")

            def stats(t, signal):
                dve.bn_stats(stat[:, ds(t, 1), :].rearrange("p a c -> p (a c)"), tile(t)).then_inc(signal, 1)

            def finish_stats(n):
                k = 6 * (n - 1)
                mean_e, dev_e, mean_o, dev_o = (stat[:, :, c] for c in (1, 2, 4, 5))
                dve.tensor_tensor(st_s[:, 0, :], mean_e, mean_o, op=ALU.add).then_inc(s_ns, 1)
                dve.tensor_tensor(st_s[:, 1, :], mean_e, mean_o, op=ALU.subtract).then_inc(s_ns, 1)
                dve.tensor_tensor(st_s[:, 3, :], dev_e, dev_o, op=ALU.add).then_inc(s_ns, 1)
                dve.wait_ge(s_ns, k + 2)
                dve.tensor_tensor(st_s[:, 2, :], st_s[:, 1, :], st_s[:, 1, :], op=ALU.mult).then_inc(s_ns, 1)
                dve.wait_ge(s_ns, k + 4)
                dve.tensor_scalar(st_s[:, 1, :], st_s[:, 2, :], 0.25, EPS, op0=ALU.mult, op1=ALU.add
                                  ).then_inc(s_ns, 1)
                dve.wait_ge(s_ns, k + 5)
                dve.scalar_tensor_tensor(st_s[:, 2, :], st_s[:, 3, :], 1.0 / C, st_s[:, 1, :],
                                         op0=ALU.mult, op1=ALU.add).then_inc(s_vare, 1)
                dve.wait_ge(s_std, n)
                dve.reciprocal(rstd[:, :], std[:, :]).then_inc(s_ns, 1)
                dve.wait_ge(s_ns, k + 6)
                dve.scalar_tensor_tensor(nmr[:, :], st_s[:, 0, :], -0.5, rstd[:, :],
                                         op0=ALU.mult, op1=ALU.mult).then_inc(s_rstd, 1)

            per = NT // 5
            for g in range(5):
                dve.wait_ge(s_x[g], 16)
                with dve.Fori(g * per, (g + 1) * per) as t:
                    stats(t, s_stat)
            dve.wait_ge(s_stat, NT)
            finish_stats(1)

            dve.wait_ge(s_fold, 1)
            dve.tensor_copy(w_gat[:, :, C:HCOL].rearrange("p c (k h) -> p c h k", k=2),
                            pb[7][:, 0:16].rearrange("p (c h k) -> p c h k", c=CC, k=2)).then_inc(s_foldc, 1)
            dve.wait_ge(s_fold, 2)
            dve.tensor_tensor(b1eff[:, :], pb[7][:, 64:66], b1col[:, :], op=ALU.add)
            for c in range(CC):
                dve.tensor_scalar(w1g[:, c, :], w1g[:, c, :], g1col[:, c:c + 1], None, op0=ALU.mult)
            dve.tensor_tensor(c1rep[:, :], c1rep[:, :], b2rep[:, :], op=ALU.add)
            dve.tensor_scalar(c2rep[:, :], c2rep[:, :], -1.0, None, op0=ALU.add).then_inc(s_prep, 1)

            dve.wait_ge(s_keys, 32)
            dve.wait_ge(s_const, 1)
            ka, kb = key_a.bitcast(I32), key_b.bitcast(I32)
            for b in range(7):
                dve.tensor_scalar(bit_i[:, b:b + 1], part_i[:, b:b + 1], b, 1,
                                  op0=ALU.logical_shift_right, op1=ALU.bitwise_and)
            dve.tensor_scalar(ka, ka, FIELD, KEY_ONE, op0=ALU.logical_shift_left, op1=ALU.bitwise_or
                              ).then_inc(s_key, 1)
            dve.wait_ge(s_key, 1)
            dve.tensor_scalar(sign[:, 0:7], bit_i[:, 0:7], -2.0, 1.0, op0=ALU.mult, op1=ALU.add)
            dve.tensor_tensor(ka, ka, kb, op=ALU.bitwise_or).then_inc(s_key, 1)
            dve.wait_ge(s_key, 2)

            count = [0, 0]
            cur, last_bit = 0, None

            def halves(buf, j, sbit, v):
                hi, lo = max(j, sbit), min(j, sbit)
                view = buf.rearrange("p (a f b g d) -> p a f b g d", f=2, b=1 << (hi - lo - 1), g=2, d=1 << lo)
                if j > sbit:
                    return view[:, :, 0, :, v, :], view[:, :, 1, :, v, :]
                return view[:, :, v, :, 0, :], view[:, :, v, :, 1, :]

            def stage(j, sbit, falling):
                nonlocal cur, last_bit
                before = list(count)
                for v in range(2):
                    for w in (range(2) if sbit != last_bit else [v]):
                        if before[w]:
                            dve.wait_ge(s_st[w], before[w])
                    lo, hi = halves(keys[cur], j, sbit, v)
                    to_lo, to_hi = halves(keys[1 - cur], j, sbit, v)
                    down = falling and v == 1
                    dve.tensor_tensor(to_lo, lo, hi, op=ALU.max if down else ALU.min).then_inc(s_st[v], 1)
                    dve.tensor_tensor(to_hi, lo, hi, op=ALU.min if down else ALU.max).then_inc(s_st[v], 1)
                    count[v] += 2
                cur, last_bit = 1 - cur, sbit

            def both_done():
                nonlocal last_bit
                dve.wait_ge(s_st[0], count[0])
                dve.wait_ge(s_st[1], count[1])
                last_bit = None

            def lane_stages():
                for j in range(6, -1, -1):
                    stage(j, LOG_SC - 1, False)

            signed = [0]
            def sign_all(level, signal, n):
                both_done()
                dve.tensor_scalar(keys[cur], keys[cur], sign[:, level - LOG_SC:level - LOG_SC + 1], None,
                                  op0=ALU.mult).then_inc(signal, 1)
                dve.wait_ge(signal, n)

            def turn(n, level):
                nonlocal cur
                cur = 1 - cur
                dve.wait_ge(s_tp, 2 * n + 2)
                half = keys[cur][:, SC // 2:SC]
                if n % 2 and level < LOG_SLOTS:
                    dve.tensor_scalar(half, sortp[1][:, :], sign[:, level - LOG_SC:level - LOG_SC + 1], None,
                                      op0=ALU.mult).then_inc(s_te[1], 1)
                else:
                    dve.tensor_copy(half, sortp[1][:, :]).then_inc(s_te[1], 1)
                dve.wait_ge(s_te[0], n + 1)
                dve.wait_ge(s_te[1], n + 1)

            for level in range(1, LOG_SC):
                for j in range(level - 1, -1, -1):
                    stage(j, level, True)
            sign_all(LOG_SC, s_key, 3)
            stage(9, 8, False)
            for j in range(8, -1, -1):
                stage(j, LOG_SC - 1, False)
            sign_all(LOG_SC, s_sg, 1)
            n = 0
            for level in range(LOG_SC + 1, LOG_SLOTS + 1):
                turn(n, level)
                n += 1
                if level < LOG_SLOTS:
                    for bit in range(level - 1, 6, -1):
                        stage(bit - LOG_SC if bit >= LOG_SC else bit, level - LOG_SC, True)
                else:
                    for j in range(6, -1, -1):
                        stage(j, 9, False)
                    stage(9, 8, False)
                    stage(8, 9, False)
                    stage(7, 9, False)
                both_done()
                dve.sem_inc(s_sg, 1)
                turn(n, level)
                n += 1
                lane_stages()
                if level < LOG_SLOTS:
                    sign_all(level, s_sg, n + 1)
            both_done()

            sk = sorted_keys.bitcast(I32)
            SCALES = [(20, 63, 128.0), (13, 127, 1.0), (7, 63, 128.0), (0, 127, 1.0)]
            for f, (shift, mask, scale) in enumerate(SCALES):
                if f >= 2:
                    dve.wait_ge(s_dec, f - 1)
                    dve.wait_ge(s_tabs, f + 1)
                dve.tensor_scalar(fint[f % 2], sk, shift, mask, op0=ALU.logical_shift_right,
                                  op1=ALU.bitwise_and).then_inc(s_tabs, 1)
                dve.wait_ge(s_tabs, f + 1 + (f > 0))
                dve.tensor_scalar(field[f], fint[f % 2], scale, None, op0=ALU.mult).then_inc(s_dec, 1)
                if f == 0:
                    bins = fint[0].rearrange("p (b e) -> p b e", b=TPP)
                    dve.tensor_copy(small[:, 0, :], bins[:, :, 0])
                    dve.tensor_scalar(small[:, 1, :], bins[:, :, PAIR - 1], float(BINS - 1), None, op0=ALU.min
                                      ).then_inc(s_tabs, 1)
            dve.wait_ge(s_dec, 4)
            chain = [5]

            def step(ins):
                chain[0] += 1
                ins.then_inc(s_tabs, 1)
                dve.wait_ge(s_tabs, chain[0])

            step(dve.scalar_tensor_tensor(small[:, 2, :], small[:, 1, :], 1.0, small[:, 0, :],
                                          op0=ALU.add, op1=ALU.subtract))
            step(dve.tensor_scalar(small[:, 3, :], small[:, 2, :], 0.0, None, op0=ALU.max))
            step(dve.memset(small[:, 4, :], 0.0))
            step(dve.tensor_tensor_scan(small[:, 5, :], small[:, 3, :], small[:, 4, :], 0.0,
                                        op0=ALU.add, op1=ALU.add))
            dve.tensor_copy(small[:, 15, 0:1], small[:, 5, TPP - 1:TPP]).then_inc(s_cnt, 1)
            dve.wait_ge(s_cross, 1)
            step(dve.tensor_scalar(small[:, 6, :], small[:, 5, :], pb[0][:, 0:1], None, op0=ALU.add))
            step(dve.tensor_tensor(small[:, 7, :], small[:, 6, :], small[:, 3, :], op=ALU.subtract))
            step(dve.tensor_tensor(small[:, 8, :], small[:, 0, :], small[:, 7, :], op=ALU.subtract))
            step(dve.tensor_scalar(smalli[:, 0, :], small[:, 8, :], 0.125, None, op0=ALU.mult))
            step(dve.tensor_scalar(small[:, 9, :], smalli[:, 0, :], 8.0, None, op0=ALU.mult))
            step(dve.tensor_tensor(small[:, 10, :], small[:, 8, :], small[:, 9, :], op=ALU.subtract))
            dve.tensor_copy(rep[:, 0], small[:, 9, :, None].to_broadcast([P, TPP, P]))
            dve.tensor_copy(rep[:, 1], small[:, 10, :, None].to_broadcast([P, TPP, P]))
            for b in range(TPP):
                if b >= 2:
                    dve.wait_ge(s_self, b - 1)
                step(dve.tensor_scalar(selg[:, b % 2, :], iota_k[:, :], small[:, 7, b:b + 1], None, op0=ALU.is_ge))
                dve.scalar_tensor_tensor(sel[:, b, :], iota_k[:, :], small[:, 6, b:b + 1], selg[:, b % 2, :],
                                         op0=ALU.is_lt, op1=ALU.mult).then_inc(s_self, 1)

            dve.memset(dst_tab[:, 2 * ITEMS:], 0)
            dve.memset(srcrel[:, 2 * ITEMS:], -1.0)
            dve.memset(bin_acc[:, :], 0)
            step(dve.memset(bin_asrc[:, :], 0))
            dve.wait_ge(s_tab, 1)
            step(dve.tensor_tensor(binf, pb[5][:, 0:ITEMS], iota_k[:, :], op=ALU.add))
            for h in range(2):
                dve.scalar_tensor_tensor(srcrel[:, 0:2 * ITEMS].rearrange("p (k h) -> p k h", h=2)[:, :, h],
                                         binf, -float(P), pb[1 + h][:, 0:ITEMS], op0=ALU.mult, op1=ALU.add)
                dve.tensor_scalar(dst_tab[:, 0:2 * ITEMS].rearrange("p (k h) -> p k h", h=2)[:, :, h],
                                  pb[3 + h][:, 0:ITEMS], float(N_NODES - 1), None, op0=ALU.min)
            step(dve.tensor_scalar(binc, binf, float(BINS - 1), None, op0=ALU.min))
            dve.tensor_scalar(bin_acc[0:1, 4:4 + ITEMS], binc[0:1, :], float(HROW), None, op0=ALU.mult)
            dve.tensor_scalar(bin_asrc[0:1, 0:ITEMS], binc[0:1, :], float(HEADS), None, op0=ALU.mult
                              ).then_inc(s_items, 1)
            dve.wait_ge(s_items, 1)
            dve.wait_ge(s_hw[0], 16 * NPAIR)
            dve.wait_ge(s_hw[1], 16 * NPAIR)
            dve.wait_ge(s_kvbd, 1)
            for g in range(4):
                dve.tensor_copy(idx_buf[:, 4 * g:4 * g + 4], dst_tab[:, 4 * g:4 * g + 4]).then_inc(s_idx, 1)
            dve.memset(acc, 0.0).then_inc(s_acc0, 1)
            dve.wait_ge(s_acc0, 1)

            def onehots(q, g):
                dve.wait_ge(s_agg, 2 * q - 8 + 2 + IA)
                dve.tensor_tensor(onehot[:, 4 * g:4 * g + 4, :],
                                  iota_p[:, None, :].to_broadcast([P, 4, P]),
                                  srcrel[:, ds(4 * q, 4)][:, :, None].to_broadcast([P, 4, P]),
                                  op=ALU.is_equal).then_inc(s_oh, 1)

            def add_item(k, bank, off):
                dve.wait_ge(s_agg, k + 1 + IA)
                dve.wait_ge(s_add, k + IA)
                mine = acc[:, ds(off, HROW)]
                dve.tensor_tensor(mine, psG[bank][:, 0:HROW], mine, op=ALU.add).then_inc(s_add, 1)

            def group_scores(q, g, b):
                slots = rows[:, 4 * g:4 * g + 4, :]
                dve.wait_ge(s_al, q + 1 + GA)
                dve.wait_ge(s_gat[g], 64 * b + 64)
                dve.wait_ge(s_lk, q - 2 + 1 + GA)
                dve.tensor_tensor(score[:, g % 2], score_ps[:, g % 2], slots[:, :, C:HROW], op=ALU.add
                                  ).then_inc(s_sc, 1)

            def group_leaky(q, g):
                dve.wait_ge(s_sc, q + 1 + GA)
                dve.wait_ge(s_ex, q - 2 + 1 + GA)
                dve.scalar_tensor_tensor(leaky[:, g % 2], score[:, g % 2], 0.2, score[:, g % 2],
                                         op0=ALU.mult, op1=ALU.max).then_inc(s_lk, 1)

            def group_guard(q, g):
                dve.wait_ge(s_ex, q + 1 + GA)
                dve.tensor_scalar(rows[:, 4 * g:4 * g + 4, C:HROW], expd[:, g % 2], 0.0, None, op0=ALU.max
                                  ).then_inc(s_eg, 1)

            def group_messages(q, g):
                slots = rows[:, 4 * g:4 * g + 4, :]
                h = slots[:, :, 0:C].rearrange("p s (k d) -> p s k d", k=HEADS)
                dve.wait_ge(s_eg, q + 1 + GA)
                dve.tensor_tensor(h, h, slots[:, :, C:HROW][:, :, :, None].to_broadcast([P, 4, HEADS, HID]),
                                  op=ALU.mult).then_inc(s_msg, 1)

            def mix_q_kernel(i):
                dve.wait_ge(m_qe, i + 1 + MA)
                dve.wait_ge(m_q, i + MA)
                dve.tensor_scalar(em[:, :, :], ev[:, :, :], 1.0, None, op0=ALU.min).then_inc(m_qm, 1)
                dve.wait_ge(m_qm, i + 1 + MA)
                dve.wait_ge(m_tps, i + MA)
                dve.scalar_tensor_tensor(qs.rearrange("p c n -> p (c n)"), pb[5][:, :], 0.0,
                                         em.rearrange("p j c -> p (j c)"), op0=ALU.max, op1=ALU.add
                                         ).then_inc(m_q, 1)

            def mix_q_divide(i):
                dve.wait_ge(m_tps, i + 1 + MA)
                dve.wait_ge(m_z, 2 * (i + MA))
                dve.tensor_scalar(zden, psA[:, 32:32 + 2 * MH], EPS_ATTN, None, op0=ALU.add).then_inc(m_z, 1)
                dve.wait_ge(m_z, 2 * (i + MA) + 1)
                dve.wait_ge(m_tz, i + MA)
                dve.reciprocal(zrec, zden).then_inc(m_z, 1)
                dve.wait_ge(m_z, 2 * (i + MA) + 2)
                dve.wait_ge(m_r, i + MA)
                dve.tensor_tensor(tz.rearrange("p (z d) -> p z d", d=MD),
                                  pb[4][:, :].rearrange("p (z d) -> p z d", d=MD),
                                  zrec[:, :, None].to_broadcast([P, 2 * MH, MD]), op=ALU.mult).then_inc(m_tz, 1)

            def mix_q_residual(i):
                dve.wait_ge(m_xi, 2 * (i + 1 + MA))
                dve.wait_ge(m_tz, i + 1 + MA)
                pair = xall[:, ds(2 * i, 2), :]
                dve.tensor_tensor(pair, two(tz), pair, op=ALU.add).then_inc(m_r, 1)
                dve.wait_ge(m_r, i + 1 + MA)
                for u in range(2):
                    stats(2 * i + u, m_bs)

            def mix_q(i, g, before):
                if g == 0 and before >= 1:
                    mix_q_kernel(i - 1)
                if g == 1 and before >= 2:
                    mix_q_residual(i - 2)

            def mix_mlp_gain(i):
                dve.wait_ge(n_xn, 2 * (i + 1 + MA))
                dve.wait_ge(n_c, i + MA)
                dve.tensor_tensor(ev[:, :, :], xs[:, :, :], g1rep[:, None, :].to_broadcast([P, 2, C]),
                                  op=ALU.mult).then_inc(n_g, 1)

            def mix_mlp_shift(i):
                dve.wait_ge(n_g, i + 1 + MA)
                dve.wait_ge(n_y, i + MA)
                dve.tensor_tensor(em[:, :, :], ev[:, :, :], c1rep[:, None, :].to_broadcast([P, 2, C]),
                                  op=ALU.add).then_inc(n_c, 1)

            def mix_mlp_residual(i):
                dve.wait_ge(n_yp, i + 1 + MA)
                dve.wait_ge(n_c, i + 1 + MA)
                dve.tensor_tensor(xall[:, ds(2 * i, 2), :], mixY[:, :, :], em[:, :, :], op=ALU.add
                                  ).then_inc(n_y, 1)

            def mix_mlp_stats(i):
                dve.wait_ge(n_y, i + 1 + MA)
                for u in range(2):
                    stats(2 * i + u, n_bs)

            def mix_mlp(i, g, before):
                if g == 0 and before >= 2:
                    mix_mlp_stats(i - 2)
                if g == 1 and before >= 1:
                    mix_mlp_shift(i - 1)
                if g == 2:
                    mix_mlp_gain(i)

            acc_regs = [dve.alloc_register(f"acc_bin{n}") for n in range(PER_BATCH)]

            def edge_batch(b, mix, i, first=False, last=False, pairs_before=2):
                dve.load(acc_regs, bin_acc[0:1, ds(b * PER_BATCH, PER_BATCH)])
                offs = [dve.snap(r, min_val=0, max_val=(BINS - 1) * HROW) for r in acc_regs]
                for g in range(4):
                    q = 4 * b + g
                    if mix and g == 0 and pairs_before >= 2:
                        (mix_q_divide if mix is mix_q else mix_mlp_residual)(i - 2)
                    group_scores(q, g, b)
                    if not last:
                        dve.wait_ge(s_const, 1)
                        dve.tensor_copy(idx_buf[:, 4 * g:4 * g + 4], dst_tab[:, ds(4 * q + 16, 4)]
                                        ).then_inc(s_idx, 1)
                    if not (first and g == 0):
                        group_guard(q - 1, (g - 1) % 4)
                    group_leaky(q, g)
                    if not (first and g == 0):
                        group_messages(q - 1, (g - 1) % 4)
                    bank = 2 * (g % 2)
                    if not (first and g < 2):
                        add_item(2 * q - 4, bank, offs[2 * g])
                    if not (last and g >= 2):
                        onehots(q + 2, (g + 2) % 4)
                    if not (first and g < 2):
                        add_item(2 * q - 3, bank + 1, offs[2 * g + 1])
                    if mix:
                        mix(i, g, pairs_before)

            def between(n):
                if n == 0:
                    mix_q_divide(NPAIR - 2)
                    mix_q_kernel(NPAIR - 1)
                    mix_q_residual(NPAIR - 2)
                    mix_q_divide(NPAIR - 1)
                    mix_q_residual(NPAIR - 1)
                    dve.wait_ge(m_bs, NT)
                    finish_stats(2)
                else:
                    mix_mlp_residual(NPAIR - 2)
                    mix_mlp_stats(NPAIR - 2)
                    mix_mlp_shift(NPAIR - 1)
                    mix_mlp_residual(NPAIR - 1)
                    mix_mlp_stats(NPAIR - 1)

            onehots(0, 0)
            onehots(1, 1)
            edge_batches(dve, edge_batch, mix_q, mix_mlp, between=between)
            group_guard(4 * NBATCH - 1, 3)
            group_messages(4 * NBATCH - 1, 3)
            dve.load(acc_regs[0:4], bin_acc[0:1, ITEMS:ITEMS + 4])
            for m in range(4):
                add_item(ITEMS - 4 + m, m, dve.snap(acc_regs[m], min_val=0, max_val=(BINS - 1) * HROW))
            dve.wait_ge(n_bs, NT)
            finish_stats(3)
            dve.wait_ge(s_add, ITEMS + IA)

            def x2_pair(i):
                sums = acc_t[:, ds(2 * i, 2), :]
                dve.tensor_scalar(rsum, sums[:, :, C:HROW], TINY, None, op0=ALU.max).then_inc(u_rs, 1)
                dve.wait_ge(u_rs, 2 * i + 1)
                dve.reciprocal(rrec, rsum.rearrange("p j c -> p (j c)")).then_inc(u_rs, 1)
                dve.wait_ge(u_rs, 2 * i + 2)
                dve.tensor_tensor(hpn.rearrange("p (j h d) -> p j h d", j=2, h=HEADS),
                                  sums[:, :, 0:C].rearrange("p j (h d) -> p j h d", h=HEADS),
                                  rrec.rearrange("p (j h) -> p j h", j=2)[:, :, :, None]
                                  .to_broadcast([P, 2, HEADS, HID]), op=ALU.mult).then_inc(u_hp, 1)
                dve.wait_ge(u_hp, i + 1)
                dve.wait_ge(u_e1, i)
                dve.tensor_scalar(gneg, hpn, 0.0, None, op0=ALU.min).then_inc(u_ng, 1)
                dve.wait_ge(u_e2, i + 1)
                dve.scalar_tensor_tensor(gout, hpn, 0.0, ge2, op0=ALU.max, op1=ALU.add).then_inc(u_g, 1)
                dve.wait_ge(u_g, i + 1)
                dve.wait_ge(u_p, 3 * i + 3)
                dve.tensor_tensor(xall[:, ds(2 * i, 2), :], two(gout), n2x, op=ALU.add).then_inc(u_x2, 1)
                dve.wait_ge(u_x2, i + 1)
                for u in range(2):
                    stats(2 * i + u, u_bs)
            with dve.Fori(0, NPAIR) as i:
                x2_pair(i)
            dve.wait_ge(u_bs, NT)
            finish_stats(4)

            dve.wait_ge(f_w, 16 * 5)
            dve.wait_ge(f_c, 1)
            def ff_copy(i):
                dve.wait_ge(f_tp, i + 1)
                dve.wait_ge(f_hp, FC * i)
                dve.tensor_copy(xT.rearrange("p c n -> p (c n)"), pb[0][:, :]).then_inc(f_xt, 1)

            def by_expert(v):
                return v[:, :, None].to_broadcast([P, 2, EXPERTS])

            def ff_pair(i, last_pair):
                k = NROUTE * i
                steps = [0]

                def step(ins):
                    steps[0] += 1
                    ins.then_inc(f_rt, 1)
                    dve.wait_ge(f_rt, k + steps[0])
                if not last_pair:
                    ff_copy(i + 1)
                dve.wait_ge(f_lp, i + 1)
                step(dve.tensor_tensor(lg, pb[5][:, 0:2 * EXPERTS].rearrange("p (u e) -> p u e", u=2),
                                       fbg_s[:, None, :].to_broadcast([P, 2, EXPERTS]), op=ALU.add))
                step(dve.tensor_reduce(lmax, lg, axis=AX_X, op=ALU.max))
                dve.wait_ge(f_le, i)
                step(dve.tensor_tensor(lsh, lg, by_expert(lmax), op=ALU.subtract))
                dve.wait_ge(f_le, i + 1)
                step(dve.tensor_reduce(lsum, lexp, axis=AX_X, op=ALU.add))
                dve.wait_ge(f_x2, 2 * i)
                step(dve.reciprocal(ptop, lsum))
                step(dve.tensor_reduce(letop, lexp, axis=AX_X, op=ALU.max))
                step(dve.tensor_tensor(leq, lexp, by_expert(letop), op=ALU.is_equal))
                step(dve.tensor_tensor(lix, leq, iota_e8[:, None, :].to_broadcast([P, 2, EXPERTS]), op=ALU.mult))
                step(dve.tensor_reduce(lidx, lix, axis=AX_X, op=ALU.min))
                step(dve.tensor_tensor(oh_e.rearrange("p e t -> p t e")[:, ds(2 * i, 2), :],
                                       iota_e8[:, None, :].to_broadcast([P, 2, EXPERTS]), by_expert(lidx),
                                       op=ALU.is_equal))
                assert steps[0] == NROUTE
                for n in range(4):
                    u, half = n // 2, n % 2
                    if half == 0:
                        dve.wait_ge(f_st[u], 16 * i)
                    dve.wait_ge(f_htp, 4 * i + n + 1)
                    dve.tensor_scalar(frow[:, u, half * 512:(half + 1) * 512], pb[6 + half][:, :],
                                      ptop[:, u:u + 1], None, op0=ALU.mult).then_inc(f_hr, 1)
            ff_copy(0)
            with dve.Fori(0, NPAIR - 1) as i:
                ff_pair(i, False)
            ff_pair(NPAIR - 1, True)

            tables = [0]

            def rstep(ins):
                tables[0] += 1
                ins.then_inc(r_st, 1)
                dve.wait_ge(r_st, tables[0])
            dve.wait_ge(f_hr, 4 * NPAIR + AHEAD)
            rstep(dve.memset(zeros_r, 0.0))
            dve.wait_ge(r_mm, 1)
            pre, tot = head(pb[1][:, 0:EXPERTS * NT]), head(pb[2][:, 0:EXPERTS * NT])
            for e in range(EXPERTS):
                ins = dve.tensor_tensor_scan(rk_base[:, e, :], tot[:, e, :], zeros_r[:, 0:NT], 0.0,
                                             op0=ALU.add, op1=ALU.add)
            rstep(ins)
            rstep(dve.tensor_tensor(rk_all, rk_base, tot, op=ALU.subtract))
            rstep(dve.tensor_tensor(rk_all, rk_all, pre, op=ALU.add))
            rstep(dve.tensor_scalar(rti[:, 0, :], rk_base[:, :, NT - 1], float(P - 1), None, op0=ALU.add))
            rstep(dve.tensor_scalar(rti[:, 1, :], rti[:, 0, :], 7, None, op0=ALU.logical_shift_right))
            rstep(dve.tensor_copy(rt[:, 0, :], rti[:, 1, :]))
            rstep(dve.tensor_tensor_scan(rt[:, 1, :], rt[:, 0, :], zeros_r[:, 0:EXPERTS], 0.0,
                                         op0=ALU.add, op1=ALU.add))
            rstep(dve.tensor_tensor(rt[:, 2, :], rt[:, 1, :], rt[:, 0, :], op=ALU.subtract))
            rstep(dve.tensor_scalar(rt[:, 3, :], rt[:, 2, :], float(P), None, op0=ALU.mult))
            rstep(dve.tensor_tensor(rk_all, rk_all, rt[:, 3, :][:, :, None].to_broadcast([P, EXPERTS, NT]),
                                    op=ALU.add))
            rstep(dve.tensor_tensor(rk_mul, rk_all, oh_e, op=ALU.mult))
            rstep(dve.tensor_reduce(posf, rk_mul.rearrange("p e t -> p t e"), axis=AX_X, op=ALU.add))
            rstep(dve.tensor_copy(posi[:, 0, :], posf))
            rstep(dve.tensor_scalar(posi[:, 1, :], posi[:, 0, :], P - 1, None, op0=ALU.bitwise_and))
            rstep(dve.tensor_scalar(posi[:, 2, :], posi[:, 0, :], 7, None, op0=ALU.logical_shift_right))
            rstep(dve.tensor_copy(lanef, posi[:, 1, :]))
            rstep(dve.tensor_copy(tilef, posi[:, 2, :]))
            rstep(dve.memset(sl_e, 0.0))
            for e in range(1, EXPERTS):
                rstep(dve.scalar_tensor_tensor(sl_e, iota_k[:, 0:NSLOT], rt[:, 2, e:e + 1], sl_e,
                                               op0=ALU.is_ge, op1=ALU.add))
            dve.tensor_scalar(slot_wd[0:1, 0:NSLOT], sl_e[0:1, :], float(FC * C), None, op0=ALU.mult)
            dve.tensor_scalar(slot_bd[0:1, 0:NSLOT], sl_e[0:1, :], float(C), None, op0=ALU.mult)
            def permute(i, u):
                t = 2 * i + u
                dve.wait_ge(r_acc, 2 * i)
                dve.tensor_scalar(lane_oh[:, u, :], iota_p[:, :], lanef[:, ds(t, 1)], None, op0=ALU.is_equal)
                dve.tensor_scalar(tile_oh[:, u, :], iota_k[:, 0:NSLOT], tilef[:, ds(t, 1)], tok1[:, ds(t, 1)],
                                  op0=ALU.is_equal, op1=ALU.mult).then_inc(r_oh, 1)
            with dve.Fori(0, NPAIR) as i:
                permute(i, 0)
                permute(i, 1)
            dve.wait_ge(r_acc, NT)
            perm = pb[3][:, 0:NSLOT]
            rstep(dve.tensor_scalar(permz, perm, 0.0, float(SKIP), op0=ALU.is_equal, op1=ALU.mult))
            rstep(dve.scalar_tensor_tensor(permz, perm, -1.0, permz, op0=ALU.add, op1=ALU.add))
            dve.wait_ge(f_st[0], 16 * NPAIR)
            dve.wait_ge(f_st[1], 16 * NPAIR)
            rstep(dve.tensor_copy(permi, permz))
            dve.memset(grow[:, :, :], 0.0).then_inc(r_done, 1)
            dve.wait_ge(r_done, 1)

            bd_regs = [dve.alloc_register(f"bd_slot{n}") for n in range(2)]

            def name_rows(s, u, i):
                held(dve, e_g[u], 16 * i)
                dve.tensor_copy(gidx[:, u:u + 1], permi[:, ds(s, 1)]).then_inc(e_ix, 1)

            def expert_out(s, u, i, off):
                held(dve, e_out[u], 16 * i)
                dve.tensor_copy(oidx[:, u:u + 1], permi[:, ds(s, 1)])
                dve.wait_ge(e_g[u], 16 * i + 16)
                dve.scalar_tensor_tensor(gx[:, u, :], bd_s[:, ds(off, C)], grow[:, u, FF + C:FF + C + 1],
                                         grow[:, u, FF:FF + C], op0=ALU.mult, op1=ALU.add).then_inc(e_b, 1)
                dve.wait_ge(e_b, s + 1)
                dve.wait_ge(e_yp, s + 1 + AHEAD)
                dve.tensor_tensor(yout[:, u, :], pb[4 + u][:, 0:C], gx[:, u, :], op=ALU.add).then_inc(e_y, 1)
                dve.wait_ge(e_y, s + 1 + AHEAD)

            def expert_pair(i, last_pair):
                dve.load(bd_regs, slot_bd[0:1, ds(2 * i, 2)])
                offs = [dve.snap(r, min_val=0, max_val=(EXPERTS - 1) * C) for r in bd_regs]
                name_rows(2 * i + 1, 1, i)
                expert_out(2 * i, 0, i, offs[0])
                if not last_pair:
                    name_rows(2 * i + 2, 0, i + 1)
                expert_out(2 * i + 1, 1, i, offs[1])
            name_rows(0, 0, 0)
            with dve.Fori(0, NSLOT // 2 - 1) as i:
                expert_pair(i, False)
            expert_pair(NSLOT // 2 - 1, True)


def kernel(x, src, dst, L0_gnn_W, L0_gnn_a, L0_mix_Wqkv, L0_mix_ln1_g, L0_mix_ln1_b, L0_mix_W1, L0_mix_b1,
           L0_mix_W2, L0_mix_b2, L0_mix_ln2_g, L0_mix_ln2_b, L0_ffn_W1, L0_ffn_b1, L0_ffn_Wg, L0_ffn_bg,
           L0_ffn_Wd, L0_ffn_bd):
    import numpy as np
    import concourse.bacc as bacc
    from concourse.bass_utils import run_bass_kernel_spmd

    def rows(a):
        return np.ascontiguousarray(np.broadcast_to(np.asarray(a).reshape(1, -1), (P, np.asarray(a).size)))

    def columns(a):
        return np.asarray(a).reshape(-1, P).T

    def slots(a):
        a = np.asarray(a)
        return np.concatenate([a, np.full(SLOTS - a.shape[0], NOBODY, a.dtype)])

    x = np.asarray(x)
    ga = np.asarray(L0_gnn_a).reshape(HEADS, 2, HID)[:, ::-1]
    laid = {
        "x": np.concatenate([x, np.zeros((ROWS - N_NODES, C), x.dtype)]),
        "src": slots(src),
        "dst": slots(dst),
        "gw": np.asarray(L0_gnn_W).transpose(1, 0, 2).reshape(C, C),
        "gwt": np.asarray(L0_gnn_W).transpose(2, 0, 1),
        "ga": ga.transpose(2, 0, 1),
        "wqkv_t": np.asarray(L0_mix_Wqkv).T,
        "ln1_g": columns(L0_mix_ln1_g), "ln1_b": columns(L0_mix_ln1_b),
        "w1_t": np.asarray(L0_mix_W1).T, "b1": columns(L0_mix_b1),
        "w2_t": np.asarray(L0_mix_W2).T, "b2": rows(L0_mix_b2),
        "ln2_g": rows(L0_mix_ln2_g), "ln2_b": rows(L0_mix_ln2_b),
        "ln1_g_rows": rows(L0_mix_ln1_g), "ln1_b_rows": rows(L0_mix_ln1_b),
        "fw1": L0_ffn_W1, "fb1": columns(L0_ffn_b1), "fwg": L0_ffn_Wg, "fbg": rows(L0_ffn_bg),
        "fwd": L0_ffn_Wd, "fbd": rows(L0_ffn_bd),
    }
    laid = {f"in_{k}": np.ascontiguousarray(v) for k, v in laid.items()}
    nc = bacc.Bacc("TRN2", target_bir_lowering=False, num_devices=1)
    aps = {k[3:]: nc.dram_tensor(k, a.shape, mybir.dt.from_np(a.dtype), kind="ExternalInput").ap()
           for k, a in laid.items()}
    out = nc.dram_tensor("out", [ROWS, C], F32, kind="ExternalOutput").ap()
    gps_layer(nc, out=out, **aps)
    r = run_bass_kernel_spmd(nc, [laid], core_ids=[0])
    return np.asarray(r.results[0]["out"])[0:N_NODES]
```

```python
from contextlib import ExitStack

import concourse.bass as bass
from concourse import mybir

P = 128
C = 256
CC = C // P
N_NODES = 6250
NT = 50
ROWS = NT * P
BINS = -(-N_NODES // P)
N_EDGES = 100000
LOG_SLOTS = 17
SLOTS = 1 << LOG_SLOTS
SC = SLOTS // P
LOG_SC = 10
PAIR = 2 * P
TPP = SC // PAIR
FIELD = 13
NOBODY = (1 << FIELD) - 1
KEY_ONE = 1 << 30
HEADS = 4
HID = C // HEADS
HROW = C + HEADS
HCOL = C + 2 * HEADS
PER_BATCH = 8
NBATCH = -(-(-(-N_EDGES // PAIR) + BINS - 1) // PER_BATCH)
ITEMS = NBATCH * PER_BATCH
NPAIR = NT // 2
MH = 8
MD = C // MH
FF = 1024
FC = FF // P
EXPERTS = 8
GROWS = 4
NSLOT = -(-((N_NODES + EXPERTS * (P - 1)) // P) // GROWS) * GROWS
FROW = FF + C
SKIP = 100000
EPS = 1e-5
EPS_ATTN = 1e-6
TINY = 1.1754944e-38

ALU = mybir.AluOpType
ACT = mybir.ActivationFunctionType
AX_X = mybir.AxisListType.X
F32 = mybir.dt.float32
BF16 = mybir.dt.bfloat16
I32 = mybir.dt.int32
ds = bass.ds


def gps_layer(nc, x, src, dst, gw, gwt, ga, wqkv_t, ln1_g, ln1_b, ln1_g_rows, ln1_b_rows, w1_t, b1, w2_t,
              b2, ln2_g, ln2_b, fw1, fb1, fwg, fbg, fwd, fbd, out):
    ctx = ExitStack()
    with ctx:
        def sb(name, shape, dt=F32):
            return ctx.enter_context(nc.sbuf_tensor(name, shape, dt))

        def sem(name):
            return ctx.enter_context(nc.semaphore(name))

        node_table = nc.dram_tensor("node_table", [ROWS, HROW], F32, kind="Internal").ap()
        expert_table = nc.dram_tensor("expert_table", [ROWS, FROW], F32, kind="Internal").ap()

        xall = sb("xall", [P, NT, C])
        asrc = sb("asrc", [P, NT * HEADS])
        w_gat = sb("w_gat", [P, CC, HCOL])
        w_kv = sb("w_kv", [P, CC, 2 * C])
        w_q = sb("w_q", [P, CC, C])
        w1g = sb("w1g", [P, CC, C])
        w2s = sb("w2s", [P, CC, C])
        wt_heads = sb("wt_heads", [HID, HEADS, C])
        a_heads = sb("a_heads", [HID, HEADS, 2])
        b1col = sb("b1col", [P, CC])
        b1eff = sb("b1eff", [P, CC])
        g1col = sb("g1col", [P, CC])
        be1col = sb("be1col", [P, CC])
        g1rep = sb("g1rep", [P, C])
        c1rep = sb("c1rep", [P, C])
        b2rep = sb("b2rep", [P, C])
        g2rep = sb("g2rep", [P, C])
        c2rep = sb("c2rep", [P, C])
        kvbd = sb("kvbd", [P, CC, P + HEADS])
        std = sb("std", [P, NT])
        rstd = sb("rstd", [P, NT])
        nmr = sb("nmr", [P, NT])
        ident = sb("ident", [P, P])
        upper = sb("upper", [P, P])
        ones = sb("ones", [P, P])
        iota_p = sb("iota_p", [P, P])
        iota_k = sb("iota_k", [P, ITEMS])
        valid = sb("valid", [P, NT + 1])
        minus1 = sb("minus1", [P, 1])
        pm1 = sb("pm1", [P, 2])
        part_i = sb("part_i", [P, 8], I32)
        bit_i = sb("bit_i", [P, 8], I32)
        sign = sb("sign", [P, 8])
        srcrel = sb("srcrel", [P, (ITEMS + PER_BATCH) * 2])
        dst_tab = sb("dst_tab", [P, (ITEMS + PER_BATCH) * 2], I32)
        bin_acc = sb("bin_acc", [1, ITEMS + PER_BATCH], I32)
        bin_asrc = sb("bin_asrc", [1, ITEMS + PER_BATCH], I32)
        xs = sb("xs", [P, 2, C])
        xT = sb("xT", [P, CC, 2 * P])
        ev = sb("ev", [P, 2, C])
        em = sb("em", [P, 2, C])
        qs = sb("qs", [P, CC, 2 * P])

        stat = sb("stat", [P, NT, 6])
        st_s = sb("st_s", [P, 4, NT])
        slot_wd = sb("slot_wd", [1, 64], I32)
        slot_bd = sb("slot_bd", [1, 64], I32)

        ACC = NT * HROW
        WD = EXPERTS * FC * C
        ARENA = 27300
        arena = sb("arena", [P, ARENA])

        class Carve:
            def __init__(self, at):
                self.at = at

            def take(self, n, dt=F32):
                view = arena[:, self.at:self.at + n]
                self.at += n
                assert self.at <= ARENA, self.at
                return view if dt is F32 else view.bitcast(dt)

        def two(view):
            return view.rearrange("p (j c) -> p j c", j=2)

        c0 = Carve(0)
        key_a = c0.take(SC)
        key_b = c0.take(SC)
        hbuf, hpos, hneg, hcl = (two(c0.take(2 * HCOL)) for _ in range(4))
        kexp, kpos, kcap, kbuf, vbuf = (two(c0.take(2 * C)) for _ in range(5))
        field = [c0.take(SC // 2, BF16) for _ in range(4)]
        fint = [c0.take(SC, I32) for _ in range(2)]
        sel = c0.take(TPP * ITEMS // 2, BF16).rearrange("p (b k) -> p b k", b=TPP)
        selg = two(c0.take(2 * ITEMS))
        rep = c0.take(TPP * P, BF16).rearrange("p (s b m) -> p s b m", s=2, b=TPP)
        small = c0.take(16 * TPP).rearrange("p (s b) -> p s b", b=TPP)
        smalli = c0.take(4 * TPP, I32).rearrange("p (s b) -> p s b", b=TPP)
        binf = c0.take(ITEMS)
        binc = c0.take(ITEMS)
        acc = arena[:, 0:ACC]
        acc_t = acc.rearrange("p (t c) -> p t c", c=HROW)
        c1 = Carve(ACC)
        rows = c1.take(16 * HROW).rearrange("p (s c) -> p s c", c=HROW)
        onehot = c1.take(16 * P).rearrange("p (s c) -> p s c", c=P)
        onehot_t = c1.take(8 * P).rearrange("p (q c) -> p q c", q=2)
        score, leaky, expd = (c1.take(8 * HEADS).rearrange("p (q s h) -> p q s h", q=2, h=HEADS)
                              for _ in range(3))
        idx_buf = c1.take(16, I32)
        zden = c1.take(2 * MH)
        zrec = c1.take(2 * MH)
        tz = c1.take(2 * C)
        hT = c1.take(2 * C).rearrange("p (c n) -> p c n", c=CC)
        c2 = Carve(ACC)
        xin = two(c2.take(2 * C))
        rsum = two(c2.take(2 * HEADS))
        rrec = c2.take(2 * HEADS)
        hpn, gneg, ge1, ge2, gout = (c2.take(2 * C) for _ in range(5))
        n2, n2g, n2b, n2x = (two(c2.take(2 * C)) for _ in range(4))
        st4 = two(c2.take(2 * 6))
        norm4 = c2.take(12 * 2).rearrange("p (s u) -> p s u", u=2)
        wd_s = arena[:, 0:WD]
        bd_s = arena[:, WD:WD + EXPERTS * C]
        c3 = Carve(max(c2.at, WD + EXPERTS * C))
        fb1_s = c3.take(FC)
        fbg_s = c3.take(EXPERTS)
        iota_e8 = c3.take(EXPERTS)
        ptop, lmax, lsum, lidx, tok1 = (c3.take(NT) for _ in range(5))
        oh_e = c3.take(EXPERTS * NT).rearrange("p (e t) -> p e t", e=EXPERTS)
        sl_e = c3.take(NSLOT)
        sl_p = c3.take(NSLOT)
        fhT = c3.take(FC * PAIR)
        fhT_p = fhT.rearrange("p (c n) -> p c n", c=FC)
        gT = fhT.rearrange("p (j c n) -> p j c n", j=2, c=FC)
        c4 = Carve(c3.at)
        fw1_s = c3.take(CC * FF).rearrange("p (c n) -> p c n", c=CC)
        fwg_s = c3.take(FC * EXPERTS).rearrange("p (c n) -> p c n", c=FC)
        frow = two(c3.take(2 * FF))
        lg, lex, lix = (c3.take(EXPERTS * NT).rearrange("p (e t) -> p e t", e=EXPERTS) for _ in range(3))
        grow = c4.take(GROWS * FROW).rearrange("p (u c) -> p u c", u=GROWS)
        yout = two(c4.take(2 * C))
        gidx = c4.take(GROWS, I32)
        oidx = c4.take(2, I32)
        permi = c4.take(NSLOT, I32)
        rk_base, rk_all, rk_mul = (v.rearrange("p (e t) -> p e t", e=EXPERTS)
                                   for v in (ev.rearrange("p j c -> p (j c)")[:, 0:EXPERTS * NT],
                                                   em.rearrange("p j c -> p (j c)")[:, 0:EXPERTS * NT],
                                                   qs.rearrange("p c n -> p (c n)")[:, 0:EXPERTS * NT]))
        xTf = xT.rearrange("p c n -> p (c n)")
        xsf = xs.rearrange("p j c -> p (j c)")
        lane_oh = two(xTf[:, 0:2 * P])
        tile_oh = xTf[:, 2 * P:2 * P + 4 * NSLOT].rearrange("p (u k n) -> p u k n", u=2, k=2)
        posf = xsf[:, 0:NT]
        posi = xsf[:, 64:64 + 3 * NT].bitcast(I32).rearrange("p (s t) -> p s t", s=3)
        lanef = xsf[:, 220:220 + NT]
        tilef = xsf[:, 272:272 + NT]
        rt = xsf[:, 324:324 + 5 * EXPERTS].rearrange("p (s e) -> p s e", e=EXPERTS)
        rti = xsf[:, 364:364 + 2 * EXPERTS].bitcast(I32).rearrange("p (s e) -> p s e", e=EXPERTS)
        zeros_r = xsf[:, 384:384 + 2 * NSLOT]
        permz = ev.rearrange("p j c -> p (j c)")[:, EXPERTS * NT:EXPERTS * NT + NSLOT]

        pb = [ctx.enter_context(nc.psum_tensor(f"bank{n}", [P, 512], F32)) for n in range(8)]

        s_x = [sem(f"x_loaded{g}") for g in range(5)]
        s_keys = sem("keys_loaded")
        s_wgt = sem("weights_loaded")
        s_const = sem("constants_ready")
        s_cstep = sem("constant_step")
        s_stat = sem("row_stats")
        s_vare = sem("variance_plus_eps")
        s_std = sem("row_std")
        s_rstd = sem("row_rstd")
        s_norm = sem("row_norm_ready")
        s_fold = sem("folded_weight_in_psum")
        s_foldc = sem("folded_weight_ready")
        s_prep = sem("prepared_vectors")
        s_xn = sem("xn_ready")
        s_xtp = sem("xnT_in_psum")
        s_xt = sem("xnT_ready")
        s_hp = sem("h_in_psum")
        s_kvp = sem("kv_in_psum")
        s_hc = sem("h_copied")
        s_kc = sem("kv_copied")
        s_hs = sem("h_signs")
        s_hcl = sem("h_clean")
        s_as = sem("asrc_saved")
        s_km = sem("k_exp_capped")
        s_kk = sem("k_ready")
        s_gram = sem("gram_added")
        s_hw = [sem(f"h_row_stored{j}") for j in range(2)]
        s_kvbd0 = sem("kvbd_cleared")
        s_kvbd = sem("kvbd_ready")
        s_key = sem("key_built")
        s_st = [sem("sort_stream_a"), sem("sort_stream_b")]
        s_tp = sem("sort_transposed")
        s_te = [sem("sort_half_a_copied"), sem("sort_half_b_copied")]
        s_ns = sem("norm_step")
        s_sg = sem("sort_signed")
        s_dec = sem("decoded")
        s_cnt = sem("tile_counts")
        s_cross = sem("tile_prefix_in_psum")
        s_self = sem("selectors_ready")
        s_tab = sem("item_tables_in_psum")
        s_tabs = sem("item_table_steps")
        s_items = sem("item_tables_ready")
        s_acc0 = sem("acc_cleared")
        s_idx = sem("gather_rows_named")
        s_gat = [sem(f"rows_gathered{g}") for g in range(4)]
        s_oh = sem("onehot_ready")
        s_otp = sem("onehotT_in_psum")
        s_ot = sem("onehotT_ready")
        s_al = sem("src_score_in_psum")
        s_sc = sem("score_ready")
        s_lk = sem("leaky_ready")
        s_ex = sem("exp_ready")
        s_eg = sem("exp_guarded")
        s_msg = sem("messages_ready")
        s_agg = sem("aggregated")
        s_add = sem("added")
        m_xn = sem("m_xn")
        m_xi = sem("m_xn_in_place")
        m_tp = sem("m_xT_in_psum")
        m_xt = sem("m_xT_ready")
        m_qp = sem("m_q_in_psum")
        m_qe = sem("m_q_exp")
        m_qm = sem("m_q_capped")
        m_q = sem("m_q_ready")
        m_tps = sem("m_t_in_psum")
        m_z = sem("m_z_steps")
        m_tz = sem("m_tz_ready")
        m_r = sem("m_r_ready")
        m_bs = sem("m_r_stats")
        m_mv = sem("m_r_mean_var")
        n_xn = sem("n_ready")
        n_tp = sem("n_T_in_psum")
        n_xt = sem("n_T_ready")
        n_hp = sem("n_h_in_psum")
        n_h = sem("n_h_ready")
        n_yp = sem("n_y_in_psum")
        n_g = sem("n_gained")
        n_c = sem("n_shifted")
        n_y = sem("n_y_ready")
        n_bs = sem("n_y_stats")
        n_mv = sem("n_y_mean_var")
        u_x = sem("u_x_loaded")
        u_n = sem("u_normed")
        u_rs = sem("u_rowsum_steps")
        u_hp = sem("u_hp_divided")
        u_ng = sem("u_negative_part")
        u_e1 = sem("u_exp_once")
        u_e2 = sem("u_exp_twice")
        u_g = sem("u_gat_ready")
        u_p = sem("u_mixer_steps")
        u_m = sem("u_mixer_plus_x")
        u_x2 = sem("u_x2_ready")
        u_bs = sem("u_x2_stats")
        u_c = sem("u_x2_norm_steps")
        f_w = sem("f_weights_loaded")
        f_wd = sem("f_wd_loaded")
        f_c = sem("f_consts")
        f_xn = sem("f_xn_ready")
        f_tp = sem("f_xT_in_psum")
        f_xt = sem("f_xT_ready")
        f_hp = sem("f_h_in_psum")
        f_h = sem("f_h_ready")
        f_lp = sem("f_logits_in_psum")
        f_lg = sem("f_logits_kept")
        f_rt = sem("f_route_step")
        f_le = sem("f_logit_exp")
        f_xs = sem("f_x2_stored")
        f_htp = sem("f_hrow_in_psum")
        f_hr = sem("f_hrow_ready")
        f_st = [sem(f"f_row_stored{j}") for j in range(2)]
        r_mm = sem("r_counts_in_psum")
        r_st = sem("r_step")
        r_oh = sem("r_onehots_ready")
        r_acc = sem("r_perm_added")
        r_done = sem("r_tables_ready")
        e_ix = sem("e_rows_named")
        e_clr = sem("e_rows_cleared")
        e_g = [sem(f"e_rows_gathered{j}") for j in range(GROWS)]
        e_tp = sem("e_rowT_in_psum")
        e_t = sem("e_rowT_ready")
        e_yp = sem("e_y_in_psum")
        e_b = sem("e_bias_added")
        e_y = sem("e_y_ready")
        e_out = [sem(f"e_out_stored{j}") for j in range(2)]

        block = ctx.enter_context(nc.Block())

        AHEAD, GA, IA, FA = 2, 4, 8, 4
        MA = 2
        XA = 2

        def head(view):
            return view.rearrange("p (e t) -> p e t", e=EXPERTS)

        SEGMENTS = [(0, NPAIR, 0), (NPAIR, 2, None), (NPAIR + 2, NPAIR, 1),
                    (2 * NPAIR + 2, NBATCH - 2 * NPAIR - 2, None)]

        def edge_batches(eng, batch, *mixer, between=None):
            for n, (at, count, kind) in enumerate(SEGMENTS):
                mix = None if kind is None else mixer[kind]
                start, end = at, at + count
                if mix:
                    batch(at, mix, 0, first=(at == 0), pairs_before=0)
                    batch(at + 1, mix, 1, pairs_before=1)
                    start += 2
                if end == NBATCH:
                    end -= 1
                with eng.Fori(start, end) as b:
                    batch(b, mix, b - at)
                if end == NBATCH - 1:
                    batch(end, None, 0, last=True)
                if between and mix:
                    between(n)

        keys = [key_a, key_b]
        turn_src, at = [], (sum(range(1, LOG_SC)) + LOG_SC) % 2
        for level in range(LOG_SC + 1, LOG_SLOTS + 1):
            for stages in (level - 7, 7):
                turn_src.append(keys[at])
                at = (at + 1 + stages) % 2
        TURNS = len(turn_src)
        sorted_keys = keys[at]
        NROUTE = 11
        NNORM = 9

        def chunked(w):
            return w.rearrange("(c p) n -> p c n", p=P)

        WEIGHTS = [
            (wt_heads[:, :, :], gwt), (a_heads[:, :, :], ga), (w_gat[:, :, 0:C], chunked(gw)),
            (w_kv[:, :, :], chunked(wqkv_t[:, C:3 * C])), (w_q[:, :, :], chunked(wqkv_t[:, 0:C])),
            (w1g[:, :, :], chunked(w1_t)), (w2s[:, :, :], chunked(w2_t)),
            (b1col[:, :], b1), (g1col[:, :], ln1_g), (be1col[:, :], ln1_b),
            (g1rep[:, :], ln1_g_rows), (c1rep[:, :], ln1_b_rows), (b2rep[:, :], b2),
            (g2rep[:, :], ln2_g), (c2rep[:, :], ln2_b),
        ]
        N_WEIGHTS = len(WEIGHTS)

        trp = [pb[0][:, 0:C], pb[0][:, C:2 * C]]
        hps = [pb[1][:, 0:HCOL], pb[2][:, 0:HCOL]]
        kvps = [pb[3], pb[4]]
        gram = pb[5][:, 0:CC * (P + 1)].rearrange("p (c m) -> p c m", c=CC)
        sortp = [pb[6], pb[7]]
        psT, psA = pb[0], pb[1]
        psG = [pb[2], pb[3], pb[6], pb[7]]
        score_ps = psA[:, 0:32].rearrange("p (q s h) -> p q s h", q=2, h=HEADS)
        den_ps = psA[:, 32:32 + 2 * MH].rearrange("p (u c h) -> p u c h", u=2, c=CC)
        mixT = pb[4][:, :].rearrange("p (c n) -> p c n", c=CC)
        mixQ = pb[5][:, :].rearrange("p (c n) -> p c n", c=CC)
        mixY = pb[4][:, :].rearrange("p (u n) -> p u n", u=2)

        due_reg = {}

        def held(eng, signal, value):
            due = due_reg[eng.engine]
            eng.reg_mov(due, value)
            eng.wait_ge(s_const, 1)
            eng.wait_ge(signal, due)

        def ones_start(eng, sems, n):
            for s in sems:
                eng.sem_inc(s, n)

        @block.sync
        def _(sp):
            due_reg[sp.engine] = sp.alloc_register("due_count")
            for g in range(5):
                t0 = g * (NT // 5)
                sp.dma_start(xall[:, t0:t0 + NT // 5, :],
                             x[t0 * P:(t0 + NT // 5) * P, :].rearrange("(t p) c -> p t c", p=P)
                             ).then_inc(s_x[g], 16)
                if g == 0:
                    sp.dma_start(key_a.bitcast(I32), src.rearrange("(p c) -> p c", p=P)).then_inc(s_keys, 16)
                    sp.dma_start(key_b.bitcast(I32), dst.rearrange("(p c) -> p c", p=P)).then_inc(s_keys, 16)
            def store(i, j):
                held(sp, s_hcl, 2 * i + j + 1 + AHEAD)
                sp.dma_start(node_table[ds((2 * i + j) * P, P), :], hcl[:, j, 0:HROW]).then_inc(s_hw[j], 16)
            with sp.Fori(0, NPAIR) as i:
                store(i, 0)
                store(i, 1)
            def reload(k):
                held(sp, u_p, 3 * (k + XA))
                sp.dma_start(xin, x[ds(2 * k * P, 2 * P), :].rearrange("(t p) c -> p t c", p=P)
                             ).then_inc(u_x, 16)
            def store_x2(k):
                held(sp, u_x2, k + 1 + XA)
                sp.dma_start(expert_table[ds(2 * k * P, 2 * P), FF:FROW].rearrange("(t p) c -> p t c", p=P),
                             xall[:, ds(2 * k, 2), :]).then_inc(f_xs, 16)
            def store_rows(i):
                for u in range(2):
                    held(sp, f_hr, 4 * i + 2 * u + 2 + AHEAD)
                    sp.dma_start(expert_table[ds((2 * i + u) * P, P), 0:FF], frow[:, u, :]).then_inc(f_st[u], 16)
            sp.wait_ge(s_add, ITEMS + IA)
            reload(0)
            sp.dma_start(fw1_s, fw1.rearrange("(c p) n -> p c n", p=P)).then_inc(f_w, 16)
            sp.dma_start(fwg_s, fwg.rearrange("(c p) n -> p c n", p=P)).then_inc(f_w, 16)
            sp.dma_start(fb1_s, fb1).then_inc(f_w, 16)
            sp.dma_start(fbg_s, fbg).then_inc(f_w, 16)
            reload(1)
            store_x2(0)
            with sp.Fori(0, NPAIR - 2) as i:
                reload(i + 2)
                store_x2(i + 1)
                store_rows(i)
            store_x2(NPAIR - 1)
            store_rows(NPAIR - 2)
            for e in range(EXPERTS):
                sp.dma_start(wd_s[:, e * FC * C:(e + 1) * FC * C].rearrange("p (c n) -> p c n", c=FC),
                             fwd[e].rearrange("(c p) n -> p c n", p=P)).then_inc(f_wd, 16)
            sp.dma_start(bd_s, fbd).then_inc(f_wd, 16)
            store_rows(NPAIR - 1)

        @block.gpsimd
        def _(pool):
            due_reg[pool.engine] = pool.alloc_register("due_count")
            ones_start(pool, (s_hs, s_hcl, s_as, s_km, s_kk), AHEAD)
            ones_start(pool, (u_p,), 3 * XA)
            ones_start(pool, (u_c,), NNORM * XA)
            ones_start(pool, (*f_st, *s_hw), 16)
            pool.memset(ident[:, :], 0.0).then_inc(s_cstep, 1)
            pool.memset(upper[:, :], 1.0).then_inc(s_cstep, 1)
            pool.memset(valid[:, :], 1.0).then_inc(s_cstep, 1)
            pool.memset(ones[:, :], 1.0)
            pool.memset(minus1[:, :], -1.0)
            pool.memset(ev[:, :, :], 0.0)
            pool.memset(em[:, :, :], 0.0)
            pool.memset(kbuf[:, 1, :], 0.0)
            pool.memset(vbuf[:, 1, :], 0.0)
            pool.memset(kvbd[:, :, :], 0.0)
            pool.iota(iota_p[:, :], [[1, P]], 0, 0, allow_small_or_imprecise_dtypes=True)
            pool.iota(iota_k[:, :], [[1, ITEMS]], 0, 0, allow_small_or_imprecise_dtypes=True)
            pool.iota(pm1[:, :], [[-2, 2]], 1, 0, allow_small_or_imprecise_dtypes=True)
            pool.iota(part_i[:, :], [[0, 8]], 0, 1)
            pool.wait_ge(s_cstep, 3)
            pool.affine_select(out=ident[:, :], in_=ident[:, :], compare_op=ALU.not_equal, fill=1.0,
                               base=0, pattern=[[-1, P]], channel_multiplier=1)
            pool.affine_select(out=upper[:, :], in_=upper[:, :], compare_op=ALU.is_gt, fill=0.0,
                               base=0, pattern=[[1, P]], channel_multiplier=-1)
            pool.affine_select(out=valid[:, :], in_=valid[:, :], compare_op=ALU.is_ge, fill=0.0,
                               base=N_NODES - 1 + P, pattern=[[-P, NT + 1]], channel_multiplier=-1
                               ).then_inc(s_const, 1)

            def guard(i, j):
                t = 2 * i + j
                done, two_ago = t + 1 + AHEAD, t + 1
                held(pool, s_hc, done)
                held(pool, s_hcl, two_ago)
                pool.tensor_scalar(hpos[:, j, :], hbuf[:, j, :], 0.0, None, op0=ALU.max)
                pool.tensor_scalar(hneg[:, j, :], hbuf[:, j, :], 0.0, None, op0=ALU.min).then_inc(s_hs, 1)
                held(pool, s_hs, done)
                held(pool, s_hw[j], 16 * (i + 1))
                held(pool, s_as, two_ago)
                pool.tensor_tensor(hcl[:, j, :], hpos[:, j, :], hneg[:, j, :], op=ALU.add).then_inc(s_hcl, 1)
                held(pool, s_kc, done)
                held(pool, s_kk, two_ago)
                pool.tensor_scalar(kcap[:, j, :], kexp[:, j, :], 1.0, None, op0=ALU.min).then_inc(s_km, 1)
                held(pool, s_hcl, done)
                pool.tensor_copy(asrc[:, ds(t * HEADS, HEADS)], hcl[:, j, HROW:HCOL]).then_inc(s_as, 1)
                held(pool, s_km, done)
                held(pool, s_gram, two_ago)
                pool.tensor_tensor(kbuf[:, j, :], kcap[:, j, :], kpos[:, j, :], op=ALU.add).then_inc(s_kk, 1)
            with pool.Fori(0, NPAIR) as i:
                guard(i, 0)
                guard(i, 1)

            pool.wait_ge(s_hw[0], 16 * NPAIR + 16)
            pool.wait_ge(s_hw[1], 16 * NPAIR + 16)
            def gather(b):
                for g in range(4):
                    q = 4 * b + g
                    held(pool, s_idx, q + 1)
                    held(pool, s_agg, 2 * q - 8 + IA + 2)
                    for s in range(4 * g, 4 * g + 4):
                        pool.indirect_dma_start(
                            out=rows[:, s, :], out_offset=None, in_=node_table[:, :],
                            in_offset=bass.IndirectOffsetOnAxis(ap=idx_buf[:, s:s + 1], axis=0)
                        ).then_inc(s_gat[g], 16)
            with pool.Fori(0, NBATCH) as b:
                gather(b)

            pool.wait_ge(s_add, ITEMS + IA)
            pool.iota(tok1, [[P, NT]], 1, 1, allow_small_or_imprecise_dtypes=True)
            pool.iota(iota_e8, [[1, EXPERTS]], -EXPERTS, 0, allow_small_or_imprecise_dtypes=True)
            pool.memset(norm4[:, 11, :], -0.5).then_inc(f_c, 1)
            pool.wait_ge(f_c, 1)

            def mixer_out(k):
                before = 3 * (k + XA)
                held(pool, u_n, 2 * (k + 1 + XA))
                held(pool, u_p, before)
                pool.tensor_tensor(n2g, n2, g2rep[:, None, :].to_broadcast([P, 2, C]), op=ALU.mult
                                   ).then_inc(u_p, 1)
                held(pool, u_p, before + 1)
                pool.tensor_tensor(n2b, n2g, c2rep[:, None, :].to_broadcast([P, 2, C]), op=ALU.add
                                   ).then_inc(u_p, 1)
                held(pool, u_p, before + 2)
                held(pool, u_x, 16 * (k + 1))
                held(pool, u_x2, k + XA)
                pool.tensor_tensor(n2x, n2b, xin, op=ALU.add).then_inc(u_p, 1)

            def x2_norm(k):
                before = NNORM * (k + XA)
                mean_e, dev_e, mean_o, dev_o = (st4[:, :, c] for c in (1, 2, 4, 5))
                v = lambda n: norm4[:, n, :]
                held(pool, u_bs, 2 * (k + 1 + XA))
                held(pool, f_xn, 2 * (k + XA))
                pool.tensor_tensor(v(0), mean_e, mean_o, op=ALU.add)
                pool.tensor_tensor(v(1), mean_e, mean_o, op=ALU.subtract)
                pool.tensor_tensor(v(2), dev_e, dev_o, op=ALU.add).then_inc(u_c, 1)
                held(pool, u_c, before + 1)
                pool.tensor_tensor(v(3), v(1), v(1), op=ALU.mult).then_inc(u_c, 1)
                pool.tensor_scalar(v(4), v(2), 1.0 / C, EPS, op0=ALU.mult, op1=ALU.add).then_inc(u_c, 1)
                held(pool, u_c, before + 3)
                pool.tensor_scalar(v(5), v(3), 0.25, None, op0=ALU.mult).then_inc(u_c, 1)
                held(pool, u_c, before + 4)
                pool.tensor_tensor(v(6), v(4), v(5), op=ALU.add).then_inc(u_c, 1)
                held(pool, u_c, before + 5)
                pool.tensor_tensor(v(7), v(6), v(11), op=ALU.pow).then_inc(u_c, 1)
                held(pool, u_c, before + 6)
                pool.tensor_tensor(v(8), v(0), v(7), op=ALU.mult).then_inc(u_c, 1)
                held(pool, u_c, before + 7)
                pool.tensor_tensor(v(9), v(8), v(11), op=ALU.mult).then_inc(u_c, 2)
                held(pool, u_c, before + 9)

            mixer_out(0)
            mixer_out(1)
            x2_norm(0)
            with pool.Fori(0, NPAIR - 2) as i:
                x2_norm(i + 1)
                mixer_out(i + 2)
            x2_norm(NPAIR - 1)

            pool.wait_ge(f_xs, 16 * NPAIR)
            pool.wait_ge(f_st[0], 16 * NPAIR + 16)
            pool.wait_ge(f_st[1], 16 * NPAIR + 16)
            def take(s, u):
                held(pool, e_ix, s + 1)
                pool.indirect_dma_start(
                    out=grow[:, u, :], out_offset=None, in_=expert_table[:, :],
                    in_offset=bass.IndirectOffsetOnAxis(ap=gidx[:, u:u + 1], axis=0),
                    bounds_check=ROWS - 1, oob_is_err=False).then_inc(e_g[u], 16)
            def give(s, v):
                held(pool, e_y, s + 1 + AHEAD)
                pool.indirect_dma_start(
                    out=out[:, :], out_offset=bass.IndirectOffsetOnAxis(ap=oidx[:, v:v + 1], axis=0),
                    in_=yout[:, v, :], in_offset=None,
                    bounds_check=ROWS - 1, oob_is_err=False).then_inc(e_out[v], 16)
            for u in range(GROWS - 1):
                take(u, u)
            def experts(i, last):
                for u in range(GROWS):
                    s = GROWS * i + u
                    if not (last and u):
                        take(s + GROWS - 1, (u + GROWS - 1) % GROWS)
                    give(s, u % 2)
            with pool.Fori(0, NSLOT // GROWS - 1) as i:
                experts(i, False)
            experts(NSLOT // GROWS - 1, True)
            pool.wait_ge(e_out[0], 16 * (NSLOT // 2))
            pool.wait_ge(e_out[1], 16 * (NSLOT // 2))

        @block.tensor
        def _(pe):
            ones_start(pe, (s_xtp, s_hp, s_kvp), AHEAD)
            ones_start(pe, (s_otp, s_al), GA)
            ones_start(pe, (s_agg,), IA)
            ones_start(pe, (e_yp,), AHEAD)
            ones_start(pe, (f_tp, f_lp, r_acc), XA)
            ones_start(pe, (f_htp,), 4 * XA)
            ones_start(pe, (m_tp, m_qp, m_tps, n_tp, n_hp, n_yp), MA)
            pe.sem_inc(s_gram, 1)

            def transpose(psum, tile):
                return pe.transpose(psum, tile, ident[:, :])

            pe.wait_ge(s_const, 1)
            pe.wait_ge(s_wgt, 16 * N_WEIGHTS)
            for c in range(CC):
                for h in range(HEADS):
                    at = (c * HEADS + h) * 2
                    last = pe.matmul(pb[7][:, at:at + 2], lhsT=wt_heads[:, h, c * P:(c + 1) * P],
                                     rhs=a_heads[:, h, :], start=True, stop=True)
            last.then_inc(s_fold, 1)
            pe.wait_ge(s_foldc, 1)
            for oc in range(CC):
                for c in range(CC):
                    last = pe.matmul(pb[7][:, 64 + oc:65 + oc], lhsT=w1g[:, c, oc * P:(oc + 1) * P],
                                     rhs=be1col[:, c:c + 1], start=(c == 0), stop=(c == CC - 1))
            last.then_inc(s_fold, 1)

            def node_t(t, j):
                pe.wait_ge(s_xn, t + 1 + AHEAD)
                pe.wait_ge(s_xt, t + 1)
                for c in range(CC):
                    last = transpose(trp[j][:, c * P:(c + 1) * P], xs[:, j, c * P:(c + 1) * P])
                last.then_inc(s_xtp, 1)

            def node_mm(t, j):
                pe.wait_ge(s_xt, t + 1 + AHEAD)
                pe.wait_ge(s_hc, t + 1)
                for c in range(CC):
                    last = pe.matmul(hps[j], lhsT=xT[:, c, j * P:(j + 1) * P], rhs=w_gat[:, c, :],
                                     start=(c == 0), stop=(c == CC - 1))
                last.then_inc(s_hp, 1)
                pe.wait_ge(s_kc, t + 1)
                for c in range(CC):
                    last = pe.matmul(kvps[j][:, :], lhsT=xT[:, c, j * P:(j + 1) * P], rhs=w_kv[:, c, :],
                                     start=(c == 0), stop=(c == CC - 1))
                last.then_inc(s_kvp, 1)

            def node_gram(t, j):
                pe.wait_ge(s_kk, t + 1 + AHEAD)
                for c in range(CC):
                    pe.matmul(gram[:, c, 0:P], lhsT=kbuf[:, j, c * P:(c + 1) * P],
                              rhs=vbuf[:, j, c * P:(c + 1) * P], start=False, stop=False,
                              skip_group_check=True)
                    last = pe.matmul(gram[:, c, P:P + 1], lhsT=kbuf[:, j, c * P:(c + 1) * P],
                                     rhs=valid[:, ds(t + 1, 1)], start=False, stop=False,
                                     skip_group_check=True)
                last.then_inc(s_gram, 1)

            pe.matmul(pb[5][:, 0:CC * (P + 1)], lhsT=ones[:, :],
                      rhs=ev.rearrange("p j c -> p (j c)")[:, 0:CC * (P + 1)], start=True, stop=False,
                      skip_group_check=True)
            node_t(0, 0)
            def node_pair(i, last):
                node_t(2 * i + 1, 1)
                node_mm(2 * i, 0)
                node_gram(2 * i - 1, 1)
                if not last:
                    node_t(2 * i + 2, 0)
                node_mm(2 * i + 1, 1)
                node_gram(2 * i, 0)
            with pe.Fori(0, NPAIR - 1) as i:
                node_pair(i, False)
            node_pair(NPAIR - 1, True)
            node_gram(NT - 1, 1)

            for n in range(TURNS):
                pe.wait_ge(s_sg, n + 1)
                for half in range(2):
                    for k in range(4):
                        blk = 4 * half + k
                        last = transpose(sortp[half][:, k * P:(k + 1) * P],
                                         turn_src[n][:, blk * P:(blk + 1) * P])
                    last.then_inc(s_tp, 1)

            pe.wait_ge(s_cnt, 1)
            pe.matmul(pb[0][:, 0:1], lhsT=upper[:, :], rhs=small[:, 15, 0:1], start=True, stop=True
                      ).then_inc(s_cross, 1)
            pe.wait_ge(s_dec, 4)
            pe.wait_ge(s_self, TPP)
            for f in range(2):
                for h in range(2):
                    for n in range(2 * TPP):
                        b, part = n // 2, n % 2
                        blk = 2 * b + h
                        last = pe.matmul(pb[1 + 2 * f + h][:, 0:ITEMS],
                                         lhsT=field[2 * f + part][:, blk * P:(blk + 1) * P],
                                         rhs=sel[:, b, :], start=(n == 0), stop=(n == 2 * TPP - 1))
            for n in range(2 * TPP):
                b, part = n // 2, n % 2
                last = pe.matmul(pb[5][:, 0:ITEMS], lhsT=rep[:, part, b, :], rhs=sel[:, b, :],
                                 start=(n == 0), stop=(n == 2 * TPP - 1))
            last.then_inc(s_tab, 1)

            def onehot_transpose(q, g):
                pe.wait_ge(s_oh, q + 1 + GA)
                pe.wait_ge(s_ot, q + GA)
                for n in range(4):
                    last = transpose(psT[:, n * P:(n + 1) * P], onehot[:, 4 * g + n, :])
                last.then_inc(s_otp, 1)

            def src_scores(q, g, bins):
                pe.wait_ge(s_ot, q + 1 + GA)
                pe.wait_ge(s_sc, q + GA)
                for n in range(4):
                    last = pe.matmul(score_ps[:, g % 2, n, :], lhsT=onehot_t[:, g % 2, n * P:(n + 1) * P],
                                     rhs=asrc[:, ds(bins[n // 2], HEADS)], start=True, stop=True,
                                     skip_group_check=True)
                last.then_inc(s_al, 1)

            def aggregate(q, g):
                pe.wait_ge(s_msg, q + 1 + GA)
                for m in range(2):
                    pe.wait_ge(s_add, 2 * q + m - 4 + 1 + IA)
                    for h in range(2):
                        s = 4 * g + 2 * m + h
                        last = pe.matmul(psG[2 * (g % 2) + m][:, 0:HROW], lhsT=onehot[:, s, :], rhs=rows[:, s, :],
                                         start=(h == 0), stop=(h == 1))
                    last.then_inc(s_agg, 1)

            def mix_turn(i, normed, free):
                pe.wait_ge(normed, 2 * (i + 1 + MA))
                pe.wait_ge(free, i - 1 + MA)
                for c in range(CC):
                    for u in range(2):
                        last = transpose(mixT[:, c, u * P:(u + 1) * P], xs[:, u, c * P:(c + 1) * P])
                return last

            def mix_columns(w, oc):
                for c in range(CC):
                    last = pe.matmul(mixQ[:, oc, :], lhsT=w[:, c, oc * P:(oc + 1) * P],
                                     rhs=xT[:, c, :], start=(c == 0), stop=(c == CC - 1))
                return last

            def mix_q_products(i):
                pe.wait_ge(m_q, i + 1 + MA)
                pe.wait_ge(m_tz, i + MA)
                for u in range(2):
                    for c in range(CC):
                        pe.matmul(mixY[:, u, c * P:(c + 1) * P], lhsT=qs[:, c, u * P:(u + 1) * P],
                                  rhs=kvbd[:, c, 0:P], start=True, stop=True)
                        last = pe.matmul(den_ps[:, u, c, :], lhsT=qs[:, c, u * P:(u + 1) * P],
                                         rhs=kvbd[:, c, P:P + HEADS], start=True, stop=True,
                                         skip_group_check=True)
                last.then_inc(m_tps, 1)

            def mix_q(i, g, before):
                if g == 0:
                    mix_turn(i, m_xn, m_tz).then_inc(m_tp, 1)
                if g == 1:
                    pe.wait_ge(m_xt, i + 1 + MA)
                    pe.wait_ge(m_q, i + MA)
                    mix_columns(w_q, 0)
                if g == 2:
                    mix_columns(w_q, 1).then_inc(m_qp, 1)
                if g == 3 and before >= 1:
                    mix_q_products(i - 1)

            def mix_mlp_products(i):
                pe.wait_ge(n_h, 2 * (i + 1 + MA))
                pe.wait_ge(n_y, i + MA)
                for u in range(2):
                    for oc in range(CC):
                        last = pe.matmul(mixY[:, u, :], lhsT=hT[:, oc, u * P:(u + 1) * P],
                                         rhs=w2s[:, oc, :], start=(oc == 0), stop=(oc == CC - 1))
                last.then_inc(n_yp, 1)

            def mix_mlp(i, g, before):
                if g == 0:
                    mix_turn(i, n_xn, n_y).then_inc(n_tp, 1)
                if g == 1:
                    pe.wait_ge(n_xt, i + 1 + MA)
                    pe.wait_ge(n_h, 2 * (i + MA))
                    mix_columns(w1g, 0)
                if g == 2:
                    mix_columns(w1g, 1).then_inc(n_hp, 1)
                if g == 3 and before >= 1:
                    mix_mlp_products(i - 1)

            def between(n):
                (mix_q_products if n == 0 else mix_mlp_products)(NPAIR - 1)

            asrc_regs = [pe.alloc_register(f"asrc_bin{n}") for n in range(PER_BATCH)]

            def edge_batch(b, mix, i, first=False, last=False, pairs_before=2):
                pe.load(asrc_regs, bin_asrc[0:1, ds(b * PER_BATCH + 2, PER_BATCH)])
                bins = [pe.snap(r, min_val=0, max_val=(BINS - 1) * HEADS) for r in asrc_regs]
                for g in range(4):
                    q = 4 * b + g
                    if not (last and g == 3):
                        src_scores(q + 1, (g + 1) % 4, bins[2 * g:2 * g + 2])
                    if not (first and g == 0):
                        aggregate(q - 1, (g - 1) % 4)
                    if not (last and g >= 2):
                        onehot_transpose(q + 2, (g + 2) % 4)
                    if mix:
                        mix(i, g, pairs_before)

            pe.wait_ge(s_items, 1)
            pe.wait_ge(s_as, NT + AHEAD)
            pe.wait_ge(s_kvbd, 1)
            onehot_transpose(0, 0)
            pe.load(asrc_regs[0:2], bin_asrc[0:1, 0:2])
            src_scores(0, 0, [pe.snap(r, min_val=0, max_val=(BINS - 1) * HEADS) for r in asrc_regs[0:2]])
            onehot_transpose(1, 1)
            edge_batches(pe, edge_batch, mix_q, mix_mlp, between=between)
            aggregate(4 * NBATCH - 1, 3)

            fT = pb[0][:, :].rearrange("p (c n) -> p c n", c=CC)
            lps = pb[5][:, 0:2 * EXPERTS].rearrange("p (u e) -> p u e", u=2)
            def ff_t(i):
                pe.wait_ge(f_xn, 2 * (i + 1 + XA))
                pe.wait_ge(f_xt, i + XA)
                for c in range(CC):
                    for u in range(2):
                        last = transpose(fT[:, c, u * P:(u + 1) * P], xs[:, u, c * P:(c + 1) * P])
                last.then_inc(f_tp, 1)
            def ff_pair(i, last_pair):
                pe.wait_ge(f_xt, i + 1 + XA)
                for oc in range(FC):
                    pe.wait_ge(f_h, FC * i + oc + 1)
                    for c in range(CC):
                        last = pe.matmul(pb[1 + oc % 4][:, 0:C],
                                         lhsT=fw1_s[:, c, oc * P:(oc + 1) * P], rhs=xT[:, c, :],
                                         start=(c == 0), stop=(c == CC - 1), skip_group_check=True)
                    last.then_inc(f_hp, 1)
                if not last_pair:
                    ff_t(i + 1)
                pe.wait_ge(f_h, FC * i + FC + FA)
                pe.wait_ge(f_lg, i + XA)
                for u in range(2):
                    for c in range(FC):
                        last = pe.matmul(lps[:, u, :], lhsT=fhT_p[:, c, u * P:(u + 1) * P],
                                         rhs=fwg_s[:, c, :], start=(c == 0), stop=(c == FC - 1))
                last.then_inc(f_lp, 1)
                for n in range(4):
                    u, half = n // 2, n % 2
                    pe.wait_ge(f_hr, 4 * i + n + 1)
                    for k in range(4):
                        last = transpose(pb[6 + half][:, k * P:(k + 1) * P],
                                         fhT_p[:, 4 * half + k, u * P:(u + 1) * P])
                    last.then_inc(f_htp, 1)
            pe.wait_ge(f_w, 16 * 4)
            ff_t(0)
            with pe.Fori(0, NPAIR - 1) as i:
                ff_pair(i, False)
            ff_pair(NPAIR - 1, True)

            pe.wait_ge(f_rt, NROUTE)
            ohf = oh_e.rearrange("p e t -> p (e t)")
            pe.matmul(pb[1][:, 0:EXPERTS * NT], lhsT=upper[:, :], rhs=ohf, start=True, stop=True)
            pe.matmul(pb[2][:, 0:EXPERTS * NT], lhsT=ones[:, :], rhs=ohf, start=True, stop=True
                      ).then_inc(r_mm, 1)
            perm = pb[3][:, 0:2 * NSLOT]
            pe.wait_ge(r_st, 1)
            pe.matmul(perm, lhsT=ones[:, :], rhs=zeros_r[:, 0:2 * NSLOT], start=True, stop=False,
                      skip_group_check=True)
            def permute(i, u):
                pe.wait_ge(r_oh, 2 * i + u + 1)
                pe.matmul(perm, lhsT=lane_oh[:, u, :], rhs=tile_oh[:, u].rearrange("p k n -> p (k n)"), start=False, stop=False,
                          skip_group_check=True).then_inc(r_acc, 1)
            pe.wait_ge(r_mm, 1)
            with pe.Fori(0, NPAIR) as i:
                permute(i, 0)
                permute(i, 1)

            wd_regs = [pe.alloc_register(f"wd_slot{n}") for n in range(GROWS)]
            def row_t(s, u, i):
                pe.wait_ge(e_g[u], 16 * i + 16)
                pe.wait_ge(e_t, 2 * s + 2)
                for half in range(2):
                    for k in range(4):
                        blk = 4 * half + k
                        last = transpose(pb[2 * (u % 2) + half][:, k * P:(k + 1) * P],
                                         grow[:, u, blk * P:(blk + 1) * P])
                    last.then_inc(e_tp, 1)
            def expert_mm(s, u, off):
                pe.wait_ge(e_t, 2 * s + 2 + 2 * AHEAD)
                pe.wait_ge(e_y, s + 1)
                for c in range(FC):
                    last = pe.matmul(pb[4 + u % 2][:, 0:C], lhsT=gT[:, u % 2, c, :],
                                     rhs=wd_s[:, ds(off + c * C, C)], start=(c == 0), stop=(c == FC - 1))
                last.then_inc(e_yp, 1)
            def expert_tiles(i, last):
                pe.load(wd_regs, slot_wd[0:1, ds(GROWS * i, GROWS)])
                offs = [pe.snap(r, min_val=0, max_val=(EXPERTS - 1) * FC * C) for r in wd_regs]
                for u in range(GROWS):
                    s = GROWS * i + u
                    if u < GROWS - 1:
                        row_t(s + 1, u + 1, i)
                    elif not last:
                        row_t(s + 1, 0, i + 1)
                    expert_mm(s, u, offs[u])
            pe.wait_ge(r_done, 1)
            pe.wait_ge(f_wd, 16 * (EXPERTS + 1))
            row_t(0, 0, 0)
            with pe.Fori(0, NSLOT // GROWS - 1) as i:
                expert_tiles(i, False)
            expert_tiles(NSLOT // GROWS - 1, True)

        @block.scalar
        def _(act):
            ones_start(act, (s_xn, s_xt, s_hc, s_kc), AHEAD)
            ones_start(act, (s_ot, s_ex), GA)
            ones_start(act, (f_h,), FA)
            ones_start(act, (e_t,), 2 * AHEAD)
            ones_start(act, (u_e1, u_e2), XA)
            ones_start(act, (u_n, f_xn), 2 * XA)
            ones_start(act, (m_xt, m_qe, n_xt), MA)
            ones_start(act, (m_xn, m_xi, n_xn, n_h), 2 * MA)
            due_reg[act.engine] = act.alloc_register("due_count")
            for dst_ap, src_ap in WEIGHTS:
                act.dma_start(dst_ap, src_ap).then_inc(s_wgt, 16)

            def root(n):
                act.wait_ge(s_vare, n)
                act.activation(std[:, :], st_s[:, 2, :], ACT.Sqrt).then_inc(s_std, 1)

            def normalise(dst_ap, t, signal):
                act.activation(dst_ap, tile(t), ACT.Identity, bias=nmr[:, ds(t, 1)],
                               scale=rstd[:, ds(t, 1)]).then_inc(signal, 1)

            def tile(t):
                return xall[:, ds(t, 1), :].rearrange("p a c -> p (a c)")

            root(1)
            act.wait_ge(s_rstd, 1)

            def node_norm(t, j):
                act.wait_ge(s_xtp, t + 1)
                normalise(xs[:, j, :], t, s_xn)

            def node_copies(t, j):
                done, two_ago = t + 1 + AHEAD, t + 1
                act.wait_ge(s_xtp, done)
                act.wait_ge(s_kvp, two_ago)
                act.activation(xT[:, :, j * P:(j + 1) * P], trp[j].rearrange("p (c n) -> p c n", c=CC),
                               ACT.Copy).then_inc(s_xt, 1)

            def node_out(t, j):
                done, two_ago = t + 1 + AHEAD, t + 1
                act.wait_ge(s_hp, done)
                act.wait_ge(s_hs, two_ago)
                act.activation(hbuf[:, j, :], hps[j], ACT.Copy).then_inc(s_hc, 1)
                act.wait_ge(s_kvp, done)
                act.wait_ge(s_kk, two_ago)
                act.activation(kexp[:, j, :], kvps[j][:, 0:C], ACT.Exp)
                act.activation(kpos[:, j, :], kvps[j][:, 0:C], ACT.Relu)
                act.wait_ge(s_gram, two_ago)
                act.activation(vbuf[:, j, :], kvps[j][:, C:2 * C], ACT.Copy).then_inc(s_kc, 1)

            node_norm(0, 0)
            node_copies(0, 0)
            def node_pair(i, last):
                node_norm(2 * i + 1, 1)
                node_copies(2 * i + 1, 1)
                node_out(2 * i, 0)
                if not last:
                    node_norm(2 * i + 2, 0)
                    node_copies(2 * i + 2, 0)
                node_out(2 * i + 1, 1)
            with act.Fori(0, NPAIR - 1) as i:
                node_pair(i, False)
            node_pair(NPAIR - 1, True)
            act.wait_ge(s_gram, NT + 2)
            act.wait_ge(s_const, 1)
            for c in range(CC):
                for h in range(P // MD):
                    rs = slice(h * MD, (h + 1) * MD)
                    act.activation(kvbd[rs, c, h * MD:(h + 1) * MD], gram[rs, c, h * MD:(h + 1) * MD], ACT.Copy)
                    last = act.activation(kvbd[rs, c, P + h:P + h + 1], gram[rs, c, P:P + 1], ACT.Copy)
            last.then_inc(s_kvbd, 1)

            for n in range(TURNS):
                level = LOG_SC + 1 + n // 2
                act.wait_ge(s_tp, 2 * n + 1)
                dst_ap = keys[1 - (0 if turn_src[n] is keys[0] else 1)][:, 0:SC // 2]
                if n % 2 and level < LOG_SLOTS:
                    act.activation(dst_ap, sortp[0][:, :], ACT.Copy,
                                   scale=sign[:, level - LOG_SC:level - LOG_SC + 1]).then_inc(s_te[0], 1)
                else:
                    act.activation(dst_ap, sortp[0][:, :], ACT.Copy).then_inc(s_te[0], 1)

            def copy_onehot(q, g):
                act.wait_ge(s_otp, q + 1 + GA)
                act.wait_ge(s_al, q - 2 + 1 + GA)
                act.activation(onehot_t[:, g % 2, :], psT[:, :], ACT.Copy).then_inc(s_ot, 1)

            def mix_q(i, g, before):
                if g == 0:
                    act.wait_ge(m_tp, i + MA)
                    for u in range(2):
                        normalise(xs[:, u, :], 2 * i + u, m_xn)
                    held(act, m_xn, 2 * (i + 1 + MA))
                    for u in range(2):
                        normalise(tile(2 * i + u), 2 * i + u, m_xi)
                if g == 1:
                    act.wait_ge(m_tp, i + 1 + MA)
                    act.activation(xT[:, :, :], mixT[:, :, :], ACT.Copy).then_inc(m_xt, 1)
                if g == 3:
                    act.wait_ge(m_qp, i + 1 + MA)
                    act.wait_ge(m_qm, i + MA)
                    act.activation(ev.rearrange("p j c -> p (j c)"), pb[5][:, :], ACT.Exp).then_inc(m_qe, 1)

            def mix_gelu(i):
                act.wait_ge(n_hp, i + 1 + MA)
                act.wait_ge(n_yp, i + MA)
                for oc in range(CC):
                    act.activation(hT[:, oc, :], mixQ[:, oc, :], ACT.Gelu,
                                   bias=b1eff[:, oc:oc + 1]).then_inc(n_h, 1)

            def mix_mlp(i, g, before):
                if g == 0:
                    act.wait_ge(n_g, i + MA)
                    for u in range(2):
                        normalise(xs[:, u, :], 2 * i + u, n_xn)
                    if before >= 1:
                        mix_gelu(i - 1)
                if g == 1:
                    act.wait_ge(n_tp, i + 1 + MA)
                    act.activation(xT[:, :, :], mixT[:, :, :], ACT.Copy).then_inc(n_xt, 1)

            def edge_batch(b, mix, i, first=False, last=False, pairs_before=2):
                for g in range(4):
                    q = 4 * b + g
                    act.wait_ge(s_lk, q + 1 + GA)
                    act.wait_ge(s_eg, q - 2 + 1 + GA)
                    act.activation(expd[:, g % 2], leaky[:, g % 2], ACT.Exp, scale=-1.0).then_inc(s_ex, 1)
                    if mix:
                        mix(i, g, pairs_before)
                    if not (last and g >= 2):
                        copy_onehot(q + 2, (g + 2) % 4)

            def between(n):
                if n == 0:
                    root(2)
                    act.wait_ge(s_rstd, 2)
                else:
                    mix_gelu(NPAIR - 1)

            copy_onehot(0, 0)
            copy_onehot(1, 1)
            edge_batches(act, edge_batch, mix_q, mix_mlp, between=between)

            root(3)
            act.wait_ge(s_rstd, 3)
            def mixer_norm(k):
                act.wait_ge(u_p, 3 * (k + XA) - 2)
                for u in range(2):
                    normalise(n2[:, u, :], 2 * k + u, u_n)

            def elu_exps(k):
                act.wait_ge(u_ng, k + 1 + XA)
                act.wait_ge(u_e2, k + XA)
                act.activation(ge1, gneg, ACT.Exp).then_inc(u_e1, 1)
                act.wait_ge(u_e1, k + 1 + XA)
                act.wait_ge(u_g, k + XA)
                act.activation(ge2, ge1, ACT.Exp, bias=minus1[:, :]).then_inc(u_e2, 1)

            def x2_normalise(k):
                held(act, f_tp, k + XA)
                held(act, u_c, NNORM * (k + 1 + XA))
                for u in range(2):
                    act.activation(xs[:, u, :], tile(2 * k + u), ACT.Identity, bias=norm4[:, 9, u:u + 1],
                                   scale=norm4[:, 7, u:u + 1]).then_inc(f_xn, 1)

            def ff_pair(i, last_pair, ahead=True):
                if ahead:
                    mixer_norm(i + 2)
                act.wait_ge(f_htp, 4 * (i + XA))
                for oc in range(FC):
                    if oc == 6 and not last_pair:
                        x2_normalise(i + 1)
                    act.wait_ge(f_hp, FC * i + oc + 1)
                    act.activation(fhT_p[:, oc, :], pb[1 + oc % 4][:, 0:C],
                                   ACT.Gelu, bias=fb1_s[:, oc:oc + 1]).then_inc(f_h, 1)
                if ahead:
                    elu_exps(i + 2)
            mixer_norm(0)
            elu_exps(0)
            mixer_norm(1)
            elu_exps(1)
            x2_normalise(0)
            act.wait_ge(f_w, 16 * 4)
            with act.Fori(0, NPAIR - 2) as i:
                ff_pair(i, False)
            ff_pair(NPAIR - 2, False, ahead=False)
            ff_pair(NPAIR - 1, True, ahead=False)
            act.wait_ge(f_rt, 2)
            act.activation(lex, lix, ACT.Exp).then_inc(f_le, 1)

            act.wait_ge(r_done, 1)
            def expert_copies(s, u):
                act.wait_ge(e_yp, s + 1)
                for half in range(2):
                    act.wait_ge(e_tp, 2 * s + half + 1)
                    act.activation(gT[:, u, 4 * half:4 * half + 4, :],
                                   pb[2 * u + half][:, :].rearrange("p (k n) -> p k n", k=4),
                                   ACT.Copy).then_inc(e_t, 1)
            with act.Fori(0, NSLOT // GROWS) as i:
                for u in range(GROWS):
                    expert_copies(GROWS * i + u, u % 2)

        @block.vector
        def _(dve):
            due_reg[dve.engine] = dve.alloc_register("due_count")
            ones_start(dve, (s_oh, s_sc, s_lk, s_eg, s_msg), GA)
            ones_start(dve, (s_add,), IA)
            ones_start(dve, (f_hr, e_y), AHEAD)
            ones_start(dve, (m_qm, m_q, m_tz, m_r, n_g, n_c, n_y), MA)
            ones_start(dve, (m_z,), 2 * MA)
            ones_start(dve, (u_hp, u_ng, u_g, u_x2, f_xt, f_lg), XA)
            ones_start(dve, (u_rs, u_bs), 2 * XA)

            def tile(t):
                return xall[:, ds(t, 1), :].rearrange("p a c -> p (a c)")

            def stats(t, signal):
                dve.bn_stats(stat[:, ds(t, 1), :].rearrange("p a c -> p (a c)"), tile(t)).then_inc(signal, 1)

            def finish_stats(n):
                k = 6 * (n - 1)
                mean_e, dev_e, mean_o, dev_o = (stat[:, :, c] for c in (1, 2, 4, 5))
                dve.tensor_tensor(st_s[:, 0, :], mean_e, mean_o, op=ALU.add).then_inc(s_ns, 1)
                dve.tensor_tensor(st_s[:, 1, :], mean_e, mean_o, op=ALU.subtract).then_inc(s_ns, 1)
                dve.tensor_tensor(st_s[:, 3, :], dev_e, dev_o, op=ALU.add).then_inc(s_ns, 1)
                dve.wait_ge(s_ns, k + 2)
                dve.tensor_tensor(st_s[:, 2, :], st_s[:, 1, :], st_s[:, 1, :], op=ALU.mult).then_inc(s_ns, 1)
                dve.wait_ge(s_ns, k + 4)
                dve.tensor_scalar(st_s[:, 1, :], st_s[:, 2, :], 0.25, EPS, op0=ALU.mult, op1=ALU.add
                                  ).then_inc(s_ns, 1)
                dve.wait_ge(s_ns, k + 5)
                dve.scalar_tensor_tensor(st_s[:, 2, :], st_s[:, 3, :], 1.0 / C, st_s[:, 1, :],
                                         op0=ALU.mult, op1=ALU.add).then_inc(s_vare, 1)
                dve.wait_ge(s_std, n)
                dve.reciprocal(rstd[:, :], std[:, :]).then_inc(s_ns, 1)
                dve.wait_ge(s_ns, k + 6)
                dve.scalar_tensor_tensor(nmr[:, :], st_s[:, 0, :], -0.5, rstd[:, :],
                                         op0=ALU.mult, op1=ALU.mult).then_inc(s_rstd, 1)

            per = NT // 5
            for g in range(5):
                dve.wait_ge(s_x[g], 16)
                with dve.Fori(g * per, (g + 1) * per) as t:
                    stats(t, s_stat)
            dve.wait_ge(s_stat, NT)
            finish_stats(1)

            dve.wait_ge(s_fold, 1)
            dve.tensor_copy(w_gat[:, :, C:HCOL].rearrange("p c (k h) -> p c h k", k=2),
                            pb[7][:, 0:16].rearrange("p (c h k) -> p c h k", c=CC, k=2)).then_inc(s_foldc, 1)
            dve.wait_ge(s_fold, 2)
            dve.tensor_tensor(b1eff[:, :], pb[7][:, 64:66], b1col[:, :], op=ALU.add)
            for c in range(CC):
                dve.tensor_scalar(w1g[:, c, :], w1g[:, c, :], g1col[:, c:c + 1], None, op0=ALU.mult)
            dve.tensor_tensor(c1rep[:, :], c1rep[:, :], b2rep[:, :], op=ALU.add)
            dve.tensor_scalar(c2rep[:, :], c2rep[:, :], -1.0, None, op0=ALU.add).then_inc(s_prep, 1)

            dve.wait_ge(s_keys, 32)
            dve.wait_ge(s_const, 1)
            ka, kb = key_a.bitcast(I32), key_b.bitcast(I32)
            for b in range(7):
                dve.tensor_scalar(bit_i[:, b:b + 1], part_i[:, b:b + 1], b, 1,
                                  op0=ALU.logical_shift_right, op1=ALU.bitwise_and)
            dve.tensor_scalar(ka, ka, FIELD, KEY_ONE, op0=ALU.logical_shift_left, op1=ALU.bitwise_or
                              ).then_inc(s_key, 1)
            dve.wait_ge(s_key, 1)
            dve.tensor_scalar(sign[:, 0:7], bit_i[:, 0:7], -2.0, 1.0, op0=ALU.mult, op1=ALU.add)
            dve.tensor_tensor(ka, ka, kb, op=ALU.bitwise_or).then_inc(s_key, 1)
            dve.wait_ge(s_key, 2)

            count = [0, 0]
            cur, last_bit = 0, None

            def halves(buf, j, sbit, v):
                hi, lo = max(j, sbit), min(j, sbit)
                view = buf.rearrange("p (a f b g d) -> p a f b g d", f=2, b=1 << (hi - lo - 1), g=2, d=1 << lo)
                if j > sbit:
                    return view[:, :, 0, :, v, :], view[:, :, 1, :, v, :]
                return view[:, :, v, :, 0, :], view[:, :, v, :, 1, :]

            def stage(j, sbit, falling):
                nonlocal cur, last_bit
                before = list(count)
                for v in range(2):
                    for w in (range(2) if sbit != last_bit else [v]):
                        if before[w]:
                            dve.wait_ge(s_st[w], before[w])
                    lo, hi = halves(keys[cur], j, sbit, v)
                    to_lo, to_hi = halves(keys[1 - cur], j, sbit, v)
                    down = falling and v == 1
                    dve.tensor_tensor(to_lo, lo, hi, op=ALU.max if down else ALU.min).then_inc(s_st[v], 1)
                    dve.tensor_tensor(to_hi, lo, hi, op=ALU.min if down else ALU.max).then_inc(s_st[v], 1)
                    count[v] += 2
                cur, last_bit = 1 - cur, sbit

            def both_done():
                nonlocal last_bit
                dve.wait_ge(s_st[0], count[0])
                dve.wait_ge(s_st[1], count[1])
                last_bit = None

            def lane_stages():
                for j in range(6, -1, -1):
                    stage(j, LOG_SC - 1, False)

            signed = [0]
            def sign_all(level, signal, n):
                both_done()
                dve.tensor_scalar(keys[cur], keys[cur], sign[:, level - LOG_SC:level - LOG_SC + 1], None,
                                  op0=ALU.mult).then_inc(signal, 1)
                dve.wait_ge(signal, n)

            def turn(n, level):
                nonlocal cur
                cur = 1 - cur
                dve.wait_ge(s_tp, 2 * n + 2)
                half = keys[cur][:, SC // 2:SC]
                if n % 2 and level < LOG_SLOTS:
                    dve.tensor_scalar(half, sortp[1][:, :], sign[:, level - LOG_SC:level - LOG_SC + 1], None,
                                      op0=ALU.mult).then_inc(s_te[1], 1)
                else:
                    dve.tensor_copy(half, sortp[1][:, :]).then_inc(s_te[1], 1)
                dve.wait_ge(s_te[0], n + 1)
                dve.wait_ge(s_te[1], n + 1)

            for level in range(1, LOG_SC):
                for j in range(level - 1, -1, -1):
                    stage(j, level, True)
            sign_all(LOG_SC, s_key, 3)
            stage(9, 8, False)
            for j in range(8, -1, -1):
                stage(j, LOG_SC - 1, False)
            sign_all(LOG_SC, s_sg, 1)
            n = 0
            for level in range(LOG_SC + 1, LOG_SLOTS + 1):
                turn(n, level)
                n += 1
                if level < LOG_SLOTS:
                    for bit in range(level - 1, 6, -1):
                        stage(bit - LOG_SC if bit >= LOG_SC else bit, level - LOG_SC, True)
                else:
                    for j in range(6, -1, -1):
                        stage(j, 9, False)
                    stage(9, 8, False)
                    stage(8, 9, False)
                    stage(7, 9, False)
                both_done()
                dve.sem_inc(s_sg, 1)
                turn(n, level)
                n += 1
                lane_stages()
                if level < LOG_SLOTS:
                    sign_all(level, s_sg, n + 1)
            both_done()

            sk = sorted_keys.bitcast(I32)
            SCALES = [(20, 63, 128.0), (13, 127, 1.0), (7, 63, 128.0), (0, 127, 1.0)]
            for f, (shift, mask, scale) in enumerate(SCALES):
                if f >= 2:
                    dve.wait_ge(s_dec, f - 1)
                    dve.wait_ge(s_tabs, f + 1)
                dve.tensor_scalar(fint[f % 2], sk, shift, mask, op0=ALU.logical_shift_right,
                                  op1=ALU.bitwise_and).then_inc(s_tabs, 1)
                dve.wait_ge(s_tabs, f + 1 + (f > 0))
                dve.tensor_scalar(field[f], fint[f % 2], scale, None, op0=ALU.mult).then_inc(s_dec, 1)
                if f == 0:
                    bins = fint[0].rearrange("p (b e) -> p b e", b=TPP)
                    dve.tensor_copy(small[:, 0, :], bins[:, :, 0])
                    dve.tensor_scalar(small[:, 1, :], bins[:, :, PAIR - 1], float(BINS - 1), None, op0=ALU.min
                                      ).then_inc(s_tabs, 1)
            dve.wait_ge(s_dec, 4)
            chain = [5]

            def step(ins):
                chain[0] += 1
                ins.then_inc(s_tabs, 1)
                dve.wait_ge(s_tabs, chain[0])

            step(dve.scalar_tensor_tensor(small[:, 2, :], small[:, 1, :], 1.0, small[:, 0, :],
                                          op0=ALU.add, op1=ALU.subtract))
            step(dve.tensor_scalar(small[:, 3, :], small[:, 2, :], 0.0, None, op0=ALU.max))
            step(dve.memset(small[:, 4, :], 0.0))
            step(dve.tensor_tensor_scan(small[:, 5, :], small[:, 3, :], small[:, 4, :], 0.0,
                                        op0=ALU.add, op1=ALU.add))
            dve.tensor_copy(small[:, 15, 0:1], small[:, 5, TPP - 1:TPP]).then_inc(s_cnt, 1)
            dve.wait_ge(s_cross, 1)
            step(dve.tensor_scalar(small[:, 6, :], small[:, 5, :], pb[0][:, 0:1], None, op0=ALU.add))
            step(dve.tensor_tensor(small[:, 7, :], small[:, 6, :], small[:, 3, :], op=ALU.subtract))
            step(dve.tensor_tensor(small[:, 8, :], small[:, 0, :], small[:, 7, :], op=ALU.subtract))
            step(dve.tensor_scalar(smalli[:, 0, :], small[:, 8, :], 0.125, None, op0=ALU.mult))
            step(dve.tensor_scalar(small[:, 9, :], smalli[:, 0, :], 8.0, None, op0=ALU.mult))
            step(dve.tensor_tensor(small[:, 10, :], small[:, 8, :], small[:, 9, :], op=ALU.subtract))
            dve.tensor_copy(rep[:, 0], small[:, 9, :, None].to_broadcast([P, TPP, P]))
            dve.tensor_copy(rep[:, 1], small[:, 10, :, None].to_broadcast([P, TPP, P]))
            for b in range(TPP):
                if b >= 2:
                    dve.wait_ge(s_self, b - 1)
                step(dve.tensor_scalar(selg[:, b % 2, :], iota_k[:, :], small[:, 7, b:b + 1], None, op0=ALU.is_ge))
                dve.scalar_tensor_tensor(sel[:, b, :], iota_k[:, :], small[:, 6, b:b + 1], selg[:, b % 2, :],
                                         op0=ALU.is_lt, op1=ALU.mult).then_inc(s_self, 1)

            dve.memset(dst_tab[:, 2 * ITEMS:], 0)
            dve.memset(srcrel[:, 2 * ITEMS:], -1.0)
            dve.memset(bin_acc[:, :], 0)
            step(dve.memset(bin_asrc[:, :], 0))
            dve.wait_ge(s_tab, 1)
            step(dve.tensor_tensor(binf, pb[5][:, 0:ITEMS], iota_k[:, :], op=ALU.add))
            for h in range(2):
                dve.scalar_tensor_tensor(srcrel[:, 0:2 * ITEMS].rearrange("p (k h) -> p k h", h=2)[:, :, h],
                                         binf, -float(P), pb[1 + h][:, 0:ITEMS], op0=ALU.mult, op1=ALU.add)
                dve.tensor_scalar(dst_tab[:, 0:2 * ITEMS].rearrange("p (k h) -> p k h", h=2)[:, :, h],
                                  pb[3 + h][:, 0:ITEMS], float(N_NODES - 1), None, op0=ALU.min)
            step(dve.tensor_scalar(binc, binf, float(BINS - 1), None, op0=ALU.min))
            dve.tensor_scalar(bin_acc[0:1, 4:4 + ITEMS], binc[0:1, :], float(HROW), None, op0=ALU.mult)
            dve.tensor_scalar(bin_asrc[0:1, 0:ITEMS], binc[0:1, :], float(HEADS), None, op0=ALU.mult
                              ).then_inc(s_items, 1)
            dve.wait_ge(s_items, 1)
            dve.wait_ge(s_hw[0], 16 * NPAIR + 16)
            dve.wait_ge(s_hw[1], 16 * NPAIR + 16)
            dve.wait_ge(s_kvbd, 1)
            for g in range(4):
                dve.tensor_copy(idx_buf[:, 4 * g:4 * g + 4], dst_tab[:, 4 * g:4 * g + 4]).then_inc(s_idx, 1)
            dve.memset(acc, 0.0).then_inc(s_acc0, 1)
            dve.wait_ge(s_acc0, 1)

            def onehots(q, g):
                dve.wait_ge(s_agg, 2 * q - 8 + 2 + IA)
                dve.tensor_tensor(onehot[:, 4 * g:4 * g + 4, :],
                                  iota_p[:, None, :].to_broadcast([P, 4, P]),
                                  srcrel[:, ds(4 * q, 4)][:, :, None].to_broadcast([P, 4, P]),
                                  op=ALU.is_equal).then_inc(s_oh, 1)

            def add_item(k, bank, off):
                dve.wait_ge(s_agg, k + 1 + IA)
                dve.wait_ge(s_add, k + IA)
                mine = acc[:, ds(off, HROW)]
                dve.tensor_tensor(mine, psG[bank][:, 0:HROW], mine, op=ALU.add).then_inc(s_add, 1)

            def group_scores(q, g, b):
                slots = rows[:, 4 * g:4 * g + 4, :]
                dve.wait_ge(s_al, q + 1 + GA)
                dve.wait_ge(s_gat[g], 64 * b + 64)
                dve.wait_ge(s_lk, q - 2 + 1 + GA)
                dve.tensor_tensor(score[:, g % 2], score_ps[:, g % 2], slots[:, :, C:HROW], op=ALU.add
                                  ).then_inc(s_sc, 1)

            def group_leaky(q, g):
                dve.wait_ge(s_sc, q + 1 + GA)
                dve.wait_ge(s_ex, q - 2 + 1 + GA)
                dve.scalar_tensor_tensor(leaky[:, g % 2], score[:, g % 2], 0.2, score[:, g % 2],
                                         op0=ALU.mult, op1=ALU.max).then_inc(s_lk, 1)

            def group_guard(q, g):
                dve.wait_ge(s_ex, q + 1 + GA)
                dve.tensor_scalar(rows[:, 4 * g:4 * g + 4, C:HROW], expd[:, g % 2], 0.0, None, op0=ALU.max
                                  ).then_inc(s_eg, 1)

            def group_messages(q, g):
                slots = rows[:, 4 * g:4 * g + 4, :]
                h = slots[:, :, 0:C].rearrange("p s (k d) -> p s k d", k=HEADS)
                dve.wait_ge(s_eg, q + 1 + GA)
                dve.tensor_tensor(h, h, slots[:, :, C:HROW][:, :, :, None].to_broadcast([P, 4, HEADS, HID]),
                                  op=ALU.mult).then_inc(s_msg, 1)

            def mix_q_kernel(i):
                dve.wait_ge(m_qe, i + 1 + MA)
                dve.wait_ge(m_q, i + MA)
                dve.tensor_scalar(em[:, :, :], ev[:, :, :], 1.0, None, op0=ALU.min).then_inc(m_qm, 1)
                dve.wait_ge(m_qm, i + 1 + MA)
                dve.wait_ge(m_tps, i + MA)
                dve.scalar_tensor_tensor(qs.rearrange("p c n -> p (c n)"), pb[5][:, :], 0.0,
                                         em.rearrange("p j c -> p (j c)"), op0=ALU.max, op1=ALU.add
                                         ).then_inc(m_q, 1)

            def mix_q_divide(i):
                dve.wait_ge(m_tps, i + 1 + MA)
                dve.wait_ge(m_z, 2 * (i + MA))
                dve.tensor_scalar(zden, psA[:, 32:32 + 2 * MH], EPS_ATTN, None, op0=ALU.add).then_inc(m_z, 1)
                dve.wait_ge(m_z, 2 * (i + MA) + 1)
                dve.wait_ge(m_tz, i + MA)
                dve.reciprocal(zrec, zden).then_inc(m_z, 1)
                dve.wait_ge(m_z, 2 * (i + MA) + 2)
                dve.wait_ge(m_r, i + MA)
                dve.tensor_tensor(tz.rearrange("p (z d) -> p z d", d=MD),
                                  pb[4][:, :].rearrange("p (z d) -> p z d", d=MD),
                                  zrec[:, :, None].to_broadcast([P, 2 * MH, MD]), op=ALU.mult).then_inc(m_tz, 1)

            def mix_q_residual(i):
                dve.wait_ge(m_xi, 2 * (i + 1 + MA))
                dve.wait_ge(m_tz, i + 1 + MA)
                pair = xall[:, ds(2 * i, 2), :]
                dve.tensor_tensor(pair, two(tz), pair, op=ALU.add).then_inc(m_r, 1)
                dve.wait_ge(m_r, i + 1 + MA)
                for u in range(2):
                    stats(2 * i + u, m_bs)

            def mix_q(i, g, before):
                if g == 0 and before >= 1:
                    mix_q_kernel(i - 1)
                if g == 1 and before >= 2:
                    mix_q_residual(i - 2)

            def mix_mlp_gain(i):
                dve.wait_ge(n_xn, 2 * (i + 1 + MA))
                dve.wait_ge(n_c, i + MA)
                dve.tensor_tensor(ev[:, :, :], xs[:, :, :], g1rep[:, None, :].to_broadcast([P, 2, C]),
                                  op=ALU.mult).then_inc(n_g, 1)

            def mix_mlp_shift(i):
                dve.wait_ge(n_g, i + 1 + MA)
                dve.wait_ge(n_y, i + MA)
                dve.tensor_tensor(em[:, :, :], ev[:, :, :], c1rep[:, None, :].to_broadcast([P, 2, C]),
                                  op=ALU.add).then_inc(n_c, 1)

            def mix_mlp_residual(i):
                dve.wait_ge(n_yp, i + 1 + MA)
                dve.wait_ge(n_c, i + 1 + MA)
                dve.tensor_tensor(xall[:, ds(2 * i, 2), :], mixY[:, :, :], em[:, :, :], op=ALU.add
                                  ).then_inc(n_y, 1)

            def mix_mlp_stats(i):
                dve.wait_ge(n_y, i + 1 + MA)
                for u in range(2):
                    stats(2 * i + u, n_bs)

            def mix_mlp(i, g, before):
                if g == 0 and before >= 2:
                    mix_mlp_stats(i - 2)
                if g == 1 and before >= 1:
                    mix_mlp_shift(i - 1)
                if g == 2:
                    mix_mlp_gain(i)

            acc_regs = [dve.alloc_register(f"acc_bin{n}") for n in range(PER_BATCH)]

            def edge_batch(b, mix, i, first=False, last=False, pairs_before=2):
                dve.load(acc_regs, bin_acc[0:1, ds(b * PER_BATCH, PER_BATCH)])
                offs = [dve.snap(r, min_val=0, max_val=(BINS - 1) * HROW) for r in acc_regs]
                for g in range(4):
                    q = 4 * b + g
                    if mix and g == 0 and pairs_before >= 2:
                        (mix_q_divide if mix is mix_q else mix_mlp_residual)(i - 2)
                    group_scores(q, g, b)
                    if not last:
                        dve.wait_ge(s_const, 1)
                        dve.tensor_copy(idx_buf[:, 4 * g:4 * g + 4], dst_tab[:, ds(4 * q + 16, 4)]
                                        ).then_inc(s_idx, 1)
                    if not (first and g == 0):
                        group_guard(q - 1, (g - 1) % 4)
                    group_leaky(q, g)
                    if not (first and g == 0):
                        group_messages(q - 1, (g - 1) % 4)
                    bank = 2 * (g % 2)
                    if not (first and g < 2):
                        add_item(2 * q - 4, bank, offs[2 * g])
                    if not (last and g >= 2):
                        onehots(q + 2, (g + 2) % 4)
                    if not (first and g < 2):
                        add_item(2 * q - 3, bank + 1, offs[2 * g + 1])
                    if mix:
                        mix(i, g, pairs_before)

            def between(n):
                if n == 0:
                    mix_q_divide(NPAIR - 2)
                    mix_q_kernel(NPAIR - 1)
                    mix_q_residual(NPAIR - 2)
                    mix_q_divide(NPAIR - 1)
                    mix_q_residual(NPAIR - 1)
                    dve.wait_ge(m_bs, NT)
                    finish_stats(2)
                else:
                    mix_mlp_residual(NPAIR - 2)
                    mix_mlp_stats(NPAIR - 2)
                    mix_mlp_shift(NPAIR - 1)
                    mix_mlp_residual(NPAIR - 1)
                    mix_mlp_stats(NPAIR - 1)

            onehots(0, 0)
            onehots(1, 1)
            edge_batches(dve, edge_batch, mix_q, mix_mlp, between=between)
            group_guard(4 * NBATCH - 1, 3)
            group_messages(4 * NBATCH - 1, 3)
            dve.load(acc_regs[0:4], bin_acc[0:1, ITEMS:ITEMS + 4])
            for m in range(4):
                add_item(ITEMS - 4 + m, m, dve.snap(acc_regs[m], min_val=0, max_val=(BINS - 1) * HROW))
            dve.wait_ge(n_bs, NT)
            finish_stats(3)
            dve.wait_ge(s_add, ITEMS + IA)

            def x2_sums(k):
                sums = acc_t[:, ds(2 * k, 2), :]
                dve.tensor_scalar(rsum, sums[:, :, C:HROW], TINY, None, op0=ALU.max).then_inc(u_rs, 1)
                dve.wait_ge(u_rs, 2 * (k + XA) + 1)
                dve.reciprocal(rrec, rsum.rearrange("p j c -> p (j c)")).then_inc(u_rs, 1)
                dve.wait_ge(u_rs, 2 * (k + XA) + 2)
                dve.wait_ge(u_g, k + XA)
                dve.tensor_tensor(hpn.rearrange("p (j h d) -> p j h d", j=2, h=HEADS),
                                  sums[:, :, 0:C].rearrange("p j (h d) -> p j h d", h=HEADS),
                                  rrec.rearrange("p (j h) -> p j h", j=2)[:, :, :, None]
                                  .to_broadcast([P, 2, HEADS, HID]), op=ALU.mult).then_inc(u_hp, 1)
                dve.wait_ge(u_hp, k + 1 + XA)
                dve.wait_ge(u_e1, k + XA)
                dve.tensor_scalar(gneg, hpn, 0.0, None, op0=ALU.min).then_inc(u_ng, 1)

            def x2_add(k):
                dve.wait_ge(u_e2, k + 1 + XA)
                dve.wait_ge(u_x2, k + XA)
                dve.scalar_tensor_tensor(gout, hpn, 0.0, ge2, op0=ALU.max, op1=ALU.add).then_inc(u_g, 1)
                dve.wait_ge(u_g, k + 1 + XA)
                dve.wait_ge(u_p, 3 * (k + 1 + XA))
                dve.tensor_tensor(xall[:, ds(2 * k, 2), :], two(gout), n2x, op=ALU.add).then_inc(u_x2, 1)
                dve.wait_ge(u_x2, k + 1 + XA)
                held(dve, u_c, NNORM * (k + XA))
                for u in range(2):
                    dve.bn_stats(st4[:, u, :], tile(2 * k + u)).then_inc(u_bs, 1)

            def ff_copy(k, first=False):
                dve.wait_ge(f_tp, k + 1 + XA)
                if not first:
                    dve.wait_ge(f_hp, FC * k)
                dve.tensor_copy(xT.rearrange("p c n -> p (c n)"), pb[0][:, :]).then_inc(f_xt, 1)

            def ff_pair(i, last_pair, ahead=True):
                if not last_pair:
                    x2_add(i + 1)
                if ahead:
                    x2_sums(i + 2)
                if not last_pair:
                    ff_copy(i + 1)
                dve.wait_ge(f_lp, i + 1 + XA)
                dve.tensor_tensor(lg.rearrange("p e t -> p t e")[:, ds(2 * i, 2), :],
                                  pb[5][:, 0:2 * EXPERTS].rearrange("p (u e) -> p u e", u=2),
                                  fbg_s[:, None, :].to_broadcast([P, 2, EXPERTS]), op=ALU.add).then_inc(f_lg, 1)
                for n in range(4):
                    u, half = n // 2, n % 2
                    if half == 0:
                        dve.wait_ge(f_st[u], 16 * (i + 1))
                    dve.wait_ge(f_htp, 4 * (i + XA) + n + 1)
                    dve.tensor_copy(frow[:, u, half * 512:(half + 1) * 512], pb[6 + half][:, :]
                                    ).then_inc(f_hr, 1)
            dve.wait_ge(f_c, 1)
            x2_sums(0)
            x2_add(0)
            x2_sums(1)
            dve.wait_ge(f_w, 16 * 4)
            ff_copy(0, first=True)
            with dve.Fori(0, NPAIR - 2) as i:
                ff_pair(i, False)
            ff_pair(NPAIR - 2, False, ahead=False)
            ff_pair(NPAIR - 1, True, ahead=False)

            routed = [0]

            def step(ins):
                routed[0] += 1
                ins.then_inc(f_rt, 1)
                dve.wait_ge(f_rt, routed[0])

            def over_experts(v):
                return v[:, None, :].to_broadcast([P, EXPERTS, NT])

            def by_tile(v):
                return v.rearrange("p e t -> p t e")
            dve.wait_ge(f_lg, NPAIR + XA)
            step(dve.tensor_reduce(lmax, by_tile(lg), axis=AX_X, op=ALU.max))
            step(dve.tensor_tensor(lix, lg, over_experts(lmax), op=ALU.subtract))
            dve.wait_ge(f_le, 1)
            step(dve.tensor_reduce(lsum, by_tile(lex), axis=AX_X, op=ALU.add))
            step(dve.reciprocal(lmax, lsum))
            step(dve.tensor_tensor(lg, lex, over_experts(lmax), op=ALU.mult))
            step(dve.tensor_reduce(ptop, by_tile(lg), axis=AX_X, op=ALU.max))
            step(dve.tensor_tensor(lex, lg, over_experts(ptop), op=ALU.is_equal))
            step(dve.tensor_tensor(lix, lex, iota_e8[:, :, None].to_broadcast([P, EXPERTS, NT]), op=ALU.mult))
            step(dve.tensor_reduce(lidx, by_tile(lix), axis=AX_X, op=ALU.min))
            step(dve.tensor_tensor(lex, iota_e8[:, :, None].to_broadcast([P, EXPERTS, NT]), over_experts(lidx),
                                   op=ALU.is_equal))
            dve.tensor_tensor(ptop, ptop, valid[:, 1:NT + 1], op=ALU.mult)
            dve.tensor_tensor(tok1, tok1, valid[:, 1:NT + 1], op=ALU.mult)
            step(dve.tensor_tensor(oh_e, lex, over_experts(valid[:, 1:NT + 1]), op=ALU.mult))
            assert routed[0] == NROUTE

            tables = [0]

            def rstep(ins):
                tables[0] += 1
                ins.then_inc(r_st, 1)
                dve.wait_ge(r_st, tables[0])
            dve.wait_ge(f_hr, 4 * NPAIR + AHEAD)
            rstep(dve.memset(zeros_r[:, :], 0.0))
            dve.wait_ge(r_mm, 1)
            pre, tot = head(pb[1][:, 0:EXPERTS * NT]), head(pb[2][:, 0:EXPERTS * NT])
            for e in range(EXPERTS):
                ins = dve.tensor_tensor_scan(rk_base[:, e, :], tot[:, e, :], zeros_r[:, 0:NT], 0.0,
                                             op0=ALU.add, op1=ALU.add)
            rstep(ins)
            rstep(dve.tensor_tensor(rk_all, rk_base, tot, op=ALU.subtract))
            rstep(dve.tensor_tensor(rk_all, rk_all, pre, op=ALU.add))
            rstep(dve.tensor_scalar(rti[:, 0, :], rk_base[:, :, NT - 1], float(P - 1), None, op0=ALU.add))
            rstep(dve.tensor_scalar(rti[:, 1, :], rti[:, 0, :], 7, None, op0=ALU.logical_shift_right))
            rstep(dve.tensor_copy(rt[:, 0, :], rti[:, 1, :]))
            rstep(dve.tensor_tensor_scan(rt[:, 1, :], rt[:, 0, :], zeros_r[:, 0:EXPERTS], 0.0,
                                         op0=ALU.add, op1=ALU.add))
            rstep(dve.tensor_tensor(rt[:, 2, :], rt[:, 1, :], rt[:, 0, :], op=ALU.subtract))
            rstep(dve.tensor_scalar(rt[:, 3, :], rt[:, 2, :], float(P), None, op0=ALU.mult))
            rstep(dve.tensor_tensor(rk_all, rk_all, rt[:, 3, :][:, :, None].to_broadcast([P, EXPERTS, NT]),
                                    op=ALU.add))
            rstep(dve.tensor_tensor(rk_mul, rk_all, oh_e, op=ALU.mult))
            rstep(dve.tensor_reduce(posf, rk_mul.rearrange("p e t -> p t e"), axis=AX_X, op=ALU.add))
            rstep(dve.tensor_copy(posi[:, 0, :], posf))
            rstep(dve.tensor_scalar(posi[:, 1, :], posi[:, 0, :], P - 1, None, op0=ALU.bitwise_and))
            rstep(dve.tensor_scalar(posi[:, 2, :], posi[:, 0, :], 7, None, op0=ALU.logical_shift_right))
            rstep(dve.tensor_copy(lanef, posi[:, 1, :]))
            rstep(dve.tensor_copy(tilef, posi[:, 2, :]))
            rstep(dve.memset(sl_e, 0.0))
            for e in range(1, EXPERTS):
                rstep(dve.scalar_tensor_tensor(sl_e, iota_k[:, 0:NSLOT], rt[:, 2, e:e + 1], sl_e,
                                               op0=ALU.is_ge, op1=ALU.add))
            dve.tensor_scalar(slot_wd[0:1, 0:NSLOT], sl_e[0:1, :], float(FC * C), None, op0=ALU.mult)
            dve.tensor_scalar(slot_bd[0:1, 0:NSLOT], sl_e[0:1, :], float(C), None, op0=ALU.mult)
            dve.wait_ge(f_xt, NPAIR + XA)
            def permute(i, u):
                t = 2 * i + u
                dve.wait_ge(r_acc, 2 * i + 2)
                dve.tensor_scalar(lane_oh[:, u, :], iota_p[:, :], lanef[:, ds(t, 1)], None, op0=ALU.is_equal)
                dve.tensor_scalar(tile_oh[:, u, 0, :], iota_k[:, 0:NSLOT], tilef[:, ds(t, 1)], tok1[:, ds(t, 1)],
                                  op0=ALU.is_equal, op1=ALU.mult)
                dve.tensor_scalar(tile_oh[:, u, 1, :], iota_k[:, 0:NSLOT], tilef[:, ds(t, 1)], ptop[:, ds(t, 1)],
                                  op0=ALU.is_equal, op1=ALU.mult).then_inc(r_oh, 1)
            with dve.Fori(0, NPAIR) as i:
                permute(i, 0)
                permute(i, 1)
            dve.wait_ge(r_acc, NT + 2)
            perm = pb[3][:, 0:NSLOT]
            dve.tensor_copy(sl_p, pb[3][:, NSLOT:2 * NSLOT])
            rstep(dve.tensor_scalar(permz, perm, 0.0, float(SKIP), op0=ALU.is_equal, op1=ALU.mult))
            rstep(dve.scalar_tensor_tensor(permz, perm, -1.0, permz, op0=ALU.add, op1=ALU.add))
            dve.wait_ge(f_st[0], 16 * NPAIR + 16)
            dve.wait_ge(f_st[1], 16 * NPAIR + 16)
            rstep(dve.tensor_copy(permi, permz))
            dve.memset(grow[:, :, :], 0.0).then_inc(r_done, 1)
            dve.wait_ge(r_done, 1)

            bd_regs = [dve.alloc_register(f"bd_slot{n}") for n in range(GROWS)]

            def name_rows(s, u):
                dve.wait_ge(s_const, 1)
                dve.tensor_copy(gidx[:, u:u + 1], permi[:, ds(s, 1)]).then_inc(e_ix, 1)

            def expert_out(s, u, half_before, off):
                v = u % 2
                if not (isinstance(half_before, int) and half_before == 0):
                    held(dve, e_out[v], 16 * half_before)
                dve.tensor_copy(oidx[:, v:v + 1], permi[:, ds(s, 1)])
                dve.wait_ge(e_yp, s + 1 + AHEAD)
                dve.tensor_tensor(yout[:, v, :], pb[4 + v][:, 0:C], bd_s[:, ds(off, C)], op=ALU.add
                                  ).then_inc(e_b, 1)
                dve.wait_ge(e_b, s + 1)
                dve.scalar_tensor_tensor(yout[:, v, :], yout[:, v, :], sl_p[:, ds(s, 1)], grow[:, u, FF:FROW],
                                         op0=ALU.mult, op1=ALU.add).then_inc(e_y, 1)
                dve.wait_ge(e_y, s + 1 + AHEAD)

            def expert_tiles(i, last):
                dve.load(bd_regs, slot_bd[0:1, ds(GROWS * i, GROWS)])
                offs = [dve.snap(r, min_val=0, max_val=(EXPERTS - 1) * C) for r in bd_regs]
                for u in range(GROWS):
                    s = GROWS * i + u
                    if not (last and u):
                        name_rows(s + GROWS - 1, (u + GROWS - 1) % GROWS)
                    expert_out(s, u, 2 * i + u // 2, offs[u])
            for u in range(GROWS - 1):
                name_rows(u, u)
            dve.wait_ge(f_wd, 16 * (EXPERTS + 1))
            expert_tiles(0, False)
            with dve.Fori(1, NSLOT // GROWS - 1) as i:
                expert_tiles(i, False)
            expert_tiles(NSLOT // GROWS - 1, True)


def kernel(x, src, dst, L0_gnn_W, L0_gnn_a, L0_mix_Wqkv, L0_mix_ln1_g, L0_mix_ln1_b, L0_mix_W1, L0_mix_b1,
           L0_mix_W2, L0_mix_b2, L0_mix_ln2_g, L0_mix_ln2_b, L0_ffn_W1, L0_ffn_b1, L0_ffn_Wg, L0_ffn_bg,
           L0_ffn_Wd, L0_ffn_bd):
    import numpy as np
    import concourse.bacc as bacc
    from concourse.bass_utils import run_bass_kernel_spmd

    def rows(a):
        return np.ascontiguousarray(np.broadcast_to(np.asarray(a).reshape(1, -1), (P, np.asarray(a).size)))

    def columns(a):
        return np.asarray(a).reshape(-1, P).T

    def slots(a):
        a = np.asarray(a)
        return np.concatenate([a, np.full(SLOTS - a.shape[0], NOBODY, a.dtype)])

    x = np.asarray(x)
    ga = np.asarray(L0_gnn_a).reshape(HEADS, 2, HID)[:, ::-1]
    laid = {
        "x": np.concatenate([x, np.zeros((ROWS - N_NODES, C), x.dtype)]),
        "src": slots(src),
        "dst": slots(dst),
        "gw": np.asarray(L0_gnn_W).transpose(1, 0, 2).reshape(C, C),
        "gwt": np.asarray(L0_gnn_W).transpose(2, 0, 1),
        "ga": ga.transpose(2, 0, 1),
        "wqkv_t": np.asarray(L0_mix_Wqkv).T,
        "ln1_g": columns(L0_mix_ln1_g), "ln1_b": columns(L0_mix_ln1_b),
        "w1_t": np.asarray(L0_mix_W1).T, "b1": columns(L0_mix_b1),
        "w2_t": np.asarray(L0_mix_W2).T, "b2": rows(L0_mix_b2),
        "ln2_g": rows(L0_mix_ln2_g), "ln2_b": rows(L0_mix_ln2_b),
        "ln1_g_rows": rows(L0_mix_ln1_g), "ln1_b_rows": rows(L0_mix_ln1_b),
        "fw1": L0_ffn_W1, "fb1": columns(L0_ffn_b1), "fwg": L0_ffn_Wg, "fbg": rows(L0_ffn_bg),
        "fwd": L0_ffn_Wd, "fbd": rows(L0_ffn_bd),
    }
    laid = {f"in_{k}": np.ascontiguousarray(v) for k, v in laid.items()}
    nc = bacc.Bacc("TRN2", target_bir_lowering=False, num_devices=1)
    aps = {k[3:]: nc.dram_tensor(k, a.shape, mybir.dt.from_np(a.dtype), kind="ExternalInput").ap()
           for k, a in laid.items()}
    out = nc.dram_tensor("out", [ROWS, C], F32, kind="ExternalOutput").ap()
    gps_layer(nc, out=out, **aps)
    r = run_bass_kernel_spmd(nc, [laid], core_ids=[0])
    return np.asarray(r.results[0]["out"])[0:N_NODES]
```

```python
from contextlib import ExitStack

import concourse.bass as bass
from concourse import mybir

P = 128
C = 256
CC = C // P
N_NODES = 6250
NT = 50
ROWS = NT * P
BINS = -(-N_NODES // P)
N_EDGES = 100000
LOG_SLOTS = 17
SLOTS = 1 << LOG_SLOTS
SC = SLOTS // P
LOG_SC = 10
EARLY_LEVELS = 6
PAIR = 2 * P
TPP = SC // PAIR
FIELD = 13
NOBODY = (1 << FIELD) - 1
KEY_ONE = 1 << 30
HEADS = 4
HID = C // HEADS
HROW = C + HEADS
HCOL = C + 2 * HEADS
PER_BATCH = 8
NBATCH = -(-(-(-N_EDGES // PAIR) + BINS - 1) // PER_BATCH)
ITEMS = NBATCH * PER_BATCH
NPAIR = NT // 2
MH = 8
MD = C // MH
FF = 1024
FC = FF // P
EXPERTS = 8
RG = 5
GROWS = 4
NSLOT = -(-((N_NODES + EXPERTS * (P - 1)) // P) // GROWS) * GROWS
FROW = FF + C
SKIP = 100000
EPS = 1e-5
EPS_ATTN = 1e-6
TINY = 1.1754944e-38

ALU = mybir.AluOpType
ACT = mybir.ActivationFunctionType
AX_X = mybir.AxisListType.X
F32 = mybir.dt.float32
BF16 = mybir.dt.bfloat16
I32 = mybir.dt.int32
ds = bass.ds


def gps_layer(nc, x, src, dst, gw, gwt, ga, wqkv_t, ln1_g, ln1_b, ln1_g_rows, ln1_b_rows, w1_t, b1, w2_t,
              b2, ln2_g, ln2_b, fw1, fb1, fwg, fbg, fwd, fbd, out):
    ctx = ExitStack()
    with ctx:
        def sb(name, shape, dt=F32):
            return ctx.enter_context(nc.sbuf_tensor(name, shape, dt))

        def sem(name):
            return ctx.enter_context(nc.semaphore(name))

        node_table = nc.dram_tensor("node_table", [ROWS, HROW], F32, kind="Internal").ap()
        expert_table = nc.dram_tensor("expert_table", [ROWS, FROW], F32, kind="Internal").ap()

        xall = sb("xall", [P, NT, C])
        asrc = sb("asrc", [P, NT * HEADS])
        w_gat = sb("w_gat", [P, CC, HCOL])
        w_kv = sb("w_kv", [P, CC, 2 * C])
        w_q = sb("w_q", [P, CC, C])
        w1g = sb("w1g", [P, CC, C])
        w2s = sb("w2s", [P, CC, C])
        wt_heads = sb("wt_heads", [HID, HEADS, C])
        a_heads = sb("a_heads", [HID, HEADS, 2])
        b1col = sb("b1col", [P, CC])
        b1eff = sb("b1eff", [P, CC])
        g1col = sb("g1col", [P, CC])
        be1col = sb("be1col", [P, CC])
        g1rep = sb("g1rep", [P, C])
        c1rep = sb("c1rep", [P, C])
        b2rep = sb("b2rep", [P, C])
        g2rep = sb("g2rep", [P, C])
        c2rep = sb("c2rep", [P, C])
        kvbd = sb("kvbd", [P, CC, P + HEADS])
        std = sb("std", [P, NT])
        rstd = sb("rstd", [P, NT])
        nmr = sb("nmr", [P, NT])
        ident = sb("ident", [P, P])
        upper = sb("upper", [P, P])
        ones = sb("ones", [P, P])
        iota_p = sb("iota_p", [P, P])
        iota_k = sb("iota_k", [P, ITEMS])
        valid = sb("valid", [P, NT + 1])
        minus1 = sb("minus1", [P, 1])
        pm1 = sb("pm1", [P, 2])
        part_i = sb("part_i", [P, 8], I32)
        bit_i = sb("bit_i", [P, 8], I32)
        sign = sb("sign", [P, 8])
        srcrel = sb("srcrel", [P, (ITEMS + PER_BATCH) * 2])
        dst_tab = sb("dst_tab", [P, (ITEMS + PER_BATCH) * 2], I32)
        bin_acc = sb("bin_acc", [1, ITEMS + PER_BATCH], I32)
        bin_asrc = sb("bin_asrc", [1, ITEMS + PER_BATCH], I32)
        xs = sb("xs", [P, 2, C])
        xT = sb("xT", [P, CC, 2 * P])
        ev = sb("ev", [P, 2, C])
        em = sb("em", [P, 2, C])
        qs = sb("qs", [P, CC, 2 * P])

        stat = sb("stat", [P, NT, 6])
        st_s = sb("st_s", [P, 4, NT])
        slot_wd = sb("slot_wd", [1, 64], I32)
        slot_bd = sb("slot_bd", [1, 64], I32)

        ACC = NT * HROW
        WD = EXPERTS * FC * C
        ARENA = 27300
        arena = sb("arena", [P, ARENA])

        class Carve:
            def __init__(self, at):
                self.at = at

            def take(self, n, dt=F32):
                view = arena[:, self.at:self.at + n]
                self.at += n
                assert self.at <= ARENA, self.at
                return view if dt is F32 else view.bitcast(dt)

        def two(view):
            return view.rearrange("p (j c) -> p j c", j=2)

        c0 = Carve(0)
        key_a = c0.take(SC)
        key_b = c0.take(SC)
        hbuf, hpos, hneg, hcl = (two(c0.take(2 * HCOL)) for _ in range(4))
        kexp, kpos, kneg, kbuf, vbuf = (two(c0.take(2 * C)) for _ in range(5))
        ACC_FREE = c0.at
        field = [c0.take(SC // 2, BF16) for _ in range(4)]
        fint = [c0.take(SC, I32) for _ in range(2)]
        sel = c0.take(TPP * ITEMS // 2, BF16).rearrange("p (b k) -> p b k", b=TPP)
        selg = two(c0.take(2 * ITEMS))
        rep = c0.take(TPP * P, BF16).rearrange("p (s b m) -> p s b m", s=2, b=TPP)
        small = c0.take(16 * TPP).rearrange("p (s b) -> p s b", b=TPP)
        smalli = c0.take(4 * TPP, I32).rearrange("p (s b) -> p s b", b=TPP)
        binf = c0.take(ITEMS)
        binc = c0.take(ITEMS)
        acc = arena[:, 0:ACC]
        acc_t = acc.rearrange("p (t c) -> p t c", c=HROW)
        ACC_ACT = ACC - 24 * P
        c1 = Carve(ACC)
        rows = c1.take(16 * HROW).rearrange("p (s c) -> p s c", c=HROW)
        onehot = c1.take(16 * P).rearrange("p (s c) -> p s c", c=P)
        onehot_t = c1.take(8 * P).rearrange("p (q c) -> p q c", q=2)
        score, leaky, expd = (c1.take(8 * HEADS).rearrange("p (q s h) -> p q s h", q=2, h=HEADS)
                              for _ in range(3))
        idx_buf = c1.take(16, I32)
        zden = c1.take(2 * MH)
        zrec = c1.take(2 * MH)
        tz = c1.take(2 * C)
        hT = c1.take(2 * C).rearrange("p (c n) -> p c n", c=CC)
        c2 = Carve(ACC)
        xin = two(c2.take(2 * C))
        rsum = two(c2.take(2 * HEADS))
        rrec = c2.take(2 * HEADS)
        hpn, gneg, ge1, ge2, gout = (c2.take(2 * C) for _ in range(5))
        n2, n2g, n2b, n2x = (two(c2.take(2 * C)) for _ in range(4))
        st4 = two(c2.take(2 * 6))
        norm4 = c2.take(12 * 2).rearrange("p (s u) -> p s u", u=2)
        wd_s = arena[:, 0:WD]
        bd_s = arena[:, WD:WD + EXPERTS * C]
        c3 = Carve(max(c2.at, WD + EXPERTS * C))
        fb1_s = c3.take(FC)
        fbg_s = c3.take(EXPERTS)
        iota_e8 = c3.take(EXPERTS)
        ptop, lmax, lsum, lidx = (c3.take(NT) for _ in range(4))
        sl_e = c3.take(NSLOT)
        sl_p = c3.take(NSLOT)
        fh0 = c3.take(FC * PAIR)
        c4 = Carve(c3.at)
        fhT = [v.rearrange("p (c n) -> p c n", c=FC) for v in (fh0, c3.take(FC * PAIR))]
        gT = fh0.rearrange("p (j c n) -> p j c n", j=2, c=FC)
        fw1_s = c3.take(CC * FF).rearrange("p (c n) -> p c n", c=CC)
        fwg_s = c3.take(FC * EXPERTS).rearrange("p (c n) -> p c n", c=FC)
        frow = two(c3.take(2 * FF))
        def head(view):
            return view.rearrange("p (e t) -> p e t", e=EXPERTS)
        lg, lex, lix = (head(v[:, :, :].rearrange("p a b -> p (a b)")[:, 0:EXPERTS * NT]) for v in (qs, w_q, w1g))
        oh_e = head(srcrel[:, 0:EXPERTS * NT])
        tok1 = srcrel[:, EXPERTS * NT:EXPERTS * NT + NT]
        w_kvf = w_kv[:, :, :].rearrange("p c n -> p (c n)")
        lane_oh = fh0[:, 0:2 * RG * P].rearrange("p (b g n) -> p b g n", b=2, g=RG)
        tile_oh = [v.rearrange("p (g k n) -> p g k n", g=RG, k=2) for v in
                   (fh0[:, 2 * RG * P:2 * RG * P + 2 * RG * NSLOT], w_kvf[:, 0:2 * RG * NSLOT])]
        tile_eq = w_kvf[:, 2 * RG * NSLOT:3 * RG * NSLOT].rearrange("p (g n) -> p g n", g=RG)
        grow = c4.take(GROWS * FROW).rearrange("p (u c) -> p u c", u=GROWS)
        yout = two(c4.take(2 * C))
        gidx = c4.take(GROWS, I32)
        oidx = c4.take(2, I32)
        permi = c4.take(NSLOT, I32)
        rk_base, rk_all, rk_mul = (v.rearrange("p (e t) -> p e t", e=EXPERTS)
                                   for v in (ev.rearrange("p j c -> p (j c)")[:, 0:EXPERTS * NT],
                                                   em.rearrange("p j c -> p (j c)")[:, 0:EXPERTS * NT],
                                                   qs.rearrange("p c n -> p (c n)")[:, 0:EXPERTS * NT]))
        xsf = xs.rearrange("p j c -> p (j c)")
        posf = xsf[:, 0:NT]
        posi = xsf[:, 64:64 + 3 * NT].bitcast(I32).rearrange("p (s t) -> p s t", s=3)
        lanef = xsf[:, 220:220 + NT]
        tilef = xsf[:, 272:272 + NT]
        rt = xsf[:, 324:324 + 5 * EXPERTS].rearrange("p (s e) -> p s e", e=EXPERTS)
        rti = xsf[:, 364:364 + 2 * EXPERTS].bitcast(I32).rearrange("p (s e) -> p s e", e=EXPERTS)
        zeros_r = xsf[:, 384:384 + 2 * NSLOT]
        permz = ev.rearrange("p j c -> p (j c)")[:, EXPERTS * NT:EXPERTS * NT + NSLOT]

        pb = [ctx.enter_context(nc.psum_tensor(f"bank{n}", [P, 512], F32)) for n in range(8)]

        s_x = [sem(f"x_loaded{g}") for g in range(5)]
        s_keys = sem("keys_loaded")
        s_wgt = sem("weights_loaded")
        s_const = sem("constants_ready")
        s_cstep = sem("constant_step")
        s_stat = sem("row_stats")
        s_vare = sem("variance_plus_eps")
        s_std = sem("row_std")
        s_rstd = sem("row_rstd")
        s_fold = sem("folded_weight_in_psum")
        s_foldc = sem("folded_weight_ready")
        s_prep = sem("prepared_vectors")
        s_xn = sem("xn_ready")
        s_xtp = sem("xnT_in_psum")
        s_xt = sem("xnT_ready")
        s_hp = sem("h_in_psum")
        s_kvp = sem("kv_in_psum")
        s_hc = sem("h_copied")
        s_kc = sem("kv_copied")
        s_hs = sem("h_signs")
        s_hcl = sem("h_clean")
        s_as = sem("asrc_saved")
        s_kn = sem("k_negative_part")
        s_kk = sem("k_ready")
        s_gram = sem("gram_added")
        s_hw = [sem(f"h_row_stored{j}") for j in range(2)]
        s_kvbd = sem("kvbd_ready")
        s_key = sem("key_built")
        s_st = [sem("sort_stream_a"), sem("sort_stream_b")]
        s_tp = sem("sort_transposed")
        s_te = sem("sort_turn_copied")
        s_ns = sem("norm_step")
        s_sg = sem("sort_signed")
        s_dec = sem("decoded")
        s_cnt = sem("tile_counts")
        s_cross = sem("tile_prefix_in_psum")
        s_self = sem("selectors_ready")
        s_tab = sem("item_tables_in_psum")
        s_tabs = sem("item_table_steps")
        s_items = sem("item_tables_ready")
        s_acc0 = sem("acc_cleared")
        s_idx = sem("gather_rows_named")
        s_gat = [sem(f"rows_gathered{g}") for g in range(4)]
        s_oh = sem("onehot_ready")
        s_otp = sem("onehotT_in_psum")
        s_ot = sem("onehotT_ready")
        s_al = sem("src_score_in_psum")
        s_sc = sem("score_ready")
        s_lk = sem("leaky_ready")
        s_ex = sem("exp_ready")
        s_eg = sem("exp_guarded")
        s_msg = sem("messages_ready")
        s_agg = sem("aggregated")
        s_add = sem("added")
        m_xn = sem("m_xn")
        m_xi = sem("m_xn_in_place")
        m_tp = sem("m_xT_in_psum")
        m_xt = sem("m_xT_ready")
        m_qp = sem("m_q_in_psum")
        m_qe = sem("m_q_exp")
        m_qm = sem("m_q_capped")
        m_q = sem("m_q_ready")
        m_tps = sem("m_t_in_psum")
        m_z = sem("m_z_steps")
        m_tz = sem("m_tz_ready")
        m_r = sem("m_r_ready")
        m_bs = sem("m_r_stats")
        n_xn = sem("n_ready")
        n_tp = sem("n_T_in_psum")
        n_xt = sem("n_T_ready")
        n_hp = sem("n_h_in_psum")
        n_h = sem("n_h_ready")
        n_yp = sem("n_y_in_psum")
        n_g = sem("n_gained")
        n_c = sem("n_shifted")
        n_y = sem("n_y_ready")
        n_bs = sem("n_y_stats")
        u_x = sem("u_x_loaded")
        u_n = sem("u_normed")
        u_rs = sem("u_rowsum_steps")
        u_hp = sem("u_hp_divided")
        u_ng = sem("u_negative_part")
        u_e1 = sem("u_exp_once")
        u_e2 = sem("u_exp_twice")
        u_g = sem("u_gat_ready")
        u_p = sem("u_mixer_steps")
        u_x2 = sem("u_x2_ready")
        u_bs = sem("u_x2_stats")
        u_c = sem("u_x2_norm_steps")
        f_w = sem("f_weights_loaded")
        f_wd = sem("f_wd_loaded")
        f_c = sem("f_consts")
        f_xn = sem("f_xn_ready")
        f_tp = sem("f_xT_in_psum")
        f_xt = sem("f_xT_ready")
        f_hp = sem("f_h_in_psum")
        f_h = sem("f_h_ready")
        f_lp = sem("f_logits_in_psum")
        f_lg = sem("f_logits_kept")
        f_rt = sem("f_route_step")
        f_le = sem("f_logit_exp")
        f_xs = sem("f_x2_stored")
        f_htp = sem("f_hrow_in_psum")
        f_hr = sem("f_hrow_ready")
        f_st = [sem(f"f_row_stored{j}") for j in range(2)]
        r_mm = sem("r_counts_in_psum")
        r_st = sem("r_step")
        r_eq = sem("r_tiles_matched")
        r_oh = sem("r_onehots_ready")
        r_acc = sem("r_perm_added")
        r_done = sem("r_tables_ready")
        e_ix = sem("e_rows_named")
        e_clr = sem("e_rows_cleared")
        e_g = [sem(f"e_rows_gathered{j}") for j in range(GROWS)]
        e_tp = sem("e_rowT_in_psum")
        e_t = sem("e_rowT_ready")
        e_yp = sem("e_y_in_psum")
        e_b = sem("e_bias_added")
        e_y = sem("e_y_ready")
        e_out = [sem(f"e_out_stored{j}") for j in range(2)]

        block = ctx.enter_context(nc.Block())

        AHEAD, GA, IA, FA = 2, 4, 8, 4
        MA = 2
        XA = 2

        HALF = NPAIR + 2
        assert NBATCH > 2 * HALF

        def edge_batches(eng, batch, mix_q, mix_mlp, after=None):
            for n, mix in enumerate((mix_q, mix_mlp)):
                at = n * HALF
                batch(at, mix, 0, (0,), first=(n == 0))
                batch(at + 1, mix, 1, (0, 1))
                with eng.Fori(at + 2, at + NPAIR) as b:
                    batch(b, mix, b - at, (0, 1, 2))
                batch(at + NPAIR, mix, NPAIR, (1, 2))
                batch(at + NPAIR + 1, mix, NPAIR + 1, (2,))
                if after:
                    after(n)
            for b in range(2 * HALF, NBATCH):
                batch(b, None, 0, (), last=(b == NBATCH - 1))

        keys = [key_a, key_b]
        turn_stages = [n for level in range(LOG_SC + 1, LOG_SLOTS + 1) for n in (level - 7, 7)]
        TURNS = len(turn_stages)
        DOUBLES = 4
        FIRST_TURN = NPAIR - 1 - DOUBLES - TURNS
        sorted_keys = key_b
        NROUTE = 11
        NNORM = 9

        def chunked(w):
            return w.rearrange("(c p) n -> p c n", p=P)

        WEIGHTS = [
            (wt_heads[:, :, :], gwt), (a_heads[:, :, :], ga), (w_gat[:, :, 0:C], chunked(gw)),
            (w_kv[:, :, :], chunked(wqkv_t[:, C:3 * C])), (w_q[:, :, :], chunked(wqkv_t[:, 0:C])),
            (w1g[:, :, :], chunked(w1_t)), (w2s[:, :, :], chunked(w2_t)),
            (b1col[:, :], b1), (g1col[:, :], ln1_g), (be1col[:, :], ln1_b),
            (g1rep[:, :], ln1_g_rows), (c1rep[:, :], ln1_b_rows), (b2rep[:, :], b2),
            (g2rep[:, :], ln2_g), (c2rep[:, :], ln2_b),
        ]
        N_WEIGHTS = len(WEIGHTS)

        trp = [pb[0][:, 0:C], pb[0][:, C:2 * C]]
        hps = [pb[1][:, 0:HCOL], pb[2][:, 0:HCOL]]
        kvps = [pb[3], pb[4]]
        gram = pb[5][:, 0:CC * (P + 1)].rearrange("p (c m) -> p c m", c=CC)
        sortp = [pb[6], pb[7]]
        psT, psA = pb[0], pb[1]
        psG = [pb[2], pb[3], pb[6], pb[7]]
        score_ps = psA[:, 0:32].rearrange("p (q s h) -> p q s h", q=2, h=HEADS)
        den_ps = psA[:, 32:32 + 2 * MH].rearrange("p (u c h) -> p u c h", u=2, c=CC)
        mixT = pb[4][:, :].rearrange("p (c n) -> p c n", c=CC)
        mixQ = pb[5][:, :].rearrange("p (c n) -> p c n", c=CC)
        mixY = pb[4][:, :].rearrange("p (u n) -> p u n", u=2)

        due_reg = {}

        def held(eng, signal, value):
            due = due_reg[eng.engine]
            eng.reg_mov(due, value)
            eng.wait_ge(s_const, 1)
            eng.wait_ge(signal, due)

        def ones_start(eng, sems, n):
            for s in sems:
                eng.sem_inc(s, n)

        @block.sync
        def _(sp):
            due_reg[sp.engine] = sp.alloc_register("due_count")
            sp.dma_start(key_a.bitcast(I32), src.rearrange("(p c) -> p c", p=P)).then_inc(s_keys, 16)
            sp.dma_start(key_b.bitcast(I32), dst.rearrange("(p c) -> p c", p=P)).then_inc(s_keys, 16)
            for g in range(5):
                t0 = g * (NT // 5)
                sp.dma_start(xall[:, t0:t0 + NT // 5, :],
                             x[t0 * P:(t0 + NT // 5) * P, :].rearrange("(t p) c -> p t c", p=P)
                             ).then_inc(s_x[g], 16)
            def store(i, j):
                held(sp, s_hcl, 2 * i + j + 1 + AHEAD)
                sp.dma_start(node_table[ds((2 * i + j) * P, P), :], hcl[:, j, 0:HROW]).then_inc(s_hw[j], 16)
            with sp.Fori(0, NPAIR) as i:
                store(i, 0)
                store(i, 1)
            def reload(k):
                held(sp, u_p, 3 * (k + XA))
                sp.dma_start(xin, x[ds(2 * k * P, 2 * P), :].rearrange("(t p) c -> p t c", p=P)
                             ).then_inc(u_x, 16)
            def store_x2(k):
                held(sp, u_x2, k + 1 + XA)
                sp.dma_start(expert_table[ds(2 * k * P, 2 * P), FF:FROW].rearrange("(t p) c -> p t c", p=P),
                             xall[:, ds(2 * k, 2), :]).then_inc(f_xs, 16)
            def store_rows(i):
                for u in range(2):
                    held(sp, f_hr, 4 * i + 2 * u + 2 + AHEAD)
                    sp.dma_start(expert_table[ds((2 * i + u) * P, P), 0:FF], frow[:, u, :]).then_inc(f_st[u], 16)
            sp.wait_ge(s_add, ITEMS + IA)
            reload(0)
            sp.dma_start(fw1_s, fw1.rearrange("(c p) n -> p c n", p=P)).then_inc(f_w, 16)
            sp.dma_start(fwg_s, fwg.rearrange("(c p) n -> p c n", p=P)).then_inc(f_w, 16)
            sp.dma_start(fb1_s, fb1).then_inc(f_w, 16)
            sp.dma_start(fbg_s, fbg).then_inc(f_w, 16)
            reload(1)
            store_x2(0)
            reload(2)
            store_x2(1)
            with sp.Fori(0, NPAIR - 3) as i:
                reload(i + 3)
                store_x2(i + 2)
                store_rows(i)
            store_x2(NPAIR - 1)
            with sp.Fori(NPAIR - 3, NPAIR) as i:
                store_rows(i)

        @block.gpsimd
        def _(pool):
            due_reg[pool.engine] = pool.alloc_register("due_count")
            ones_start(pool, (s_hs, s_hcl, s_as, s_kk), AHEAD)
            ones_start(pool, (u_p,), 3 * XA)
            ones_start(pool, (u_c,), NNORM * XA)
            ones_start(pool, (*f_st, *s_hw), 16)
            pool.memset(ident[:, :], 0.0).then_inc(s_cstep, 1)
            pool.memset(upper[:, :], 1.0).then_inc(s_cstep, 1)
            pool.memset(valid[:, :], 1.0).then_inc(s_cstep, 1)
            pool.memset(ones[:, :], 1.0)
            pool.memset(minus1[:, :], -1.0)
            pool.memset(ev[:, :, :], 0.0)
            pool.memset(em[:, :, :], 0.0)
            pool.memset(kbuf[:, 1, :], 0.0)
            pool.memset(vbuf[:, 1, :], 0.0)
            pool.memset(kvbd[:, :, :], 0.0)
            pool.iota(iota_p[:, :], [[1, P]], 0, 0, allow_small_or_imprecise_dtypes=True)
            pool.iota(iota_k[:, :], [[1, ITEMS]], 0, 0, allow_small_or_imprecise_dtypes=True)
            pool.iota(pm1[:, :], [[-2, 2]], 1, 0, allow_small_or_imprecise_dtypes=True)
            pool.iota(part_i[:, :], [[0, 8]], 0, 1)
            pool.wait_ge(s_cstep, 3)
            pool.affine_select(out=ident[:, :], in_=ident[:, :], compare_op=ALU.not_equal, fill=1.0,
                               base=0, pattern=[[-1, P]], channel_multiplier=1)
            pool.affine_select(out=upper[:, :], in_=upper[:, :], compare_op=ALU.is_gt, fill=0.0,
                               base=0, pattern=[[1, P]], channel_multiplier=-1)
            pool.affine_select(out=valid[:, :], in_=valid[:, :], compare_op=ALU.is_ge, fill=0.0,
                               base=N_NODES - 1 + P, pattern=[[-P, NT + 1]], channel_multiplier=-1
                               ).then_inc(s_const, 1)

            def guard(i, j):
                t = 2 * i + j
                done, two_ago = t + 1 + AHEAD, t + 1
                held(pool, s_hc, done)
                held(pool, s_hcl, two_ago)
                pool.tensor_scalar(hpos[:, j, :], hbuf[:, j, :], 0.0, None, op0=ALU.max)
                pool.tensor_scalar(hneg[:, j, :], hbuf[:, j, :], 0.0, None, op0=ALU.min).then_inc(s_hs, 1)
                held(pool, s_kc, done)
                held(pool, s_gram, two_ago)
                pool.tensor_tensor(kbuf[:, j, :], kexp[:, j, :], kpos[:, j, :], op=ALU.add).then_inc(s_kk, 1)
                held(pool, s_hs, done)
                held(pool, s_hw[j], 16 * (i + 1))
                held(pool, s_as, two_ago)
                pool.tensor_tensor(hcl[:, j, :], hpos[:, j, :], hneg[:, j, :], op=ALU.add).then_inc(s_hcl, 1)
                held(pool, s_hcl, done)
                pool.tensor_copy(asrc[:, ds(t * HEADS, HEADS)], hcl[:, j, HROW:HCOL]).then_inc(s_as, 1)
            with pool.Fori(0, NPAIR) as i:
                guard(i, 0)
                guard(i, 1)

            pool.wait_ge(s_hw[0], 16 * NPAIR + 16)
            pool.wait_ge(s_hw[1], 16 * NPAIR + 16)
            pool.wait_ge(s_dec, 4)
            pool.wait_ge(s_kvbd, 1)
            pool.wait_ge(s_as, NT + AHEAD)
            pool.memset(acc[:, 0:ACC_FREE], 0.0).then_inc(s_acc0, 1)
            def gather(b):
                for g in range(4):
                    q = 4 * b + g
                    held(pool, s_idx, q + 1)
                    held(pool, s_agg, 2 * q - 8 + IA + 2)
                    for s in range(4 * g, 4 * g + 4):
                        pool.indirect_dma_start(
                            out=rows[:, s, :], out_offset=None, in_=node_table[:, :],
                            in_offset=bass.IndirectOffsetOnAxis(ap=idx_buf[:, s:s + 1], axis=0)
                        ).then_inc(s_gat[g], 16)
            with pool.Fori(0, NBATCH) as b:
                gather(b)

            pool.wait_ge(s_add, ITEMS + IA)
            pool.iota(tok1, [[P, NT]], 1, 1, allow_small_or_imprecise_dtypes=True)
            pool.iota(iota_e8, [[1, EXPERTS]], -EXPERTS, 0, allow_small_or_imprecise_dtypes=True)
            pool.memset(norm4[:, 11, :], -0.5).then_inc(f_c, 1)
            pool.wait_ge(f_c, 1)

            def mixer_out(k):
                before = 3 * (k + XA)
                held(pool, u_n, 2 * (k + 1 + XA))
                held(pool, u_p, before)
                pool.tensor_tensor(n2g, n2, g2rep[:, None, :].to_broadcast([P, 2, C]), op=ALU.mult
                                   ).then_inc(u_p, 1)
                held(pool, u_p, before + 1)
                pool.tensor_tensor(n2b, n2g, c2rep[:, None, :].to_broadcast([P, 2, C]), op=ALU.add
                                   ).then_inc(u_p, 1)
                held(pool, u_p, before + 2)
                held(pool, u_x, 16 * (k + 1))
                held(pool, u_x2, k + XA)
                pool.tensor_tensor(n2x, n2b, xin, op=ALU.add).then_inc(u_p, 1)

            def x2_norm(k):
                before = NNORM * (k + XA)
                mean_e, dev_e, mean_o, dev_o = (st4[:, :, c] for c in (1, 2, 4, 5))
                v = lambda n: norm4[:, n, :]
                held(pool, u_bs, 2 * (k + 1 + XA))
                held(pool, f_xn, 2 * (k + XA))
                pool.tensor_tensor(v(0), mean_e, mean_o, op=ALU.add)
                pool.tensor_tensor(v(1), mean_e, mean_o, op=ALU.subtract)
                pool.tensor_tensor(v(2), dev_e, dev_o, op=ALU.add).then_inc(u_c, 1)
                held(pool, u_c, before + 1)
                pool.tensor_tensor(v(3), v(1), v(1), op=ALU.mult).then_inc(u_c, 1)
                pool.tensor_scalar(v(4), v(2), 1.0 / C, EPS, op0=ALU.mult, op1=ALU.add).then_inc(u_c, 1)
                held(pool, u_c, before + 3)
                pool.tensor_scalar(v(5), v(3), 0.25, None, op0=ALU.mult).then_inc(u_c, 1)
                held(pool, u_c, before + 4)
                pool.tensor_tensor(v(6), v(4), v(5), op=ALU.add).then_inc(u_c, 1)
                held(pool, u_c, before + 5)
                pool.tensor_tensor(v(7), v(6), v(11), op=ALU.pow).then_inc(u_c, 1)
                held(pool, u_c, before + 6)
                pool.tensor_tensor(v(8), v(0), v(7), op=ALU.mult).then_inc(u_c, 1)
                held(pool, u_c, before + 7)
                pool.tensor_tensor(v(9), v(8), v(11), op=ALU.mult).then_inc(u_c, 2)
                held(pool, u_c, before + 9)

            mixer_out(0)
            mixer_out(1)
            x2_norm(0)
            mixer_out(2)
            x2_norm(1)
            with pool.Fori(0, NPAIR - 3) as i:
                x2_norm(i + 2)
                mixer_out(i + 3)
            x2_norm(NPAIR - 1)

            pool.wait_ge(f_xs, 16 * NPAIR)
            pool.wait_ge(f_st[0], 16 * NPAIR + 16)
            pool.wait_ge(f_st[1], 16 * NPAIR + 16)
            pool.wait_ge(f_lp, NPAIR + XA)
            pool.memset(grow[:, :, :], 0.0).then_inc(e_clr, 1)
            pool.wait_ge(e_clr, 1)
            def take(s, u):
                held(pool, e_ix, s + 1)
                pool.indirect_dma_start(
                    out=grow[:, u, :], out_offset=None, in_=expert_table[:, :],
                    in_offset=bass.IndirectOffsetOnAxis(ap=gidx[:, u:u + 1], axis=0),
                    bounds_check=ROWS - 1, oob_is_err=False).then_inc(e_g[u], 16)
            def give(s, v):
                held(pool, e_y, s + 1 + AHEAD)
                pool.indirect_dma_start(
                    out=out[:, :], out_offset=bass.IndirectOffsetOnAxis(ap=oidx[:, v:v + 1], axis=0),
                    in_=yout[:, v, :], in_offset=None,
                    bounds_check=ROWS - 1, oob_is_err=False).then_inc(e_out[v], 16)
            for u in range(GROWS - 1):
                take(u, u)
            def experts(i, last):
                for u in range(GROWS):
                    s = GROWS * i + u
                    if not (last and u):
                        take(s + GROWS - 1, (u + GROWS - 1) % GROWS)
                    give(s, u % 2)
            with pool.Fori(0, NSLOT // GROWS - 1) as i:
                experts(i, False)
            experts(NSLOT // GROWS - 1, True)
            pool.wait_ge(e_out[0], 16 * (NSLOT // 2))
            pool.wait_ge(e_out[1], 16 * (NSLOT // 2))

        @block.tensor
        def _(pe):
            ones_start(pe, (s_xtp, s_hp, s_kvp), AHEAD)
            ones_start(pe, (s_otp, s_al), GA)
            ones_start(pe, (s_agg,), IA)
            ones_start(pe, (e_yp,), AHEAD)
            ones_start(pe, (f_tp, f_lp, r_acc), XA)
            ones_start(pe, (f_htp,), 4 * XA)
            ones_start(pe, (m_tp, m_qp, m_tps, n_tp, n_hp, n_yp), MA)
            pe.sem_inc(s_gram, 1)

            def transpose(psum, tile):
                return pe.transpose(psum, tile, ident[:, :])

            pe.wait_ge(s_const, 1)
            pe.wait_ge(s_wgt, 16 * N_WEIGHTS)
            for c in range(CC):
                for h in range(HEADS):
                    at = (c * HEADS + h) * 2
                    last = pe.matmul(pb[7][:, at:at + 2], lhsT=wt_heads[:, h, c * P:(c + 1) * P],
                                     rhs=a_heads[:, h, :], start=True, stop=True)
            last.then_inc(s_fold, 1)
            pe.wait_ge(s_foldc, 1)
            for oc in range(CC):
                for c in range(CC):
                    last = pe.matmul(pb[7][:, 64 + oc:65 + oc], lhsT=w1g[:, c, oc * P:(oc + 1) * P],
                                     rhs=be1col[:, c:c + 1], start=(c == 0), stop=(c == CC - 1))
            last.then_inc(s_fold, 1)

            def node_t(t, j):
                pe.wait_ge(s_xn, t + 1 + AHEAD)
                pe.wait_ge(s_xt, t + 1)
                for c in range(CC):
                    last = transpose(trp[j][:, c * P:(c + 1) * P], xs[:, j, c * P:(c + 1) * P])
                last.then_inc(s_xtp, 1)

            def node_mm(t, j):
                pe.wait_ge(s_xt, t + 1 + AHEAD)
                pe.wait_ge(s_hc, t + 1)
                for c in range(CC):
                    last = pe.matmul(hps[j], lhsT=xT[:, c, j * P:(j + 1) * P], rhs=w_gat[:, c, :],
                                     start=(c == 0), stop=(c == CC - 1))
                last.then_inc(s_hp, 1)
                pe.wait_ge(s_kc, t + 1)
                for c in range(CC):
                    last = pe.matmul(kvps[j][:, :], lhsT=xT[:, c, j * P:(j + 1) * P], rhs=w_kv[:, c, :],
                                     start=(c == 0), stop=(c == CC - 1))
                last.then_inc(s_kvp, 1)

            def node_gram(t, j):
                pe.wait_ge(s_kk, t + 1 + AHEAD)
                for c in range(CC):
                    pe.matmul(gram[:, c, 0:P], lhsT=kbuf[:, j, c * P:(c + 1) * P],
                              rhs=vbuf[:, j, c * P:(c + 1) * P], start=False, stop=False,
                              skip_group_check=True)
                    last = pe.matmul(gram[:, c, P:P + 1], lhsT=kbuf[:, j, c * P:(c + 1) * P],
                                     rhs=valid[:, ds(t + 1, 1)], start=False, stop=False,
                                     skip_group_check=True)
                last.then_inc(s_gram, 1)

            pe.matmul(pb[5][:, 0:CC * (P + 1)], lhsT=ones[:, :],
                      rhs=ev.rearrange("p j c -> p (j c)")[:, 0:CC * (P + 1)], start=True, stop=False,
                      skip_group_check=True)
            node_t(0, 0)
            def node_pair(i, last):
                node_t(2 * i + 1, 1)
                node_mm(2 * i, 0)
                node_gram(2 * i - 1, 1)
                if not last:
                    node_t(2 * i + 2, 0)
                node_mm(2 * i + 1, 1)
                node_gram(2 * i, 0)
            def turn(n):
                pe.wait_ge(s_sg, n + 1)
                for half in range(2):
                    for k in range(4):
                        blk = 4 * half + k
                        last = transpose(sortp[half][:, k * P:(k + 1) * P], key_b[:, blk * P:(blk + 1) * P])
                last.then_inc(s_tp, 1)
            with pe.Fori(0, FIRST_TURN) as i:
                node_pair(i, False)
            singles = TURNS - 2 * DOUBLES
            with pe.Fori(0, singles) as n:
                turn(n)
                node_pair(n + FIRST_TURN, False)
            with pe.Fori(0, DOUBLES) as n:
                turn(2 * n + singles)
                node_pair(3 * n + FIRST_TURN + singles, False)
                turn(2 * n + singles + 1)
                node_pair(3 * n + FIRST_TURN + singles + 1, False)
                node_pair(3 * n + FIRST_TURN + singles + 2, False)
            node_pair(NPAIR - 1, True)
            node_gram(NT - 1, 1)

            pe.wait_ge(s_kvbd, 1)
            pe.wait_ge(s_cnt, 1)
            pe.matmul(pb[0][:, 0:1], lhsT=upper[:, :], rhs=small[:, 15, 0:1], start=True, stop=True
                      ).then_inc(s_cross, 1)
            pe.wait_ge(s_dec, 4)
            pe.wait_ge(s_self, TPP)
            for f in range(2):
                for h in range(2):
                    for n in range(2 * TPP):
                        b, part = n // 2, n % 2
                        blk = 2 * b + h
                        last = pe.matmul(pb[1 + 2 * f + h][:, 0:ITEMS],
                                         lhsT=field[2 * f + part][:, blk * P:(blk + 1) * P],
                                         rhs=sel[:, b, :], start=(n == 0), stop=(n == 2 * TPP - 1))
            for n in range(2 * TPP):
                b, part = n // 2, n % 2
                last = pe.matmul(pb[5][:, 0:ITEMS], lhsT=rep[:, part, b, :], rhs=sel[:, b, :],
                                 start=(n == 0), stop=(n == 2 * TPP - 1))
            last.then_inc(s_tab, 1)

            def onehot_transpose(q, g):
                pe.wait_ge(s_oh, q + 1 + GA)
                pe.wait_ge(s_ot, q + GA)
                for n in range(4):
                    last = transpose(psT[:, n * P:(n + 1) * P], onehot[:, 4 * g + n, :])
                last.then_inc(s_otp, 1)

            def src_scores(q, g, bins, beside=None):
                pe.wait_ge(s_ot, q + 1 + GA)
                pe.wait_ge(s_sc, q + GA)
                if beside:
                    beside()
                for n in range(4):
                    last = pe.matmul(score_ps[:, g % 2, n, :], lhsT=onehot_t[:, g % 2, n * P:(n + 1) * P],
                                     rhs=asrc[:, ds(bins[n // 2], HEADS)], start=True, stop=True,
                                     skip_group_check=True)
                last.then_inc(s_al, 1)

            def aggregate(q, g):
                pe.wait_ge(s_msg, q + 1 + GA)
                for m in range(2):
                    pe.wait_ge(s_add, 2 * q + m - 4 + 1 + IA)
                    for h in range(2):
                        s = 4 * g + 2 * m + h
                        last = pe.matmul(psG[2 * (g % 2) + m][:, 0:HROW], lhsT=onehot[:, s, :], rhs=rows[:, s, :],
                                         start=(h == 0), stop=(h == 1))
                    last.then_inc(s_agg, 1)

            def mix_turn(i, normed, free):
                pe.wait_ge(normed, 2 * (i + 1 + MA))
                pe.wait_ge(free, i - 1 + MA)
                for c in range(CC):
                    for u in range(2):
                        last = transpose(mixT[:, c, u * P:(u + 1) * P], xs[:, u, c * P:(c + 1) * P])
                return last

            def mix_columns(w, oc):
                for c in range(CC):
                    last = pe.matmul(mixQ[:, oc, :], lhsT=w[:, c, oc * P:(oc + 1) * P],
                                     rhs=xT[:, c, :], start=(c == 0), stop=(c == CC - 1))
                return last

            def mix_q_products(i):
                pe.wait_ge(m_q, i + 1 + MA)
                pe.wait_ge(m_tz, i + MA)
                for u in range(2):
                    for c in range(CC):
                        pe.matmul(mixY[:, u, c * P:(c + 1) * P], lhsT=qs[:, c, u * P:(u + 1) * P],
                                  rhs=kvbd[:, c, 0:P], start=True, stop=True)

            def mix_q_sums(i):
                for u in range(2):
                    for c in range(CC):
                        last = pe.matmul(den_ps[:, u, c, :], lhsT=qs[:, c, u * P:(u + 1) * P],
                                         rhs=kvbd[:, c, P:P + HEADS], start=True, stop=True,
                                         skip_group_check=True)
                last.then_inc(m_tps, 1)

            def mix_q(i, g, lags):
                if g == 1 and 0 in lags:
                    mix_turn(i, m_xn, m_tz).then_inc(m_tp, 1)
                if g == 2 and 0 in lags:
                    pe.wait_ge(m_xt, i + 1 + MA)
                    pe.wait_ge(m_q, i + MA)
                    mix_columns(w_q, 0)
                    mix_columns(w_q, 1).then_inc(m_qp, 1)
                if g == 3 and 1 in lags:
                    mix_q_products(i - 1)

            def mix_mlp_products(i):
                pe.wait_ge(n_h, 2 * (i + 1 + MA))
                pe.wait_ge(n_y, i + MA)
                for u in range(2):
                    for oc in range(CC):
                        last = pe.matmul(mixY[:, u, :], lhsT=hT[:, oc, u * P:(u + 1) * P],
                                         rhs=w2s[:, oc, :], start=(oc == 0), stop=(oc == CC - 1))
                last.then_inc(n_yp, 1)

            def mix_mlp(i, g, lags):
                if g == 1 and 0 in lags:
                    mix_turn(i, n_xn, n_y).then_inc(n_tp, 1)
                if g == 2 and 0 in lags:
                    pe.wait_ge(n_xt, i + 1 + MA)
                    pe.wait_ge(n_h, 2 * (i + MA))
                    mix_columns(w1g, 0)
                    mix_columns(w1g, 1).then_inc(n_hp, 1)
                if g == 3 and 1 in lags:
                    mix_mlp_products(i - 1)

            asrc_regs = [pe.alloc_register(f"asrc_bin{n}") for n in range(PER_BATCH)]

            def edge_batch(b, mix, i, lags, first=False, last=False):
                pe.load(asrc_regs, bin_asrc[0:1, ds(b * PER_BATCH + 2, PER_BATCH)])
                bins = [pe.snap(r, min_val=0, max_val=(BINS - 1) * HEADS) for r in asrc_regs]
                for g in range(4):
                    q = 4 * b + g
                    if not (last and g == 3):
                        sums = mix is mix_q and g == 0 and 2 in lags
                        src_scores(q + 1, (g + 1) % 4, bins[2 * g:2 * g + 2],
                                   (lambda: mix_q_sums(i - 2)) if sums else None)
                    if not (first and g == 0):
                        aggregate(q - 1, (g - 1) % 4)
                    if not (last and g >= 2):
                        onehot_transpose(q + 2, (g + 2) % 4)
                    if mix:
                        mix(i, g, lags)

            pe.wait_ge(s_items, 1)
            pe.wait_ge(s_as, NT + AHEAD)
            onehot_transpose(0, 0)
            pe.load(asrc_regs[0:2], bin_asrc[0:1, 0:2])
            src_scores(0, 0, [pe.snap(r, min_val=0, max_val=(BINS - 1) * HEADS) for r in asrc_regs[0:2]])
            onehot_transpose(1, 1)
            edge_batches(pe, edge_batch, mix_q, mix_mlp)
            aggregate(4 * NBATCH - 1, 3)

            fT = pb[0][:, :].rearrange("p (c n) -> p c n", c=CC)
            lps = pb[5][:, 0:2 * EXPERTS].rearrange("p (u e) -> p u e", u=2)
            def ff_t(i):
                pe.wait_ge(f_xn, 2 * (i + 1 + XA))
                pe.wait_ge(f_xt, i + XA)
                for c in range(CC):
                    for u in range(2):
                        last = transpose(fT[:, c, u * P:(u + 1) * P], xs[:, u, c * P:(c + 1) * P])
                last.then_inc(f_tp, 1)
            def ff_pair(i, par, last_pair=False):
                fhT_p = fhT[par]
                pe.wait_ge(f_xt, i + 1 + XA)
                for oc in range(FC):
                    pe.wait_ge(f_h, FC * i + oc + 1)
                    for c in range(CC):
                        last = pe.matmul(pb[1 + oc % 4][:, 0:C],
                                         lhsT=fw1_s[:, c, oc * P:(oc + 1) * P], rhs=xT[:, c, :],
                                         start=(c == 0), stop=(c == CC - 1), skip_group_check=True)
                    last.then_inc(f_hp, 1)
                if not last_pair:
                    ff_t(i + 1)
                pe.wait_ge(f_h, FC * i + FC + FA)
                pe.wait_ge(f_lg, i + XA)
                for n in range(4):
                    u, half = n // 2, n % 2
                    pe.wait_ge(f_hr, 4 * i + n + 1)
                    for k in range(4):
                        last = transpose(pb[6 + half][:, k * P:(k + 1) * P],
                                         fhT_p[:, 4 * half + k, u * P:(u + 1) * P])
                    last.then_inc(f_htp, 1)
                    for c in range(4 * half, 4 * half + 4):
                        last = pe.matmul(lps[:, u, :], lhsT=fhT_p[:, c, u * P:(u + 1) * P],
                                         rhs=fwg_s[:, c, :], start=(c == 0), stop=(c == FC - 1))
                last.then_inc(f_lp, 1)
            pe.wait_ge(f_w, 16 * 4)
            ff_t(0)
            with pe.Fori(0, (NPAIR - 3) // 2) as j:
                ff_pair(2 * j, 0)
                ff_pair(2 * j + 1, 1)
            ff_pair(NPAIR - 3, 0)
            ff_pair(NPAIR - 2, 1)
            ff_pair(NPAIR - 1, 0, last_pair=True)

            pe.wait_ge(f_rt, NROUTE)
            ohf = oh_e.rearrange("p e t -> p (e t)")
            pe.matmul(pb[1][:, 0:EXPERTS * NT], lhsT=upper[:, :], rhs=ohf, start=True, stop=True)
            pe.matmul(pb[2][:, 0:EXPERTS * NT], lhsT=ones[:, :], rhs=ohf, start=True, stop=True
                      ).then_inc(r_mm, 1)
            perm = pb[3][:, 0:2 * NSLOT]
            pe.wait_ge(r_st, 1)
            pe.matmul(perm, lhsT=ones[:, :], rhs=zeros_r[:, 0:2 * NSLOT], start=True, stop=False,
                      skip_group_check=True)
            def permute(n, b):
                pe.wait_ge(r_oh, n + 1 + XA)
                for g in range(RG):
                    last = pe.matmul(perm, lhsT=lane_oh[:, b, g, :], rhs=tile_oh[b][:, g].rearrange("p k n -> p (k n)"),
                                     start=False, stop=False, skip_group_check=True)
                last.then_inc(r_acc, 1)
            pe.wait_ge(r_mm, 1)
            with pe.Fori(0, NT // RG // 2) as i:
                permute(2 * i, 0)
                permute(2 * i + 1, 1)

            wd_regs = [pe.alloc_register(f"wd_slot{n}") for n in range(GROWS)]
            def row_t(s, u, i):
                pe.wait_ge(e_g[u], 16 * i + 16)
                pe.wait_ge(e_t, 2 * s + 2)
                for half in range(2):
                    for k in range(4):
                        blk = 4 * half + k
                        last = transpose(pb[2 * (u % 2) + half][:, k * P:(k + 1) * P],
                                         grow[:, u, blk * P:(blk + 1) * P])
                    last.then_inc(e_tp, 1)
            def expert_mm(s, u, off):
                pe.wait_ge(e_t, 2 * s + 2 + 2 * AHEAD)
                pe.wait_ge(e_y, s + 1)
                for c in range(FC):
                    last = pe.matmul(pb[4 + u % 2][:, 0:C], lhsT=gT[:, u % 2, c, :],
                                     rhs=wd_s[:, ds(off + c * C, C)], start=(c == 0), stop=(c == FC - 1))
                last.then_inc(e_yp, 1)
            def expert_tiles(i, last):
                pe.load(wd_regs, slot_wd[0:1, ds(GROWS * i, GROWS)])
                offs = [pe.snap(r, min_val=0, max_val=(EXPERTS - 1) * FC * C) for r in wd_regs]
                for u in range(GROWS):
                    s = GROWS * i + u
                    if u < GROWS - 1:
                        row_t(s + 1, u + 1, i)
                    elif not last:
                        row_t(s + 1, 0, i + 1)
                    expert_mm(s, u, offs[u])
            pe.wait_ge(r_done, 1)
            pe.wait_ge(f_wd, 16 * (EXPERTS + 1))
            row_t(0, 0, 0)
            with pe.Fori(0, NSLOT // GROWS - 1) as i:
                expert_tiles(i, False)
            expert_tiles(NSLOT // GROWS - 1, True)

        @block.scalar
        def _(act):
            ones_start(act, (s_xn, s_xt, s_hc, s_kc), AHEAD)
            ones_start(act, (s_ot, s_ex), GA)
            ones_start(act, (f_h,), FA)
            ones_start(act, (e_t,), 2 * AHEAD)
            ones_start(act, (u_e1, u_e2), XA)
            ones_start(act, (u_n, f_xn), 2 * XA)
            ones_start(act, (m_xt, m_qe, n_xt), MA)
            ones_start(act, (m_xn, m_xi, n_xn, n_h), 2 * MA)
            due_reg[act.engine] = act.alloc_register("due_count")
            for dst_ap, src_ap in WEIGHTS:
                act.dma_start(dst_ap, src_ap).then_inc(s_wgt, 16)

            def root(n):
                act.wait_ge(s_vare, n)
                act.activation(std[:, :], st_s[:, 2, :], ACT.Sqrt).then_inc(s_std, 1)

            def normalise(dst_ap, t, signal):
                act.activation(dst_ap, tile(t), ACT.Identity, bias=nmr[:, ds(t, 1)],
                               scale=rstd[:, ds(t, 1)]).then_inc(signal, 1)

            def tile(t):
                return xall[:, ds(t, 1), :].rearrange("p a c -> p (a c)")

            root(1)
            act.wait_ge(s_rstd, 1)

            def node_norm(t, j):
                act.wait_ge(s_xtp, t + 1)
                normalise(xs[:, j, :], t, s_xn)

            def node_copies(t, j):
                done, two_ago = t + 1 + AHEAD, t + 1
                act.wait_ge(s_xtp, done)
                act.wait_ge(s_kvp, two_ago)
                act.activation(xT[:, :, j * P:(j + 1) * P], trp[j].rearrange("p (c n) -> p c n", c=CC),
                               ACT.Copy).then_inc(s_xt, 1)

            def node_out(t, j):
                done, two_ago = t + 1 + AHEAD, t + 1
                act.wait_ge(s_hp, done)
                act.wait_ge(s_hcl, two_ago)
                act.activation(hbuf[:, j, :], hps[j], ACT.Copy).then_inc(s_hc, 1)
                act.wait_ge(s_kvp, done)
                act.wait_ge(s_kk, two_ago)
                act.activation(kneg[:, j, :], kvps[j][:, 0:C], ACT.Relu, scale=-1.0).then_inc(s_kn, 1)
                act.activation(kpos[:, j, :], kvps[j][:, 0:C], ACT.Relu)
                held(act, s_kn, t + 1)
                act.activation(kexp[:, j, :], kneg[:, j, :], ACT.Exp, scale=-1.0)
                act.wait_ge(s_gram, two_ago)
                act.activation(vbuf[:, j, :], kvps[j][:, C:2 * C], ACT.Copy).then_inc(s_kc, 1)

            node_norm(0, 0)
            node_copies(0, 0)
            node_norm(1, 1)
            def node_pair(i, last):
                node_copies(2 * i + 1, 1)
                if not last:
                    node_norm(2 * i + 2, 0)
                node_out(2 * i, 0)
                if not last:
                    node_copies(2 * i + 2, 0)
                    node_norm(2 * i + 3, 1)
                node_out(2 * i + 1, 1)
            with act.Fori(0, NPAIR - 1) as i:
                node_pair(i, False)
            node_pair(NPAIR - 1, True)
            act.wait_ge(s_gram, NT + 2)
            act.wait_ge(s_const, 1)
            for c in range(CC):
                for h in range(P // MD):
                    rs = slice(h * MD, (h + 1) * MD)
                    act.activation(kvbd[rs, c, h * MD:(h + 1) * MD], gram[rs, c, h * MD:(h + 1) * MD], ACT.Copy)
                    last = act.activation(kvbd[rs, c, P + h:P + h + 1], gram[rs, c, P:P + 1], ACT.Copy)
            last.then_inc(s_kvbd, 1)

            def copy_onehot(q, g):
                act.wait_ge(s_otp, q + 1 + GA)
                act.wait_ge(s_al, q - 2 + 1 + GA)
                act.activation(onehot_t[:, g % 2, :], psT[:, :], ACT.Copy).then_inc(s_ot, 1)

            def mix_q(i, g, lags):
                if g == 0 and 0 in lags:
                    act.wait_ge(m_tp, i + MA)
                    for u in range(2):
                        normalise(xs[:, u, :], 2 * i + u, m_xn)
                    held(act, m_xn, 2 * (i + 1 + MA))
                    for u in range(2):
                        normalise(tile(2 * i + u), 2 * i + u, m_xi)
                if g == 2 and 0 in lags:
                    act.wait_ge(m_tp, i + 1 + MA)
                    act.activation(xT[:, :, :], mixT[:, :, :], ACT.Copy).then_inc(m_xt, 1)
                if g == 3 and 0 in lags:
                    act.wait_ge(m_qp, i + 1 + MA)
                    act.wait_ge(m_qm, i + MA)
                    act.activation(ev.rearrange("p j c -> p (j c)"), pb[5][:, :], ACT.Exp).then_inc(m_qe, 1)

            def mix_gelu(i):
                act.wait_ge(n_hp, i + 1 + MA)
                act.wait_ge(n_yp, i + MA)
                for oc in range(CC):
                    act.activation(hT[:, oc, :], mixQ[:, oc, :], ACT.Gelu,
                                   bias=b1eff[:, oc:oc + 1]).then_inc(n_h, 1)

            def mix_mlp(i, g, lags):
                if g == 0 and 0 in lags:
                    act.wait_ge(n_g, i + MA)
                    for u in range(2):
                        normalise(xs[:, u, :], 2 * i + u, n_xn)
                if g == 0 and 1 in lags:
                    mix_gelu(i - 1)
                if g == 2 and 0 in lags:
                    act.wait_ge(n_tp, i + 1 + MA)
                    act.activation(xT[:, :, :], mixT[:, :, :], ACT.Copy).then_inc(n_xt, 1)

            def edge_batch(b, mix, i, lags, first=False, last=False):
                for g in range(4):
                    q = 4 * b + g
                    act.wait_ge(s_lk, q + 1 + GA)
                    act.wait_ge(s_eg, q - 2 + 1 + GA)
                    act.activation(expd[:, g % 2], leaky[:, g % 2], ACT.Exp, scale=-1.0).then_inc(s_ex, 1)
                    if mix:
                        mix(i, g, lags)
                    if not (last and g >= 2):
                        copy_onehot(q + 2, (g + 2) % 4)

            def after(n):
                root(n + 2)
                act.wait_ge(s_rstd, n + 2)

            act.wait_ge(s_items, 1)
            act.activation(acc[:, ACC_ACT:].rearrange("p (r c) -> p r c", c=P),
                           ones[:, None, :].to_broadcast([P, (ACC - ACC_ACT) // P, P]), ACT.Copy, scale=0.0
                           ).then_inc(s_acc0, 1)
            copy_onehot(0, 0)
            copy_onehot(1, 1)
            edge_batches(act, edge_batch, mix_q, mix_mlp, after)

            def mixer_norm(k):
                act.wait_ge(u_p, 3 * (k + XA) - 2)
                for u in range(2):
                    normalise(n2[:, u, :], 2 * k + u, u_n)

            def elu_exps(k):
                act.wait_ge(u_ng, k + 1 + XA)
                act.wait_ge(u_e2, k + XA)
                act.activation(ge1, gneg, ACT.Exp).then_inc(u_e1, 1)
                act.wait_ge(u_e1, k + 1 + XA)
                act.wait_ge(u_g, k + XA)
                act.activation(ge2, ge1, ACT.Exp, bias=minus1[:, :]).then_inc(u_e2, 1)

            def x2_normalise(k):
                held(act, f_tp, k + XA)
                held(act, u_c, NNORM * (k + 1 + XA))
                for u in range(2):
                    act.activation(xs[:, u, :], tile(2 * k + u), ACT.Identity, bias=norm4[:, 9, u:u + 1],
                                   scale=norm4[:, 7, u:u + 1]).then_inc(f_xn, 1)

            def ff_pair(i, par, last_pair=False, ahead=True):
                fhT_p = fhT[par]
                if not last_pair:
                    x2_normalise(i + 1)
                if ahead:
                    mixer_norm(i + 3)
                act.wait_ge(f_lp, i - 1 + XA)
                for oc in range(FC):
                    act.wait_ge(f_hp, FC * i + oc + 1)
                    act.activation(fhT_p[:, oc, :], pb[1 + oc % 4][:, 0:C],
                                   ACT.Gelu, bias=fb1_s[:, oc:oc + 1]).then_inc(f_h, 1)
                if ahead:
                    elu_exps(i + 3)
            act.wait_ge(s_add, ITEMS + IA)
            mixer_norm(0)
            elu_exps(0)
            mixer_norm(1)
            elu_exps(1)
            x2_normalise(0)
            mixer_norm(2)
            elu_exps(2)
            act.wait_ge(f_w, 16 * 4)
            def load_expert(e):
                act.dma_start(wd_s[:, e * FC * C:(e + 1) * FC * C].rearrange("p (c n) -> p c n", c=FC),
                              fwd[e].rearrange("(c p) n -> p c n", p=P)).then_inc(f_wd, 16)
            start, loaded = 0, 0
            for end in (1, 3, 5, 7, 9, (NPAIR - 3) // 2):
                with act.Fori(start, end) as j:
                    ff_pair(2 * j, 0)
                    ff_pair(2 * j + 1, 1)
                start = end
                last_pair_there = ((loaded + 1) * FC * C - 1) // HROW // 2
                assert last_pair_there <= 2 * end + 2
                act.wait_ge(u_hp, last_pair_there + 1 + XA)
                load_expert(loaded)
                loaded += 1
            ff_pair(NPAIR - 3, 0, ahead=False)
            act.wait_ge(u_x2, NPAIR + XA)
            for e in range(loaded, EXPERTS):
                load_expert(e)
            ff_pair(NPAIR - 2, 1, ahead=False)
            act.wait_ge(f_xn, 2 * (NPAIR + XA))
            act.dma_start(bd_s, fbd).then_inc(f_wd, 16)
            ff_pair(NPAIR - 1, 0, last_pair=True, ahead=False)
            act.wait_ge(f_rt, 2)
            act.activation(lex, lix, ACT.Exp).then_inc(f_le, 1)

            act.wait_ge(r_done, 1)
            def expert_copies(s, u):
                act.wait_ge(e_yp, s + 1)
                for half in range(2):
                    act.wait_ge(e_tp, 2 * s + half + 1)
                    act.activation(gT[:, u, 4 * half:4 * half + 4, :],
                                   pb[2 * u + half][:, :].rearrange("p (k n) -> p k n", k=4),
                                   ACT.Copy).then_inc(e_t, 1)
            with act.Fori(0, NSLOT // GROWS) as i:
                for u in range(GROWS):
                    expert_copies(GROWS * i + u, u % 2)

        @block.vector
        def _(dve):
            due_reg[dve.engine] = dve.alloc_register("due_count")
            ones_start(dve, (s_oh, s_sc, s_lk, s_eg, s_msg), GA)
            ones_start(dve, (s_add,), IA)
            ones_start(dve, (f_hr, e_y), AHEAD)
            ones_start(dve, (m_qm, m_q, m_tz, m_r, n_g, n_c, n_y), MA)
            ones_start(dve, (m_z,), 2 * MA)
            ones_start(dve, (u_hp, u_ng, u_g, u_x2, f_xt, f_lg, r_oh), XA)
            ones_start(dve, (u_rs, u_bs), 2 * XA)

            def tile(t):
                return xall[:, ds(t, 1), :].rearrange("p a c -> p (a c)")

            def stats(t, signal):
                dve.bn_stats(stat[:, ds(t, 1), :].rearrange("p a c -> p (a c)"), tile(t)).then_inc(signal, 1)

            def finish_stats(n):
                k = 6 * (n - 1)
                mean_e, dev_e, mean_o, dev_o = (stat[:, :, c] for c in (1, 2, 4, 5))
                dve.tensor_tensor(st_s[:, 0, :], mean_e, mean_o, op=ALU.add).then_inc(s_ns, 1)
                dve.tensor_tensor(st_s[:, 1, :], mean_e, mean_o, op=ALU.subtract).then_inc(s_ns, 1)
                dve.tensor_tensor(st_s[:, 3, :], dev_e, dev_o, op=ALU.add).then_inc(s_ns, 1)
                dve.wait_ge(s_ns, k + 2)
                dve.tensor_tensor(st_s[:, 2, :], st_s[:, 1, :], st_s[:, 1, :], op=ALU.mult).then_inc(s_ns, 1)
                dve.wait_ge(s_ns, k + 4)
                dve.tensor_scalar(st_s[:, 1, :], st_s[:, 2, :], 0.25, EPS, op0=ALU.mult, op1=ALU.add
                                  ).then_inc(s_ns, 1)
                dve.wait_ge(s_ns, k + 5)
                dve.scalar_tensor_tensor(st_s[:, 2, :], st_s[:, 3, :], 1.0 / C, st_s[:, 1, :],
                                         op0=ALU.mult, op1=ALU.add).then_inc(s_vare, 1)
                dve.wait_ge(s_std, n)
                dve.reciprocal(rstd[:, :], std[:, :]).then_inc(s_ns, 1)
                dve.wait_ge(s_ns, k + 6)
                dve.scalar_tensor_tensor(nmr[:, :], st_s[:, 0, :], -0.5, rstd[:, :],
                                         op0=ALU.mult, op1=ALU.mult).then_inc(s_rstd, 1)

            dve.wait_ge(s_keys, 32)
            dve.wait_ge(s_const, 1)
            ka, kb = key_a.bitcast(I32), key_b.bitcast(I32)
            for b in range(7):
                dve.tensor_scalar(bit_i[:, b:b + 1], part_i[:, b:b + 1], b, 1,
                                  op0=ALU.logical_shift_right, op1=ALU.bitwise_and)
            dve.tensor_scalar(ka, ka, FIELD, KEY_ONE, op0=ALU.logical_shift_left, op1=ALU.bitwise_or
                              ).then_inc(s_key, 1)
            dve.wait_ge(s_key, 1)
            dve.tensor_scalar(sign[:, 0:7], bit_i[:, 0:7], -2.0, 1.0, op0=ALU.mult, op1=ALU.add)
            dve.tensor_tensor(ka, ka, kb, op=ALU.bitwise_or).then_inc(s_key, 1)
            dve.wait_ge(s_key, 2)

            count = [0, 0]
            cur, last_bit = 0, None

            def halves(buf, j, sbit, v):
                hi, lo = max(j, sbit), min(j, sbit)
                view = buf.rearrange("p (a f b g d) -> p a f b g d", f=2, b=1 << (hi - lo - 1), g=2, d=1 << lo)
                if j > sbit:
                    return view[:, :, 0, :, v, :], view[:, :, 1, :, v, :]
                return view[:, :, v, :, 0, :], view[:, :, v, :, 1, :]

            def stage(j, sbit, falling):
                nonlocal cur, last_bit
                before = list(count)
                for v in range(2):
                    for w in (range(2) if sbit != last_bit else [v]):
                        if before[w]:
                            dve.wait_ge(s_st[w], before[w])
                    lo, hi = halves(keys[cur], j, sbit, v)
                    to_lo, to_hi = halves(keys[1 - cur], j, sbit, v)
                    down = falling and v == 1
                    dve.tensor_tensor(to_lo, lo, hi, op=ALU.max if down else ALU.min).then_inc(s_st[v], 1)
                    dve.tensor_tensor(to_hi, lo, hi, op=ALU.min if down else ALU.max).then_inc(s_st[v], 1)
                    count[v] += 2
                cur, last_bit = 1 - cur, sbit

            def both_done():
                nonlocal last_bit
                dve.wait_ge(s_st[0], count[0])
                dve.wait_ge(s_st[1], count[1])
                last_bit = None

            def lane_stages():
                for j in range(6, -1, -1):
                    stage(j, LOG_SC - 1, False)

            signed = [0]
            def sign_all(level, signal, n):
                both_done()
                dve.tensor_scalar(keys[cur], keys[cur], sign[:, level - LOG_SC:level - LOG_SC + 1], None,
                                  op0=ALU.mult).then_inc(signal, 1)
                dve.wait_ge(signal, n)

            def turn(n, level):
                nonlocal cur
                cur = (1 + turn_stages[n]) % 2
                dve.wait_ge(s_tp, n + 1)
                for half in range(2):
                    to = keys[cur][:, half * (SC // 2):(half + 1) * (SC // 2)]
                    if n % 2 and level < LOG_SLOTS:
                        ins = dve.tensor_scalar(to, sortp[half][:, :], sign[:, level - LOG_SC:level - LOG_SC + 1],
                                                None, op0=ALU.mult)
                    else:
                        ins = dve.tensor_copy(to, sortp[half][:, :])
                ins.then_inc(s_te, 1)
                dve.wait_ge(s_te, n + 1)

            for level in range(1, EARLY_LEVELS + 1):
                for j in range(level - 1, -1, -1):
                    stage(j, level, True)

            for t in range(NT):
                dve.wait_ge(s_x[t // (NT // 5)], 16)
                stats(t, s_stat)
            dve.wait_ge(s_stat, NT)
            finish_stats(1)

            dve.wait_ge(s_fold, 1)
            dve.tensor_copy(w_gat[:, :, C:HCOL].rearrange("p c (k h) -> p c h k", k=2),
                            pb[7][:, 0:16].rearrange("p (c h k) -> p c h k", c=CC, k=2)).then_inc(s_foldc, 1)
            dve.wait_ge(s_fold, 2)
            dve.tensor_tensor(b1eff[:, :], pb[7][:, 64:66], b1col[:, :], op=ALU.add)
            for c in range(CC):
                dve.tensor_scalar(w1g[:, c, :], w1g[:, c, :], g1col[:, c:c + 1], None, op0=ALU.mult)
            dve.tensor_tensor(c1rep[:, :], c1rep[:, :], b2rep[:, :], op=ALU.add)
            dve.tensor_scalar(c2rep[:, :], c2rep[:, :], -1.0, None, op0=ALU.add).then_inc(s_prep, 1)

            for level in range(EARLY_LEVELS + 1, LOG_SC):
                for j in range(level - 1, -1, -1):
                    stage(j, level, True)
            sign_all(LOG_SC, s_key, 3)
            stage(9, 8, False)
            for j in range(8, -1, -1):
                stage(j, LOG_SC - 1, False)
            sign_all(LOG_SC, s_sg, 1)
            n = 0
            for level in range(LOG_SC + 1, LOG_SLOTS + 1):
                turn(n, level)
                n += 1
                if level < LOG_SLOTS:
                    for bit in range(level - 1, 6, -1):
                        stage(bit - LOG_SC if bit >= LOG_SC else bit, level - LOG_SC, True)
                else:
                    for j in range(6, -1, -1):
                        stage(j, 9, False)
                    stage(9, 8, False)
                    stage(8, 9, False)
                    stage(7, 9, False)
                both_done()
                dve.sem_inc(s_sg, 1)
                turn(n, level)
                n += 1
                lane_stages()
                if level < LOG_SLOTS:
                    sign_all(level, s_sg, n + 1)
            both_done()

            sk = sorted_keys.bitcast(I32)
            SCALES = [(20, 63, 128.0), (13, 127, 1.0), (7, 63, 128.0), (0, 127, 1.0)]
            for f, (shift, mask, scale) in enumerate(SCALES):
                if f >= 2:
                    dve.wait_ge(s_dec, f - 1)
                    dve.wait_ge(s_tabs, f + 1)
                dve.tensor_scalar(fint[f % 2], sk, shift, mask, op0=ALU.logical_shift_right,
                                  op1=ALU.bitwise_and).then_inc(s_tabs, 1)
                dve.wait_ge(s_tabs, f + 1 + (f > 0))
                dve.tensor_scalar(field[f], fint[f % 2], scale, None, op0=ALU.mult).then_inc(s_dec, 1)
                if f == 0:
                    bins = fint[0].rearrange("p (b e) -> p b e", b=TPP)
                    dve.tensor_copy(small[:, 0, :], bins[:, :, 0])
                    dve.tensor_scalar(small[:, 1, :], bins[:, :, PAIR - 1], float(BINS - 1), None, op0=ALU.min
                                      ).then_inc(s_tabs, 1)
            dve.wait_ge(s_dec, 4)
            chain = [5]

            def step(ins):
                chain[0] += 1
                ins.then_inc(s_tabs, 1)
                dve.wait_ge(s_tabs, chain[0])

            step(dve.scalar_tensor_tensor(small[:, 2, :], small[:, 1, :], 1.0, small[:, 0, :],
                                          op0=ALU.add, op1=ALU.subtract))
            step(dve.tensor_scalar(small[:, 3, :], small[:, 2, :], 0.0, None, op0=ALU.max))
            step(dve.memset(small[:, 4, :], 0.0))
            step(dve.tensor_tensor_scan(small[:, 5, :], small[:, 3, :], small[:, 4, :], 0.0,
                                        op0=ALU.add, op1=ALU.add))
            dve.tensor_copy(small[:, 15, 0:1], small[:, 5, TPP - 1:TPP]).then_inc(s_cnt, 1)
            dve.wait_ge(s_cross, 1)
            step(dve.tensor_scalar(small[:, 6, :], small[:, 5, :], pb[0][:, 0:1], None, op0=ALU.add))
            step(dve.tensor_tensor(small[:, 7, :], small[:, 6, :], small[:, 3, :], op=ALU.subtract))
            step(dve.tensor_tensor(small[:, 8, :], small[:, 0, :], small[:, 7, :], op=ALU.subtract))
            step(dve.tensor_scalar(smalli[:, 0, :], small[:, 8, :], 0.125, None, op0=ALU.mult))
            step(dve.tensor_scalar(small[:, 9, :], smalli[:, 0, :], 8.0, None, op0=ALU.mult))
            step(dve.tensor_tensor(small[:, 10, :], small[:, 8, :], small[:, 9, :], op=ALU.subtract))
            dve.tensor_copy(rep[:, 0], small[:, 9, :, None].to_broadcast([P, TPP, P]))
            dve.tensor_copy(rep[:, 1], small[:, 10, :, None].to_broadcast([P, TPP, P]))
            for b in range(TPP):
                if b >= 2:
                    dve.wait_ge(s_self, b - 1)
                step(dve.tensor_scalar(selg[:, b % 2, :], iota_k[:, :], small[:, 7, b:b + 1], None, op0=ALU.is_ge))
                dve.scalar_tensor_tensor(sel[:, b, :], iota_k[:, :], small[:, 6, b:b + 1], selg[:, b % 2, :],
                                         op0=ALU.is_lt, op1=ALU.mult).then_inc(s_self, 1)

            dve.memset(dst_tab[:, 2 * ITEMS:], 0)
            dve.memset(srcrel[:, 2 * ITEMS:], -1.0)
            dve.memset(bin_acc[:, :], 0)
            step(dve.memset(bin_asrc[:, :], 0))
            dve.wait_ge(s_tab, 1)
            step(dve.tensor_tensor(binf, pb[5][:, 0:ITEMS], iota_k[:, :], op=ALU.add))
            for h in range(2):
                dve.scalar_tensor_tensor(srcrel[:, 0:2 * ITEMS].rearrange("p (k h) -> p k h", h=2)[:, :, h],
                                         binf, -float(P), pb[1 + h][:, 0:ITEMS], op0=ALU.mult, op1=ALU.add)
                dve.tensor_scalar(dst_tab[:, 0:2 * ITEMS].rearrange("p (k h) -> p k h", h=2)[:, :, h],
                                  pb[3 + h][:, 0:ITEMS], float(N_NODES - 1), None, op0=ALU.min)
            step(dve.tensor_scalar(binc, binf, float(BINS - 1), None, op0=ALU.min))
            dve.tensor_scalar(bin_acc[0:1, 4:4 + ITEMS], binc[0:1, :], float(HROW), None, op0=ALU.mult)
            dve.tensor_scalar(bin_asrc[0:1, 0:ITEMS], binc[0:1, :], float(HEADS), None, op0=ALU.mult
                              ).then_inc(s_items, 1)
            dve.wait_ge(s_items, 1)
            dve.wait_ge(s_hw[0], 16 * NPAIR + 16)
            dve.wait_ge(s_hw[1], 16 * NPAIR + 16)
            dve.wait_ge(s_kvbd, 1)
            for g in range(4):
                dve.tensor_copy(idx_buf[:, 4 * g:4 * g + 4], dst_tab[:, 4 * g:4 * g + 4]).then_inc(s_idx, 1)
            dve.wait_ge(s_as, NT + AHEAD)
            dve.memset(acc[:, ACC_FREE:ACC_ACT], 0.0).then_inc(s_acc0, 1)
            dve.wait_ge(s_acc0, 3)

            def onehots(q, g):
                dve.wait_ge(s_agg, 2 * q - 8 + 2 + IA)
                dve.tensor_tensor(onehot[:, 4 * g:4 * g + 4, :],
                                  iota_p[:, None, :].to_broadcast([P, 4, P]),
                                  srcrel[:, ds(4 * q, 4)][:, :, None].to_broadcast([P, 4, P]),
                                  op=ALU.is_equal).then_inc(s_oh, 1)

            def add_item(k, bank, off):
                dve.wait_ge(s_agg, k + 1 + IA)
                dve.wait_ge(s_add, k + IA)
                mine = acc[:, ds(off, HROW)]
                dve.tensor_tensor(mine, psG[bank][:, 0:HROW], mine, op=ALU.add).then_inc(s_add, 1)

            def group_scores(q, g, b):
                slots = rows[:, 4 * g:4 * g + 4, :]
                dve.wait_ge(s_al, q + 1 + GA)
                dve.wait_ge(s_gat[g], 64 * b + 64)
                dve.wait_ge(s_lk, q - 2 + 1 + GA)
                dve.tensor_tensor(score[:, g % 2], score_ps[:, g % 2], slots[:, :, C:HROW], op=ALU.add
                                  ).then_inc(s_sc, 1)

            def group_leaky(q, g):
                dve.wait_ge(s_sc, q + 1 + GA)
                dve.wait_ge(s_ex, q - 2 + 1 + GA)
                dve.scalar_tensor_tensor(leaky[:, g % 2], score[:, g % 2], 0.2, score[:, g % 2],
                                         op0=ALU.mult, op1=ALU.max).then_inc(s_lk, 1)

            def group_guard(q, g):
                dve.wait_ge(s_ex, q + 1 + GA)
                dve.tensor_scalar(rows[:, 4 * g:4 * g + 4, C:HROW], expd[:, g % 2], 0.0, None, op0=ALU.max
                                  ).then_inc(s_eg, 1)

            def group_messages(q, g):
                slots = rows[:, 4 * g:4 * g + 4, :]
                h = slots[:, :, 0:C].rearrange("p s (k d) -> p s k d", k=HEADS)
                dve.wait_ge(s_eg, q + 1 + GA)
                dve.tensor_tensor(h, h, slots[:, :, C:HROW][:, :, :, None].to_broadcast([P, 4, HEADS, HID]),
                                  op=ALU.mult).then_inc(s_msg, 1)

            def mix_q_kernel(i):
                dve.wait_ge(m_qe, i + 1 + MA)
                dve.wait_ge(m_q, i + MA)
                dve.tensor_scalar(em[:, :, :], ev[:, :, :], 1.0, None, op0=ALU.min).then_inc(m_qm, 1)
                dve.wait_ge(m_qm, i + 1 + MA)
                dve.wait_ge(m_tps, i + MA)
                dve.scalar_tensor_tensor(qs.rearrange("p c n -> p (c n)"), pb[5][:, :], 0.0,
                                         em.rearrange("p j c -> p (j c)"), op0=ALU.max, op1=ALU.add
                                         ).then_inc(m_q, 1)

            def mix_q_divide(i):
                dve.wait_ge(m_tps, i + 1 + MA)
                dve.wait_ge(m_z, 2 * (i + MA))
                dve.tensor_scalar(zden, psA[:, 32:32 + 2 * MH], EPS_ATTN, None, op0=ALU.add).then_inc(m_z, 1)
                dve.wait_ge(m_z, 2 * (i + MA) + 1)
                dve.wait_ge(m_tz, i + MA)
                dve.reciprocal(zrec, zden).then_inc(m_z, 1)
                dve.wait_ge(m_z, 2 * (i + MA) + 2)
                dve.wait_ge(m_r, i + MA)
                dve.tensor_tensor(tz.rearrange("p (z d) -> p z d", d=MD),
                                  pb[4][:, :].rearrange("p (z d) -> p z d", d=MD),
                                  zrec[:, :, None].to_broadcast([P, 2 * MH, MD]), op=ALU.mult).then_inc(m_tz, 1)

            def mix_q_residual(i):
                dve.wait_ge(m_xi, 2 * (i + 1 + MA))
                dve.wait_ge(m_tz, i + 1 + MA)
                pair = xall[:, ds(2 * i, 2), :]
                dve.tensor_tensor(pair, two(tz), pair, op=ALU.add).then_inc(m_r, 1)
                dve.wait_ge(m_r, i + 1 + MA)
                for u in range(2):
                    stats(2 * i + u, m_bs)

            def mix_q(i, g, lags):
                if g == 0 and 2 in lags:
                    mix_q_divide(i - 2)
                if g == 1 and 1 in lags:
                    mix_q_kernel(i - 1)
                if g == 2 and 2 in lags:
                    mix_q_residual(i - 2)

            def mix_mlp_gain(i):
                dve.wait_ge(n_xn, 2 * (i + 1 + MA))
                dve.wait_ge(n_c, i + MA)
                dve.tensor_tensor(ev[:, :, :], xs[:, :, :], g1rep[:, None, :].to_broadcast([P, 2, C]),
                                  op=ALU.mult).then_inc(n_g, 1)

            def mix_mlp_shift(i):
                dve.wait_ge(n_g, i + 1 + MA)
                dve.wait_ge(n_y, i + MA)
                dve.tensor_tensor(em[:, :, :], ev[:, :, :], c1rep[:, None, :].to_broadcast([P, 2, C]),
                                  op=ALU.add).then_inc(n_c, 1)

            def mix_mlp_residual(i):
                dve.wait_ge(n_yp, i + 1 + MA)
                dve.wait_ge(n_c, i + 1 + MA)
                dve.tensor_tensor(xall[:, ds(2 * i, 2), :], mixY[:, :, :], em[:, :, :], op=ALU.add
                                  ).then_inc(n_y, 1)

            def mix_mlp_stats(i):
                dve.wait_ge(n_y, i + 1 + MA)
                for u in range(2):
                    stats(2 * i + u, n_bs)

            def mix_mlp(i, g, lags):
                if g == 0 and 2 in lags:
                    mix_mlp_residual(i - 2)
                if g == 1:
                    if 2 in lags:
                        mix_mlp_stats(i - 2)
                    if 1 in lags:
                        mix_mlp_shift(i - 1)
                if g == 2 and 0 in lags:
                    mix_mlp_gain(i)

            acc_regs = [dve.alloc_register(f"acc_bin{n}") for n in range(PER_BATCH)]

            def edge_batch(b, mix, i, lags, first=False, last=False):
                dve.load(acc_regs, bin_acc[0:1, ds(b * PER_BATCH, PER_BATCH)])
                offs = [dve.snap(r, min_val=0, max_val=(BINS - 1) * HROW) for r in acc_regs]
                for g in range(4):
                    q = 4 * b + g
                    group_scores(q, g, b)
                    if not last:
                        dve.wait_ge(s_const, 1)
                        dve.tensor_copy(idx_buf[:, 4 * g:4 * g + 4], dst_tab[:, ds(4 * q + 16, 4)]
                                        ).then_inc(s_idx, 1)
                    if not (first and g == 0):
                        group_guard(q - 1, (g - 1) % 4)
                    group_leaky(q, g)
                    if not (first and g == 0):
                        group_messages(q - 1, (g - 1) % 4)
                    bank = 2 * (g % 2)
                    if not (first and g < 2):
                        add_item(2 * q - 4, bank, offs[2 * g])
                    if not (last and g >= 2):
                        onehots(q + 2, (g + 2) % 4)
                    if not (first and g < 2):
                        add_item(2 * q - 3, bank + 1, offs[2 * g + 1])
                    if mix is mix_q and g == 0 and 2 in lags:
                        dve.wait_ge(s_al, q + 2 + GA)
                    if mix:
                        mix(i, g, lags)

            def after(n):
                dve.wait_ge((m_bs, n_bs)[n], NT)
                finish_stats(n + 2)

            onehots(0, 0)
            onehots(1, 1)
            edge_batches(dve, edge_batch, mix_q, mix_mlp, after)
            group_guard(4 * NBATCH - 1, 3)
            group_messages(4 * NBATCH - 1, 3)
            dve.load(acc_regs[0:4], bin_acc[0:1, ITEMS:ITEMS + 4])
            for m in range(4):
                add_item(ITEMS - 4 + m, m, dve.snap(acc_regs[m], min_val=0, max_val=(BINS - 1) * HROW))
            dve.wait_ge(s_add, ITEMS + IA)

            def x2_sums(k):
                sums = acc_t[:, ds(2 * k, 2), :]
                dve.tensor_scalar(rsum, sums[:, :, C:HROW], TINY, None, op0=ALU.max).then_inc(u_rs, 1)
                dve.wait_ge(u_rs, 2 * (k + XA) + 1)
                dve.reciprocal(rrec, rsum.rearrange("p j c -> p (j c)")).then_inc(u_rs, 1)
                dve.wait_ge(u_rs, 2 * (k + XA) + 2)
                dve.wait_ge(u_g, k + XA)
                dve.tensor_tensor(hpn.rearrange("p (j h d) -> p j h d", j=2, h=HEADS),
                                  sums[:, :, 0:C].rearrange("p j (h d) -> p j h d", h=HEADS),
                                  rrec.rearrange("p (j h) -> p j h", j=2)[:, :, :, None]
                                  .to_broadcast([P, 2, HEADS, HID]), op=ALU.mult).then_inc(u_hp, 1)
                dve.wait_ge(u_hp, k + 1 + XA)
                dve.wait_ge(u_e1, k + XA)
                dve.tensor_scalar(gneg, hpn, 0.0, None, op0=ALU.min).then_inc(u_ng, 1)

            def x2_add(k):
                dve.wait_ge(u_e2, k + 1 + XA)
                dve.wait_ge(u_x2, k + XA)
                dve.scalar_tensor_tensor(gout, hpn, 0.0, ge2, op0=ALU.max, op1=ALU.add).then_inc(u_g, 1)
                dve.wait_ge(u_g, k + 1 + XA)
                dve.wait_ge(u_p, 3 * (k + 1 + XA))
                dve.tensor_tensor(xall[:, ds(2 * k, 2), :], two(gout), n2x, op=ALU.add).then_inc(u_x2, 1)
                dve.wait_ge(u_x2, k + 1 + XA)
                held(dve, u_c, NNORM * (k + XA))
                for u in range(2):
                    dve.bn_stats(st4[:, u, :], tile(2 * k + u)).then_inc(u_bs, 1)

            def ff_copy(k, first=False):
                dve.wait_ge(f_tp, k + 1 + XA)
                if not first:
                    dve.wait_ge(f_hp, FC * k)
                dve.tensor_copy(xT.rearrange("p c n -> p (c n)"), pb[0][:, :]).then_inc(f_xt, 1)

            def ff_pair(i, last_pair=False, x2_ahead=2):
                if x2_ahead >= 1:
                    x2_add(i + 2)
                if x2_ahead >= 2:
                    x2_sums(i + 3)
                if not last_pair:
                    ff_copy(i + 1)
                for n in range(4):
                    u, half = n // 2, n % 2
                    if half == 0:
                        dve.wait_ge(f_st[u], 16 * (i + 1))
                    dve.wait_ge(f_htp, 4 * (i + XA) + n + 1)
                    dve.tensor_copy(frow[:, u, half * 512:(half + 1) * 512], pb[6 + half][:, :]
                                    ).then_inc(f_hr, 1)
                dve.wait_ge(f_lp, i + 1 + XA)
                dve.tensor_tensor(lg.rearrange("p e t -> p t e")[:, ds(2 * i, 2), :],
                                  pb[5][:, 0:2 * EXPERTS].rearrange("p (u e) -> p u e", u=2),
                                  fbg_s[:, None, :].to_broadcast([P, 2, EXPERTS]), op=ALU.add).then_inc(f_lg, 1)
            dve.wait_ge(f_c, 1)
            x2_sums(0)
            x2_add(0)
            x2_sums(1)
            dve.wait_ge(f_w, 16 * 4)
            ff_copy(0, first=True)
            x2_add(1)
            x2_sums(2)
            with dve.Fori(0, NPAIR - 3) as i:
                ff_pair(i)
            ff_pair(NPAIR - 3, x2_ahead=1)
            ff_pair(NPAIR - 2, x2_ahead=0)
            ff_pair(NPAIR - 1, last_pair=True, x2_ahead=0)

            routed = [0]

            def step(ins):
                routed[0] += 1
                ins.then_inc(f_rt, 1)
                dve.wait_ge(f_rt, routed[0])

            def over_experts(v):
                return v[:, None, :].to_broadcast([P, EXPERTS, NT])

            def by_tile(v):
                return v.rearrange("p e t -> p t e")
            dve.wait_ge(f_lg, NPAIR + XA)
            step(dve.tensor_reduce(lmax, by_tile(lg), axis=AX_X, op=ALU.max))
            step(dve.tensor_tensor(lix, lg, over_experts(lmax), op=ALU.subtract))
            dve.wait_ge(f_le, 1)
            step(dve.tensor_reduce(lsum, by_tile(lex), axis=AX_X, op=ALU.add))
            step(dve.reciprocal(lmax, lsum))
            step(dve.tensor_tensor(lg, lex, over_experts(lmax), op=ALU.mult))
            step(dve.tensor_reduce(ptop, by_tile(lg), axis=AX_X, op=ALU.max))
            step(dve.tensor_tensor(lex, lg, over_experts(ptop), op=ALU.is_equal))
            step(dve.tensor_tensor(lix, lex, iota_e8[:, :, None].to_broadcast([P, EXPERTS, NT]), op=ALU.mult))
            step(dve.tensor_reduce(lidx, by_tile(lix), axis=AX_X, op=ALU.min))
            step(dve.tensor_tensor(lex, iota_e8[:, :, None].to_broadcast([P, EXPERTS, NT]), over_experts(lidx),
                                   op=ALU.is_equal))
            dve.tensor_tensor(ptop, ptop, valid[:, 1:NT + 1], op=ALU.mult)
            dve.tensor_tensor(tok1, tok1, valid[:, 1:NT + 1], op=ALU.mult)
            step(dve.tensor_tensor(oh_e, lex, over_experts(valid[:, 1:NT + 1]), op=ALU.mult))
            assert routed[0] == NROUTE

            tables = [0]

            def rstep(ins):
                tables[0] += 1
                ins.then_inc(r_st, 1)
                dve.wait_ge(r_st, tables[0])
            dve.wait_ge(f_hr, 4 * NPAIR + AHEAD)
            rstep(dve.memset(zeros_r[:, :], 0.0))
            dve.wait_ge(r_mm, 1)
            pre, tot = head(pb[1][:, 0:EXPERTS * NT]), head(pb[2][:, 0:EXPERTS * NT])
            for e in range(EXPERTS):
                ins = dve.tensor_tensor_scan(rk_base[:, e, :], tot[:, e, :], zeros_r[:, 0:NT], 0.0,
                                             op0=ALU.add, op1=ALU.add)
            rstep(ins)
            rstep(dve.tensor_tensor(rk_all, rk_base, tot, op=ALU.subtract))
            rstep(dve.tensor_tensor(rk_all, rk_all, pre, op=ALU.add))
            rstep(dve.tensor_scalar(rti[:, 0, :], rk_base[:, :, NT - 1], float(P - 1), None, op0=ALU.add))
            rstep(dve.tensor_scalar(rti[:, 1, :], rti[:, 0, :], 7, None, op0=ALU.logical_shift_right))
            rstep(dve.tensor_copy(rt[:, 0, :], rti[:, 1, :]))
            rstep(dve.tensor_tensor_scan(rt[:, 1, :], rt[:, 0, :], zeros_r[:, 0:EXPERTS], 0.0,
                                         op0=ALU.add, op1=ALU.add))
            rstep(dve.tensor_tensor(rt[:, 2, :], rt[:, 1, :], rt[:, 0, :], op=ALU.subtract))
            rstep(dve.tensor_scalar(rt[:, 3, :], rt[:, 2, :], float(P), None, op0=ALU.mult))
            rstep(dve.tensor_tensor(rk_all, rk_all, rt[:, 3, :][:, :, None].to_broadcast([P, EXPERTS, NT]),
                                    op=ALU.add))
            rstep(dve.tensor_tensor(rk_mul, rk_all, oh_e, op=ALU.mult))
            rstep(dve.tensor_reduce(posf, rk_mul.rearrange("p e t -> p t e"), axis=AX_X, op=ALU.add))
            rstep(dve.tensor_copy(posi[:, 0, :], posf))
            rstep(dve.tensor_scalar(posi[:, 1, :], posi[:, 0, :], P - 1, None, op0=ALU.bitwise_and))
            rstep(dve.tensor_scalar(posi[:, 2, :], posi[:, 0, :], 7, None, op0=ALU.logical_shift_right))
            rstep(dve.tensor_copy(lanef, posi[:, 1, :]))
            rstep(dve.tensor_copy(tilef, posi[:, 2, :]))
            rstep(dve.memset(sl_e, 0.0))
            for e in range(1, EXPERTS):
                rstep(dve.scalar_tensor_tensor(sl_e, iota_k[:, 0:NSLOT], rt[:, 2, e:e + 1], sl_e,
                                               op0=ALU.is_ge, op1=ALU.add))
            dve.tensor_scalar(slot_wd[0:1, 0:NSLOT], sl_e[0:1, :], float(FC * C), None, op0=ALU.mult)
            dve.tensor_scalar(slot_bd[0:1, 0:NSLOT], sl_e[0:1, :], float(C), None, op0=ALU.mult)
            def permute(n, b):
                t = ds(RG * n, RG)
                dve.wait_ge(r_acc, n - 1 + XA)
                dve.tensor_tensor(lane_oh[:, b], iota_p[:, None, :].to_broadcast([P, RG, P]),
                                  lanef[:, t][:, :, None].to_broadcast([P, RG, P]), op=ALU.is_equal)
                dve.wait_ge(r_oh, n + XA)
                dve.tensor_tensor(tile_eq, iota_k[:, None, 0:NSLOT].to_broadcast([P, RG, NSLOT]),
                                  tilef[:, t][:, :, None].to_broadcast([P, RG, NSLOT]), op=ALU.is_equal
                                  ).then_inc(r_eq, 1)
                dve.wait_ge(r_eq, n + 1)
                dve.tensor_tensor(tile_oh[b][:, :, 0, :], tile_eq, tok1[:, t][:, :, None].to_broadcast([P, RG, NSLOT]),
                                  op=ALU.mult)
                dve.tensor_tensor(tile_oh[b][:, :, 1, :], tile_eq, ptop[:, t][:, :, None].to_broadcast([P, RG, NSLOT]),
                                  op=ALU.mult).then_inc(r_oh, 1)
            with dve.Fori(0, NT // RG // 2) as i:
                permute(2 * i, 0)
                permute(2 * i + 1, 1)
            dve.wait_ge(r_acc, NT // RG + XA)
            perm = pb[3][:, 0:NSLOT]
            dve.tensor_copy(sl_p, pb[3][:, NSLOT:2 * NSLOT])
            rstep(dve.tensor_scalar(permz, perm, 0.0, float(SKIP), op0=ALU.is_equal, op1=ALU.mult))
            rstep(dve.scalar_tensor_tensor(permz, perm, -1.0, permz, op0=ALU.add, op1=ALU.add))
            dve.wait_ge(f_st[0], 16 * NPAIR + 16)
            dve.wait_ge(f_st[1], 16 * NPAIR + 16)
            rstep(dve.tensor_copy(permi, permz))
            dve.sem_inc(r_done, 1)
            dve.wait_ge(r_done, 1)

            bd_regs = [dve.alloc_register(f"bd_slot{n}") for n in range(GROWS)]

            def name_rows(s, u):
                dve.wait_ge(s_const, 1)
                dve.tensor_copy(gidx[:, u:u + 1], permi[:, ds(s, 1)]).then_inc(e_ix, 1)

            def expert_out(s, u, half_before, off):
                v = u % 2
                if not (isinstance(half_before, int) and half_before == 0):
                    held(dve, e_out[v], 16 * half_before)
                dve.tensor_copy(oidx[:, v:v + 1], permi[:, ds(s, 1)])
                dve.wait_ge(e_yp, s + 1 + AHEAD)
                dve.tensor_tensor(yout[:, v, :], pb[4 + v][:, 0:C], bd_s[:, ds(off, C)], op=ALU.add
                                  ).then_inc(e_b, 1)
                dve.wait_ge(e_b, s + 1)
                dve.scalar_tensor_tensor(yout[:, v, :], yout[:, v, :], sl_p[:, ds(s, 1)], grow[:, u, FF:FROW],
                                         op0=ALU.mult, op1=ALU.add).then_inc(e_y, 1)
                dve.wait_ge(e_y, s + 1 + AHEAD)

            def expert_tiles(i, last):
                dve.load(bd_regs, slot_bd[0:1, ds(GROWS * i, GROWS)])
                offs = [dve.snap(r, min_val=0, max_val=(EXPERTS - 1) * C) for r in bd_regs]
                for u in range(GROWS):
                    s = GROWS * i + u
                    if not (last and u):
                        name_rows(s + GROWS - 1, (u + GROWS - 1) % GROWS)
                    expert_out(s, u, 2 * i + u // 2, offs[u])
            for u in range(GROWS - 1):
                name_rows(u, u)
            dve.wait_ge(f_wd, 16 * (EXPERTS + 1))
            expert_tiles(0, False)
            with dve.Fori(1, NSLOT // GROWS - 1) as i:
                expert_tiles(i, False)
            expert_tiles(NSLOT // GROWS - 1, True)


def kernel(x, src, dst, L0_gnn_W, L0_gnn_a, L0_mix_Wqkv, L0_mix_ln1_g, L0_mix_ln1_b, L0_mix_W1, L0_mix_b1,
           L0_mix_W2, L0_mix_b2, L0_mix_ln2_g, L0_mix_ln2_b, L0_ffn_W1, L0_ffn_b1, L0_ffn_Wg, L0_ffn_bg,
           L0_ffn_Wd, L0_ffn_bd):
    import numpy as np
    import concourse.bacc as bacc
    from concourse.bass_utils import run_bass_kernel_spmd

    def rows(a):
        return np.ascontiguousarray(np.broadcast_to(np.asarray(a).reshape(1, -1), (P, np.asarray(a).size)))

    def columns(a):
        return np.asarray(a).reshape(-1, P).T

    def slots(a):
        a = np.asarray(a)
        return np.concatenate([a, np.full(SLOTS - a.shape[0], NOBODY, a.dtype)])

    x = np.asarray(x)
    ga = np.asarray(L0_gnn_a).reshape(HEADS, 2, HID)[:, ::-1]
    laid = {
        "x": np.concatenate([x, np.zeros((ROWS - N_NODES, C), x.dtype)]),
        "src": slots(src),
        "dst": slots(dst),
        "gw": np.asarray(L0_gnn_W).transpose(1, 0, 2).reshape(C, C),
        "gwt": np.asarray(L0_gnn_W).transpose(2, 0, 1),
        "ga": ga.transpose(2, 0, 1),
        "wqkv_t": np.asarray(L0_mix_Wqkv).T,
        "ln1_g": columns(L0_mix_ln1_g), "ln1_b": columns(L0_mix_ln1_b),
        "w1_t": np.asarray(L0_mix_W1).T, "b1": columns(L0_mix_b1),
        "w2_t": np.asarray(L0_mix_W2).T, "b2": rows(L0_mix_b2),
        "ln2_g": rows(L0_mix_ln2_g), "ln2_b": rows(L0_mix_ln2_b),
        "ln1_g_rows": rows(L0_mix_ln1_g), "ln1_b_rows": rows(L0_mix_ln1_b),
        "fw1": L0_ffn_W1, "fb1": columns(L0_ffn_b1), "fwg": L0_ffn_Wg, "fbg": rows(L0_ffn_bg),
        "fwd": L0_ffn_Wd, "fbd": rows(L0_ffn_bd),
    }
    laid = {f"in_{k}": np.ascontiguousarray(v) for k, v in laid.items()}
    nc = bacc.Bacc("TRN2", target_bir_lowering=False, num_devices=1)
    aps = {k[3:]: nc.dram_tensor(k, a.shape, mybir.dt.from_np(a.dtype), kind="ExternalInput").ap()
           for k, a in laid.items()}
    out = nc.dram_tensor("out", [ROWS, C], F32, kind="ExternalOutput").ap()
    gps_layer(nc, out=out, **aps)
    r = run_bass_kernel_spmd(nc, [laid], core_ids=[0])
    return np.asarray(r.results[0]["out"])[0:N_NODES]
```
